# Optimizing a Trainium2 kernel written in Bass

```python
import numpy as np
import jax
import jax.numpy as jnp

def _softmax(x, axis=-1):
    return jax.nn.softmax(x, axis=axis)

def _gelu(x):
    return jax.nn.gelu(x, approximate=True)

def _silu(x):
    return jax.nn.silu(x)

def _sigmoid(x):
    return jax.nn.sigmoid(x)

def _layernorm(x, axis=-1, eps=1e-05):
    m = jnp.mean(x, axis=axis, keepdims=True)
    v = jnp.var(x, axis=axis, keepdims=True)
    return (x - m) / jnp.sqrt(v + eps)

def _scatter_add(tgt, idx, src, axis=0):
    return tgt.at[idx].add(src)

def _segment_sum(src, seg, n):
    return jax.ops.segment_sum(src, seg, n)
kernel_name = 'mk_adaln_ffn_d2_seqx_r4_01d0be'

def setup_inputs(seed: int=0):
    np.random.seed(seed)
    _w = jnp.asarray

    def _rec_inputs():
        import jax
        import jax.numpy as jnp
        _rk = jax.random.key(seed)
        x = -1.528e-05 + 0.9999 * jax.random.normal(jax.random.fold_in(_rk, 1), (16, 256, 256), jnp.float32)
        _lenS = 256 - jax.random.randint(jax.random.fold_in(_rk, 7), (16,), 0, max(1, 256 // 4) + 1, jnp.int32)
        _lenS2 = 256 - jax.random.randint(jax.random.fold_in(_rk, 8), (16,), 0, max(1, 256 // 4) + 1, jnp.int32)
        cond_1024 = -0.00608245 + 1.00131 * jax.random.normal(jax.random.fold_in(_rk, 11), (16, 256), jnp.float32)
        return (x, cond_1024)
    x, cond_1024 = _rec_inputs()

    def _L0_cond_setup():
        import jax, jax.numpy as jnp
        import numpy as np
        LATENT = 256
        key = jax.random.key(seed)
        k1, k2, k3, k4 = jax.random.split(key, 4)
        B, T, D = (64, 128, LATENT)
        h_t = jax.random.normal(k1, (B, D), dtype=jnp.float32)
        z = jax.random.normal(k2, (B, T, D), dtype=jnp.float32)
        bound = 1.0 / np.sqrt(2 * D)
        W = jax.random.uniform(k3, (D, 2 * D), minval=-bound, maxval=bound, dtype=jnp.float32)
        b = jax.random.uniform(k4, (D,), minval=-bound, maxval=bound, dtype=jnp.float32)
        alpha = jnp.full((D,), 0.1, dtype=jnp.float32)
        return {'h_t': h_t, 'z': z, 'W': W, 'b': b, 'alpha': alpha}
    _L0_cond_all = _L0_cond_setup()
    _L0_cond_in = {k: v for k, v in _L0_cond_all.items() if k in ('W', 'b', 'alpha')}
    del _L0_cond_all

    def _L0_ffn_setup():
        import jax, jax.numpy as jnp
        import numpy as np
        HIDDEN = 256
        FFN = 4 * HIDDEN
        NUM_EXPERTS = 8
        TOP_K = 2
        B, S = (4, 512)
        key = jax.random.key(seed)
        ks = jax.random.split(key, 7)
        scale = 0.02
        return {'x': jax.random.normal(ks[0], (B, S, HIDDEN), dtype=jnp.float32), 'gate_w': jax.random.normal(ks[1], (HIDDEN, NUM_EXPERTS), dtype=jnp.float32) * scale, 'gate_b': jnp.zeros((NUM_EXPERTS,), dtype=jnp.float32), 'w1': jax.random.normal(ks[2], (NUM_EXPERTS, HIDDEN, FFN), dtype=jnp.float32) * scale, 'b1': jnp.zeros((NUM_EXPERTS, FFN), dtype=jnp.float32), 'w2': jax.random.normal(ks[3], (NUM_EXPERTS, FFN, HIDDEN), dtype=jnp.float32) * scale, 'b2': jnp.zeros((NUM_EXPERTS, HIDDEN), dtype=jnp.float32)}
    _L0_ffn_all = _L0_ffn_setup()
    _L0_ffn_in = {k: v for k, v in _L0_ffn_all.items() if k in ('gate_w', 'gate_b', 'w1', 'b1', 'w2', 'b2')}
    del _L0_ffn_all

    def _L1_cond_setup():
        import jax, jax.numpy as jnp
        import numpy as np
        TOP_K = 2
        N_EXPERTS = 8
        N_SHARED = 1
        EPS = 1e-09
        key = jax.random.key(seed)
        ks = jax.random.split(key, 10)
        B, T, d = (2, 512, 256)
        h_s, h_r, E = (512, 128, N_EXPERTS)
        return {'x': jax.random.normal(ks[0], (B, T, d), jnp.float32), 't_emb': jax.random.normal(ks[1], (B, d), jnp.float32), 'router_w': jax.random.normal(ks[2], (E, d), jnp.float32) * 0.01, 'router_t_w': jax.random.normal(ks[3], (E, d), jnp.float32) * 0.01, 'router_bias': jnp.zeros((E,), jnp.float32), 'sw1': jax.random.normal(ks[4], (h_s, d), jnp.float32) * 0.02, 'sw3': jax.random.normal(ks[5], (h_s, d), jnp.float32) * 0.02, 'sw2': jax.random.normal(ks[6], (d, h_s), jnp.float32) * 0.02, 'rw1': jax.random.normal(ks[7], (E, h_r, d), jnp.float32) * 0.02, 'rw2': jax.random.normal(ks[8], (E, d, h_r), jnp.float32) * 0.02}
    _L1_cond_all = _L1_cond_setup()
    _L1_cond_in = {k: v for k, v in _L1_cond_all.items() if k in ('router_w', 'router_t_w', 'router_bias', 'sw1', 'sw3', 'sw2', 'rw1', 'rw2')}
    del _L1_cond_all

    def _L1_ffn_setup():
        import jax, jax.numpy as jnp
        import numpy as np
        EPS = 1e-08

        def _ste(x, q):
            return x + jax.lax.stop_gradient(q - x)

        def quant_act_uint8(x):
            s = jax.lax.stop_gradient(jnp.maximum(jnp.max(x), EPS)) / 255.0
            q = jnp.clip(jnp.round(x / s), 0.0, 255.0) * s
            return (_ste(x, q), s)

        def quant_weight_int8_perchannel(w):
            s = jax.lax.stop_gradient(jnp.maximum(jnp.max(jnp.abs(w), axis=1, keepdims=True), EPS)) / 127.0
            q = jnp.clip(jnp.round(w / s), -128.0, 127.0) * s
            return (_ste(w, q), s[:, 0])

        def quant_bias_int32(b, s_in, s_w):
            s = jax.lax.stop_gradient(s_in * s_w)
            q = jnp.round(b / s) * s
            return _ste(b, q)

        def quant_linear(x, w, b):
            xq, s_in = quant_act_uint8(x)
            wq, s_w = quant_weight_int8_perchannel(w)
            bq = quant_bias_int32(b, s_in, s_w)
            return jnp.einsum('btd,fd->btf', xq, wq) + bq
        key = jax.random.key(seed)
        k1, k2, k3, k4, k5 = jax.random.split(key, 5)
        B, S, D, F = (4, 512, 256, 1024)
        return {'x': jax.random.normal(k1, (B, S, D), dtype=jnp.float32), 'w1': jax.random.normal(k2, (F, D), dtype=jnp.float32) * (1.0 / np.sqrt(D)), 'b1': jax.random.normal(k3, (F,), dtype=jnp.float32) * 0.01, 'w2': jax.random.normal(k4, (D, F), dtype=jnp.float32) * (1.0 / np.sqrt(F)), 'b2': jax.random.normal(k5, (D,), dtype=jnp.float32) * 0.01}
    _L1_ffn_all = _L1_ffn_setup()
    _L1_ffn_in = {k: v for k, v in _L1_ffn_all.items() if k in ('w1', 'b1', 'w2', 'b2')}
    del _L1_ffn_all
    return {'x': x, 'cond_1024': cond_1024, 'L0_cond_W': _L0_cond_in['W'], 'L0_cond_b': _L0_cond_in['b'], 'L0_cond_alpha': _L0_cond_in['alpha'], 'L0_ffn_gate_w': _L0_ffn_in['gate_w'], 'L0_ffn_gate_b': _L0_ffn_in['gate_b'], 'L0_ffn_w1': _L0_ffn_in['w1'], 'L0_ffn_b1': _L0_ffn_in['b1'], 'L0_ffn_w2': _L0_ffn_in['w2'], 'L0_ffn_b2': _L0_ffn_in['b2'], 'L1_cond_router_w': _L1_cond_in['router_w'], 'L1_cond_router_t_w': _L1_cond_in['router_t_w'], 'L1_cond_router_bias': _L1_cond_in['router_bias'], 'L1_cond_sw1': _L1_cond_in['sw1'], 'L1_cond_sw3': _L1_cond_in['sw3'], 'L1_cond_sw2': _L1_cond_in['sw2'], 'L1_cond_rw1': _L1_cond_in['rw1'], 'L1_cond_rw2': _L1_cond_in['rw2'], 'L1_ffn_w1': _L1_ffn_in['w1'], 'L1_ffn_b1': _L1_ffn_in['b1'], 'L1_ffn_w2': _L1_ffn_in['w2'], 'L1_ffn_b2': _L1_ffn_in['b2']}

def reference(x, cond_1024, L0_cond_W, L0_cond_b, L0_cond_alpha, L0_ffn_gate_w, L0_ffn_gate_b, L0_ffn_w1, L0_ffn_b1, L0_ffn_w2, L0_ffn_b2, L1_cond_router_w, L1_cond_router_t_w, L1_cond_router_bias, L1_cond_sw1, L1_cond_sw3, L1_cond_sw2, L1_cond_rw1, L1_cond_rw2, L1_ffn_w1, L1_ffn_b1, L1_ffn_w2, L1_ffn_b2):
    import jax
    import jax.numpy as jnp

    def _L0_cond_ref(h_t, z, W, b, alpha):
        import jax, jax.numpy as jnp
        import numpy as np
        LATENT = 256
        D = h_t.shape[-1]
        Wh = W[:, :D]
        Wz = W[:, D:]
        leak = 1.0 - alpha

        def step(h, z_t):
            gate = jax.nn.sigmoid(h @ Wh.T + z_t @ Wz.T + b)
            h_new = jnp.tanh(h * leak + gate * z_t)
            return (h_new, h_new)
        _, hs = jax.lax.scan(step, h_t, jnp.swapaxes(z, 0, 1))
        return jnp.swapaxes(hs, 0, 1)

    def _L0_ffn_ref(x, gate_w, gate_b, w1, b1, w2, b2):
        import jax, jax.numpy as jnp
        import numpy as np
        HIDDEN = 256
        FFN = 4 * HIDDEN
        NUM_EXPERTS = 8
        TOP_K = 2
        B, S = (4, 512)
        b, s, h = x.shape
        xt = x.reshape(b * s, h)
        probs = jax.nn.softmax(xt @ gate_w + gate_b, axis=-1)
        _, idx = jax.lax.top_k(probs, TOP_K)
        one_hot = jax.nn.one_hot(idx, NUM_EXPERTS, dtype=xt.dtype)
        mask = (one_hot.sum(axis=1) > 0).astype(xt.dtype)
        h1 = jax.nn.relu(jnp.einsum('th,ehf->etf', xt, w1) + b1[:, None, :])
        out_e = jnp.einsum('etf,efh->eth', h1, w2) + b2[:, None, :]
        out = jnp.einsum('eth,te->th', out_e, mask)
        return out.reshape(b, s, h)

    def _L1_cond_ref(x, t_emb, router_w, router_t_w, router_bias, sw1, sw3, sw2, rw1, rw2):
        import jax, jax.numpy as jnp
        import numpy as np
        TOP_K = 2
        N_EXPERTS = 8
        N_SHARED = 1
        EPS = 1e-09
        B, T, C = x.shape
        N = B * T
        x_flat = x.reshape(N, C)
        shared_out = jnp.einsum('nh,dh->nd', jax.nn.silu(x_flat @ sw1.T) * (x_flat @ sw3.T), sw2)
        t_bias = t_emb @ router_t_w.T
        t_bias_flat = jnp.broadcast_to(t_bias[:, None, :], (B, T, N_EXPERTS)).reshape(N, N_EXPERTS)
        s = jax.nn.sigmoid((x_flat @ router_w.T + t_bias_flat).astype(jnp.float32))
        sel_scores = s + router_bias
        _, topk_idx = jax.lax.top_k(sel_scores, TOP_K)
        s_sel = jnp.take_along_axis(s, topk_idx, axis=1)
        denom = jnp.sum(s_sel, axis=1, keepdims=True)
        gates = jnp.where(denom > EPS, s_sel / (denom + EPS), 1.0 / TOP_K).astype(x.dtype)
        combine = jnp.sum(gates[:, :, None] * jax.nn.one_hot(topk_idx, N_EXPERTS, dtype=x.dtype), axis=1)
        H = jax.nn.gelu(jnp.einsum('nd,ehd->enh', x_flat, rw1), approximate=False)
        O = jnp.einsum('enh,edh->end', H, rw2)
        routed_out = jnp.einsum('end,ne->nd', O, combine)
        out = (shared_out + routed_out) / (N_SHARED + TOP_K)
        return out.reshape(B, T, C)

    def _L1_ffn_ref(x, w1, b1, w2, b2):
        import jax, jax.numpy as jnp
        import numpy as np
        EPS = 1e-08

        def _ste(x, q):
            return x + jax.lax.stop_gradient(q - x)

        def quant_act_uint8(x):
            s = jax.lax.stop_gradient(jnp.maximum(jnp.max(x), EPS)) / 255.0
            q = jnp.clip(jnp.round(x / s), 0.0, 255.0) * s
            return (_ste(x, q), s)

        def quant_weight_int8_perchannel(w):
            s = jax.lax.stop_gradient(jnp.maximum(jnp.max(jnp.abs(w), axis=1, keepdims=True), EPS)) / 127.0
            q = jnp.clip(jnp.round(w / s), -128.0, 127.0) * s
            return (_ste(w, q), s[:, 0])

        def quant_bias_int32(b, s_in, s_w):
            s = jax.lax.stop_gradient(s_in * s_w)
            q = jnp.round(b / s) * s
            return _ste(b, q)

        def quant_linear(x, w, b):
            xq, s_in = quant_act_uint8(x)
            wq, s_w = quant_weight_int8_perchannel(w)
            bq = quant_bias_int32(b, s_in, s_w)
            return jnp.einsum('btd,fd->btf', xq, wq) + bq
        h = jax.nn.relu(quant_linear(x, w1, b1))
        return quant_linear(h, w2, b2)
    x = x + _L0_ffn_ref(_L0_cond_ref(cond_1024, x, L0_cond_W, L0_cond_b, L0_cond_alpha), L0_ffn_gate_w, L0_ffn_gate_b, L0_ffn_w1, L0_ffn_b1, L0_ffn_w2, L0_ffn_b2)
    x = x + _L1_ffn_ref(_L1_cond_ref(x, cond_1024, L1_cond_router_w, L1_cond_router_t_w, L1_cond_router_bias, L1_cond_sw1, L1_cond_sw3, L1_cond_sw2, L1_cond_rw1, L1_cond_rw2), L1_ffn_w1, L1_ffn_b1, L1_ffn_w2, L1_ffn_b2)
    return x

_drawn_inputs = setup_inputs


def setup_inputs(seed=0):
    import zlib

    import numpy as np

    out = dict(_drawn_inputs(seed))
    spreads = {'L0_cond_alpha': (0.10000000149011612, 0.2),
     'L0_ffn_gate_b': (0.0, 0.1),
     'L0_ffn_b1': (0.0, 0.1),
     'L0_ffn_b2': (0.0, 0.1),
     'L1_cond_router_bias': (0.0, 0.8)}
    factors = {'cond_1024': 3.078,
     'L0_cond_b': 4.175,
     'L1_cond_router_w': 8.0,
     'L1_cond_router_t_w': 8.0,
     'L1_cond_sw1': 8.0,
     'L1_cond_sw3': 8.0,
     'L1_cond_sw2': 8.0,
     'L1_cond_rw1': 8.0,
     'L1_cond_rw2': 8.0,
     'L1_ffn_w1': 8.0,
     'L1_ffn_b1': 171.377,
     'L1_ffn_w2': 6.347,
     'L1_ffn_b2': 200.0}
    for name, (base, spread) in spreads.items():
        noise = np.random.default_rng([zlib.crc32(name.encode()), seed]).standard_normal(out[name].shape)
        drawn = base * np.exp(spread * noise) if base else spread * noise
        out[name] = jnp.asarray(drawn.astype(out[name].dtype))
    for name, factor in factors.items():
        out[name] = (out[name] * factor).astype(out[name].dtype)
    return out
```

```python
from contextlib import ExitStack

import concourse.bass as bass
from concourse import mybir

P = 128
BATCH, STEPS, D = 16, 256, 256
N = BATCH * STEPS
TILES = N // P
STEPS_PER_TILE = P // BATCH
DC = D // P
E = 8
F = 1024
FC = F // P
HS = 512
HSC = HS // P
GT = 4
GROUPS = TILES // GT
GN = GT * P
RING = 4

W_SCALE = 256.0
A_SCALE = 16.0
PRE_SCALE = W_SCALE
MAGIC = 12582912.0
EPS_GATE = 1e-9
EPS_QUANT = 1e-8
FAR = 1e30

ALU = mybir.AluOpType
ACT = mybir.ActivationFunctionType
AX = mybir.AxisListType
F32 = mybir.dt.float32
F16 = mybir.dt.float16
BF16 = mybir.dt.bfloat16
RMAX = bass.bass_isa.ReduceOp.max

HC = HSC + E
U_SHARED, U_ROUTED = 1, 1 + 2 * HSC
U_NEXT = U_ROUTED + E
U_OUT = U_NEXT + DC
U_PAIR = U_OUT + GT
UNITS = U_PAIR + GT * E // 2
PRE_UNITS = 1 + DC
YG = GT * (1 + E)
MIX_SCALE = W_SCALE * A_SCALE
LINKS = 24
V_SCALE = 4.0
OUT_SCALE = W_SCALE * V_SCALE


def build_program(nc, zT, xn, h0T, WT, b_row, alphaT, gate_wT, gate_b, w1T, b1T, w2T, b2, rwT, rtwT, rbias,
                  sw1T, sw3T, sw2T, rw1T, rw2T, fw1n, fb1T, fw2n, fb2, out):
    ctx = ExitStack()
    with ctx:
        def sb(name, shape, dt):
            return ctx.enter_context(nc.sbuf_tensor(name, shape, dt))

        def sem(name):
            return ctx.enter_context(nc.semaphore(name))

        ps = ctx.enter_context(nc.psum_tensor("ps", [P, 8, 512], F32))
        z = sb("z", [P, RING, DC, P], F32)
        wh_hi = sb("wh_hi", [P, DC, D], F16)
        wh_lo = sb("wh_lo", [P, DC, D], F16)
        wz = sb("wz", [P, DC, D], F32)
        b_mat = sb("b_mat", [P, D], F32)
        ones = sb("ones", [P, P], F32)
        h0 = sb("h0", [P, DC, BATCH], F32)
        alpha = sb("alpha", [P, DC], F32)
        leak = sb("leak", [P, DC, BATCH], F32)
        hring = sb("hring", [P, 2, 2, DC, P], F16)
        gate = sb("gate", [P, DC, BATCH], F32)
        gz = sb("gz", [P, DC, BATCH], F32)
        u = sb("u", [P, DC, BATCH], F32)
        h32 = sb("h32", [P, DC, BATCH], F32)
        hleak = sb("hleak", [P, DC, BATCH], F32)
        big = sb("big", [P, TILES * D], F32)
        HT = big[:].bitcast(F16).rearrange("p (j s c n) -> p j s c n", j=TILES, s=2, c=DC)
        x1 = sb("x1", [P, TILES, D], F32)
        stage = sb("stage", [P, 4096], F32)
        wsplit = sb("wsplit", [P, 2, 2, 2, 2048], F16)
        hid = sb("hid", [P, 2, FC, GN], F16)
        v32 = sb("v32", [P, 2, GN], F32)
        y = big[:].rearrange("p (j d) -> p j d", d=D)
        stage1 = sb("stage1", [P, 4096], F32)
        l1w = sb("l1w", [P, 2, 7168], F16)
        sw1s = l1w[:, :, 0:1024].rearrange("p s (k h) -> p s k h", k=DC)
        sw3s = l1w[:, :, 1024:2048].rearrange("p s (k h) -> p s k h", k=DC)
        sw2s = l1w[:, :, 2048:3072].rearrange("p s (k d) -> p s k d", k=HSC)
        rw1s = l1w[:, :, 3072:5120].rearrange("p s (k h) -> p s k h", k=DC)
        rw2s = l1w[:, :, 5120:7168].rearrange("p s (e d) -> p s e d", e=E)
        xs = stage[:, 2048:4096].bitcast(F16).rearrange("p (b s k n) -> p b s k n", b=2, s=2, k=DC)
        xsn = hid[:, :, 0:2].rearrange("p s c n -> p s (c n)")
        vs = stage[:, 0:3 * GN].rearrange("p (b n) -> p b n", b=3)
        inv = sb("inv", [P, 2], F32)
        neg_magic = sb("neg_magic", [P, 1], F32)
        hid1 = wsplit[:].rearrange("p a b c n -> p (a b c n)")[:, 0:2 * 12 * GN].rearrange(
            "p (s c n) -> p s c n", s=2, c=12)
        yqT = wsplit[:].rearrange("p a b c n -> p (a b c n)")[:, 0:DC * N].bitcast(BF16).rearrange(
            "p (k n) -> p k n", k=DC)
        hq = hid[:, 0].bitcast(BF16)
        yqn = hid[:, 1].bitcast(BF16).rearrange("p c n -> p (c n)")
        wq_n = sb("wq_n", [P, 2, 2048], BF16)
        w1qT = l1w[:, 0, 0:DC * F].bitcast(BF16).rearrange("p (k f) -> p k f", k=DC)
        w2qT = l1w[:, 1, 0:FC * D].bitcast(BF16).rearrange("p (f d) -> p f d", f=FC)
        sw = sb("sw", [P, FC + DC], F32)
        swr = sb("swr", [P, FC + DC], F32)
        fb1 = sb("fb1", [P, FC], F32)
        bq1 = sb("bq1", [P, FC], F32)
        sc1 = sb("sc1", [P, FC], F32)
        bq2 = sb("bq2", [P, D], F32)
        rs2 = sb("rs2", [P, D], F32)
        imax = sb("imax", [P, FC, 4], F32)
        ymax = sb("ymax", [P, GROUPS], F32)
        pmax = sb("pmax", [P, 2], F32)
        gmax = sb("gmax", [P, 2], F32)
        hmax = sb("hmax", [P, FC], F32)
        diag = sb("diag", [P, DC, P], F32)
        h0rep = sb("h0rep", [P, DC, P], F32)
        rtw = sb("rtw", [P, DC, E], F32)
        rw = sb("rw", [P, DC, E], F32)
        rw_s = sb("rw_s", [P, 2, DC, E], F16)
        rb_row = sb("rb_row", [P, E], F32)
        t_bias = sb("t_bias", [P, E], F32)
        score = sb("score", [P, GT, E], F32)
        comb = sb("comb", [P, GT, E], F32)
        den = sb("den", [P, GT, 2], F32)
        good = sb("good", [P, GT, 2], F32)
        gw = sb("gw", [P, DC, E], F32)
        gw_s = sb("gw_s", [P, 2, DC, E], F16)
        gb_row = sb("gb_row", [P, E], F32)
        b1s = sb("b1s", [P, E, FC], F32)
        b2stage = stage[0:33, 2048:4096].rearrange("p (e d) -> p e d", e=E)
        b2s = sb("b2s", [P, E, D], F16)
        a_ones = sb("a_ones", [P, P], F16)
        prio = sb("prio", [P, E], F32)
        sel, t8, one1, mask = (z[:].rearrange("p a c n -> p (a c n)")[:, k * TILES * E:(k + 1) * TILES * E].rearrange(
            "p (j e) -> p j e", e=E) for k in range(4))
        m1 = sb("m1", [P, TILES, 1], F32)
        k1 = sb("k1", [P, TILES, 1], F32)
        ident = sb("ident", [P, P], F32)
        identb = sb("identb", [P, P], BF16)
        identh = sb("identh", [P, P], F16)

        w_in = sem("w_in")
        small_in = sem("small_in")
        const0 = sem("const0")
        idents = sem("idents")
        z_in = [sem(f"z_in{i}") for i in range(RING)]
        prep = sem("prep")
        pre_ready = sem("pre_ready")
        gate_ready = sem("gate_ready")
        gz_ready = sem("gz_ready")
        u_ready = sem("u_ready")
        hi_ready = sem("hi_ready")
        h32_ready = sem("h32_ready")
        lo_ready = sem("lo_ready")
        hleak_ready = sem("hleak_ready")
        ring_out = [sem(f"ring_out{i}") for i in range(2)]
        x_in = sem("x_in")
        logits_ready = sem("logits_ready")
        vchain = sem("vchain")
        mask_ready = sem("mask_ready")
        ew_in = sem("ew_in")
        ew_split = sem("ew_split")
        l1_psum = sem("l1_psum")
        l1_v = sem("l1_v")
        split0 = sem("split0")
        l1_hid = sem("l1_hid")
        l2_psum = sem("l2_psum")
        l2_acc = sem("l2_acc")
        out_done = sem("out_done")
        l1w_in = sem("l1w_in")
        l1w_used = sem("l1w_used")
        xn_hi = sem("xn_hi")
        xn_lo = sem("xn_lo")
        xs_T = sem("xs_T")
        unit = sem("unit")
        sa_used = sem("sa_used")
        tb_ready = sem("tb_ready")
        router_step = sem("router_step")
        ymax_in = sem("ymax_in")
        wm_ready = sem("wm_ready")
        pool_step = sem("pool_step")
        bq_ready = sem("bq_ready")
        xb_ready = sem("xb_ready")
        rt_in = sem("rt_in")
        rt_sig = sem("rt_sig")
        th_ready = sem("th_ready")
        vs_ready = sem("vs_ready")
        vr_ready = sem("vr_ready")
        hi1 = sem("hi1")
        lo1 = sem("lo1")
        y_acc = sem("y_acc")
        mx_in = sem("mx_in")
        mx_out = sem("mx_out")
        wt_ps = sem("wt_ps")
        wt_cp = sem("wt_cp")
        yq_m = sem("yq_m")
        yq_n = sem("yq_n")
        yq_ps = sem("yq_ps")
        yq_T = sem("yq_T")
        ia_ps = sem("ia_ps")
        ia_mx = sem("ia_mx")
        hb_ps = sem("hb_ps")
        hb_h = sem("hb_h")
        hb_q = sem("hb_q")
        hb_s = sem("hb_s")
        ob_ps = sem("ob_ps")
        ob_s = sem("ob_s")
        ob = sem("ob")

        count = {"v": 0}

        def link(dve, ins):
            count["v"] += 1
            ins.then_inc(vchain, 1)
            dve.wait_ge(vchain, count["v"])

        def top2(dve, n):
            s, t, o, mk, a, b = sel[:, 0:n], t8[:, 0:n], one1[:, 0:n], mask[:, 0:n], m1[:, 0:n], k1[:, 0:n]
            pr = prio[:].rearrange("p (a e) -> p a e", a=1).broadcast_to([P, n, E])
            for k in range(2):
                dst = o if k == 0 else mk
                link(dve, dve.tensor_reduce(a, s, AX.X, ALU.max))
                link(dve, dve.tensor_tensor(t, s, a.broadcast_to([P, n, E]), ALU.is_equal))
                link(dve, dve.tensor_tensor(t, t, pr, ALU.mult))
                link(dve, dve.tensor_reduce(b, t, AX.X, ALU.max))
                link(dve, dve.tensor_tensor(dst, t, b.broadcast_to([P, n, E]), ALU.is_equal))
                if k == 0:
                    link(dve, dve.scalar_tensor_tensor(s, dst, -FAR, s, ALU.mult, ALU.add))
            link(dve, dve.tensor_tensor(mk, mk, o, ALU.add))

        def psh(b):
            return ps[:, b].bitcast(F16)

        def bank_of(u):
            return u % 8

        def mix_groups(eng, mix):
            mix(0, 0)
            with eng.Fori(0, GROUPS // 2 - 1) as i:
                mix(2 * i + 1, 1)
                mix(2 * i + 2, 0)
            mix(GROUPS - 1, 1)

        def is_last(g):
            return isinstance(g, int) and g == GROUPS - 1

        def acc_index(p, q, j):
            return GT + 2 * GT * p + 4 * (q // 2) + 2 * j + q % 2

        def mixture_pe(pe):
            def split_matmul(dst, lhs, rhs, ks):
                for n, (a, b) in enumerate(((0, 0), (0, 1), (1, 0))):
                    for k in ks:
                        last = pe.matmul(dst, lhs(a, k), rhs(b, k), start=(n == 0 and k == ks[0]),
                                         stop=(n == 2 and k == ks[-1]))
                return last

            def reader_done(g, u):
                if u >= 8:
                    h, v = g, u - 8
                    if is_last(g) and U_NEXT <= v < U_OUT:
                        v -= 8
                elif isinstance(g, int) and g == 0:
                    return
                else:
                    h, v = g - 1, (u + 32 if u + 32 < UNITS else u + 24)
                if v == 0:
                    pe.wait_ge(rt_in, h + 1)
                elif v < U_ROUTED:
                    c = (v - U_SHARED) // 2
                    pe.wait_ge(vs_ready if (v - U_SHARED) % 2 else sa_used, HSC * h + c + 1)
                elif v < U_NEXT:
                    pe.wait_ge(vr_ready, E * h + v - U_ROUTED + 1)
                elif v < U_OUT:
                    pe.wait_ge(xs_T, 2 * h + 2 + v - U_NEXT + 1)
                elif v < U_PAIR:
                    pe.wait_ge(y_acc, YG * h + v - U_OUT + 1)
                else:
                    p, q = (v - U_PAIR) // GT, (v - U_PAIR) % GT
                    pe.wait_ge(y_acc, YG * h + acc_index(p, q, 1) + 1)

            def transposes(g, s):
                pe.wait_ge(xn_lo if s else xn_hi, g + 1)
                for k in range(DC):
                    for q in range(GT):
                        last = pe.transpose(psh(bank_of(U_NEXT + s))[:, k * GN + q * P:k * GN + (q + 1) * P],
                                            xsn[:, s, q * D + k * P:q * D + (k + 1) * P], identh[:])
                last.then_inc(unit, 1)

            pe.wait_ge(l2_acc, E * TILES)
            pe.wait_ge(l1w_used, 3)
            for k in range(DC):
                last = pe.matmul(ps[:, 0, 0:E], h0rep[:, k], rtw[:, k], start=(k == 0), stop=(k == DC - 1))
            last.then_inc(unit, 1)
            for s in range(2):
                transposes(0, s)

            def mix(g, buf):
                xh = lambda s, k: xs[:, buf, s, k]
                if isinstance(g, int) and g == 0:
                    pe.wait_ge(tb_ready, 1)
                reader_done(g, 0)
                pe.wait_ge(xs_T, 2 * g + 2)
                for q in range(GT):
                    last = split_matmul(ps[:, 0, q * E:(q + 1) * E], lambda s, k: xs[:, buf, s, k, q * P:(q + 1) * P],
                                        lambda s, k: rw_s[:, s, k], range(DC))
                last.then_inc(unit, 1)
                for c in range(HSC):
                    for m, w in enumerate((sw1s, sw3s)):
                        u = U_SHARED + 2 * c + m
                        reader_done(g, u)
                        split_matmul(ps[:, bank_of(u)], lambda s, k: w[:, s, k, c * P:(c + 1) * P], xh,
                                     range(DC)).then_inc(unit, 1)
                for e in range(E):
                    u = U_ROUTED + e
                    reader_done(g, u)
                    split_matmul(ps[:, bank_of(u)], lambda s, k: rw1s[:, s, k, e * P:(e + 1) * P], xh,
                                 range(DC)).then_inc(unit, 1)
                if not is_last(g):
                    for s in range(2):
                        reader_done(g, U_NEXT + s)
                        transposes(g + 1, s)
                for q in range(GT):
                    u = U_OUT + q
                    reader_done(g, u)
                    if q == 0:
                        pe.wait_ge(lo1, HC * g + HSC)
                    split_matmul(ps[:, bank_of(u), 0:D], lambda s, k: hid1[:, s, k, q * P:(q + 1) * P],
                                 lambda s, k: sw2s[:, s, k], range(HSC)).then_inc(unit, 1)
                for p in range(E // 2):
                    for q in range(GT):
                        u = U_PAIR + GT * p + q
                        reader_done(g, u)
                        if q == 0:
                            pe.wait_ge(lo1, HC * g + HSC + 2 * p + 2)
                        for j in range(2):
                            last = split_matmul(ps[:, bank_of(u), j * D:(j + 1) * D],
                                                lambda s, k: hid1[:, s, HSC + 2 * p + j, q * P:(q + 1) * P],
                                                lambda s, k: rw2s[:, s, 2 * p + j], range(1))
                        last.then_inc(unit, 1)

            mix_groups(pe, mix)

        def mixture_act(act):
            def input_hi(g):
                act.activation(xsn[:, 0], x1[:, bass.ds(GT * g, GT)].rearrange("p q d -> p (q d)"), ACT.Copy,
                               scale=A_SCALE).then_inc(xn_hi, 1)

            def input_T(buf, s):
                act.activation(xs[:, buf, s].rearrange("p k n -> p (k n)"), psh(bank_of(U_NEXT + s)), ACT.Copy)\
                   .then_inc(xs_T, 1)

            act.wait_ge(l2_acc, E * TILES)
            input_hi(0)
            for s in range(2):
                act.wait_ge(unit, 2 + s)
                input_T(0, s)

            def mix(g, buf):
                base = PRE_UNITS + UNITS * g
                act.wait_ge(rt_in, g + 1)
                act.activation(score[:], sel[:, 0:GT], ACT.Tanh, scale=0.5).then_inc(rt_sig, 1)
                if not is_last(g):
                    act.wait_ge(xs_T, 2 * g + 2)
                    input_hi(g + 1)

                def hi_part(c):
                    if c < HSC:
                        act.wait_ge(vs_ready, HSC * g + c + 1)
                    else:
                        act.wait_ge(vr_ready, E * g + c - HSC + 1)
                    act.activation(hid1[:, 0, c], vs[:, c % 3], ACT.Copy,
                                   scale=V_SCALE / (2 * MIX_SCALE) if c < HSC else V_SCALE).then_inc(hi1, 1)

                for c in range(HC):
                    u = U_SHARED + 2 * c if c < HSC else U_ROUTED + c - HSC
                    act.wait_ge(unit, base + u + 1)
                    if c < HSC:
                        act.wait_ge(sa_used, HSC * g + max(c - 1, 0))
                        act.activation(v32[:, c % 2], ps[:, bank_of(u)], ACT.Tanh, scale=0.5 / MIX_SCALE)\
                           .then_inc(th_ready, 1)
                    else:
                        act.wait_ge(lo1, HC * g + c - 2)
                        act.activation(vs[:, c % 3], ps[:, bank_of(u)], ACT.Gelu, scale=1.0 / MIX_SCALE)\
                           .then_inc(vr_ready, 1)
                    if c >= 1:
                        hi_part(c - 1)
                hi_part(HC - 1)
                if not is_last(g):
                    for s in range(2):
                        act.wait_ge(unit, base + U_NEXT + s + 1)
                        input_T(1 - buf, s)

            mix_groups(act, mix)

        def mixture_dve(dve):
            dve.wait_ge(l2_acc, E * TILES)
            dve.wait_ge(unit, 1)
            dve.tensor_copy(t_bias[:], ps[:, 0, 0:E]).then_inc(tb_ready, 1)

            def input_lo(g):
                dve.wait_ge(xn_hi, g + 1)
                dve.scalar_tensor_tensor(xsn[:, 1], x1[:, bass.ds(GT * g, GT)].rearrange("p q d -> p (q d)"), A_SCALE,
                                         xsn[:, 0], ALU.mult, ALU.subtract).then_inc(xn_lo, 1)

            input_lo(0)
            wide = [P, GT, E]
            rb = rb_row[:].rearrange("p (a e) -> p a e", a=1).broadcast_to(wide)
            tb = t_bias[:].rearrange("p (a e) -> p a e", a=1).broadcast_to(wide)
            pr = prio[:].rearrange("p (a e) -> p a e", a=1).broadcast_to(wide)
            s, t, o, mk, a, b = sel[:, 0:GT], t8[:, 0:GT], one1[:, 0:GT], mask[:, 0:GT], m1[:, 0:GT], k1[:, 0:GT]

            def mix(g, buf):
                base = PRE_UNITS + UNITS * g
                made = [0]

                def then(ins):
                    made[0] += 1
                    ins.then_inc(router_step, 1)
                    dve.wait_ge(router_step, LINKS * g + made[0])

                dve.wait_ge(unit, base + 1)
                if isinstance(g, int) and g == 0:
                    dve.wait_ge(tb_ready, 1)
                dve.scalar_tensor_tensor(s, ps[:, 0, 0:GT * E].rearrange("p (q e) -> p q e", e=E),
                                         1.0 / MIX_SCALE, tb, ALU.mult, ALU.add).then_inc(rt_in, 1)
                dve.wait_ge(rt_sig, g + 1)
                then(dve.tensor_scalar(score[:], score[:], 0.5, 0.5, ALU.mult, ALU.add))
                then(dve.tensor_tensor(s, score[:], rb, ALU.add))
                for k in range(2):
                    dst = mk if k else o
                    then(dve.tensor_reduce(a, s, AX.X, ALU.max))
                    then(dve.tensor_tensor(t, s, a.broadcast_to(wide), ALU.is_equal))
                    then(dve.tensor_tensor(t, t, pr, ALU.mult))
                    then(dve.tensor_reduce(b, t, AX.X, ALU.max))
                    then(dve.tensor_tensor(dst, t, b.broadcast_to(wide), ALU.is_equal))
                    if k == 0:
                        then(dve.scalar_tensor_tensor(s, dst, -FAR, s, ALU.mult, ALU.add))
                then(dve.tensor_tensor(mk, mk, o, ALU.add))
                then(dve.tensor_tensor(t, score[:], mk, ALU.mult))
                then(dve.tensor_reduce(a, t, AX.X, ALU.add))
                then(dve.tensor_scalar(b, a, EPS_GATE, 1.0 / OUT_SCALE, ALU.is_gt, ALU.mult))
                then(dve.tensor_scalar(a, a, EPS_GATE, None, ALU.add))
                then(dve.reciprocal(a, a))
                then(dve.tensor_tensor(t, t, a.broadcast_to(wide), ALU.mult))
                then(dve.tensor_tensor(t, t, b.broadcast_to(wide), ALU.mult))
                then(dve.tensor_scalar(b, b, -0.5, 0.5 / OUT_SCALE, ALU.mult, ALU.add))
                then(dve.tensor_tensor(mk, mk, b.broadcast_to(wide), ALU.mult))
                then(dve.tensor_tensor(comb[:], t, mk, ALU.add))
                assert made[0] == LINKS
                if not is_last(g):
                    input_lo(g + 1)

                def lo_part(c):
                    dve.wait_ge(hi1, HC * g + c + 1)
                    dve.scalar_tensor_tensor(hid1[:, 1, c], vs[:, c % 3],
                                             V_SCALE / (2 * MIX_SCALE) if c < HSC else V_SCALE, hid1[:, 0, c],
                                             ALU.mult, ALU.subtract).then_inc(lo1, 1)

                for c in range(HSC):
                    dve.wait_ge(th_ready, HSC * g + c + 1)
                    dve.scalar_tensor_tensor(vs[:, c % 3], v32[:, c % 2], 1.0, ps[:, bank_of(U_SHARED + 2 * c)],
                                             ALU.add, ALU.mult).then_inc(sa_used, 1)
                    dve.wait_ge(sa_used, HSC * g + c + 1)
                    dve.wait_ge(unit, base + U_SHARED + 2 * c + 2)
                    dve.scalar_tensor_tensor(vs[:, c % 3], ps[:, bank_of(U_SHARED + 2 * c + 1)], 1.0 / MIX_SCALE,
                                             vs[:, c % 3], ALU.mult, ALU.mult).then_inc(vs_ready, 1)
                    if c >= 1:
                        lo_part(c - 1)
                for c in range(HSC, HC):
                    lo_part(c - 1)
                lo_part(HC - 1)
                if is_last(g):
                    base -= 2
                for q in range(GT):
                    dve.wait_ge(unit, base + U_OUT + q + 1)
                    dve.tensor_scalar(y[:, GT * g + q], ps[:, bank_of(U_OUT + q), 0:D], 1.0 / OUT_SCALE, None,
                                      ALU.mult).then_inc(y_acc, 1)
                for p in range(E // 2):
                    for q2 in range(0, GT, 2):
                        for j in range(2):
                            for q in (q2, q2 + 1):
                                if j == 0:
                                    dve.wait_ge(unit, base + U_PAIR + GT * p + q + 1)
                                before = acc_index(p, q, 0) if j else (acc_index(p - 1, q, 1) if p else q)
                                dve.wait_ge(y_acc, YG * g + before + 1)
                                dve.scalar_tensor_tensor(
                                    y[:, GT * g + q], ps[:, bank_of(U_PAIR + GT * p + q), j * D:(j + 1) * D],
                                    comb[:, q, 2 * p + j:2 * p + j + 1], y[:, GT * g + q], ALU.mult, ALU.add)\
                                   .then_inc(y_acc, 1)
                dve.wait_ge(y_acc, YG * g + YG)
                dve.tensor_reduce(ymax[:, bass.ds(g, 1)], y[:, bass.ds(GT * g, GT)].rearrange("p q d -> p (q d)"),
                                  AX.X, ALU.max).then_inc(ymax_in, 1)

            mix_groups(dve, mix)

        def psb(b, n=1):
            return ps[:, b:b + n].rearrange("p b n -> p (b n)").bitcast(BF16)

        def ffn_pe(pe):
            pe.wait_ge(y_acc, YG * GROUPS)
            for k in range(DC):
                for c in range(FC):
                    last = pe.transpose(psb(k)[:, c * P:(c + 1) * P],
                                        wq_n[:, 0, c * D + k * P:c * D + (k + 1) * P], identb[:])
                last.then_inc(wt_ps, 1)
            for h in range(2):
                for c in range(FC // 2):
                    for k in range(DC):
                        f = FC // 2 * h + c
                        last = pe.transpose(psb(2 + h)[:, c * D + k * P:c * D + (k + 1) * P],
                                            wq_n[:, 1, k * F + f * P:k * F + (f + 1) * P], identb[:])
                last.then_inc(wt_ps, 1)
            for k in range(DC):
                last = pe.matmul(ps[:, 4, k * P:(k + 1) * P], ones[:], diag[:, k], start=True, stop=True)
            last.then_inc(wt_ps, 1)
            for g in range(GROUPS):
                pe.wait_ge(yq_n, g + 1)
                if g >= 2:
                    pe.wait_ge(yq_T, g - 1)
                for k in range(DC):
                    for q in range(GT):
                        last = pe.transpose(psb(5 + g % 2)[:, k * GN + q * P:k * GN + (q + 1) * P],
                                            yqn[:, (g % 2) * GT * D + q * D + k * P:(g % 2) * GT * D + q * D + (k + 1) * P],
                                            identb[:])
                last.then_inc(yq_ps, 1)
            pe.wait_ge(wt_cp, 5)
            pe.wait_ge(yq_T, GROUPS)

            def row_max(f):
                for n in range(4):
                    if not (isinstance(f, int) and f == 0):
                        pe.wait_ge(ia_mx, 4 * (f - 1) + n + 1)
                    for m in range(2):
                        for k in range(DC):
                            last = pe.matmul(ps[:, 2 * n + m], w1qT[:, k, bass.ds(f * P, P)],
                                             yqT[:, k, (2 * n + m) * GN:(2 * n + m + 1) * GN],
                                             start=(k == 0), stop=(k == DC - 1))
                    last.then_inc(ia_ps, 1)

            row_max(0)
            with pe.Fori(1, FC) as f:
                row_max(f)
            pe.wait_ge(ia_mx, 4 * FC)
            with pe.Fori(0, GROUPS) as g:
                for f in range(FC):
                    pe.wait_ge(hb_h, FC * g + max(f - 3, 0))
                    for k in range(DC):
                        last = pe.matmul(ps[:, f % 4], w1qT[:, k, f * P:(f + 1) * P], yqT[:, k, bass.ds(GN * g, GN)],
                                         start=(k == 0), stop=(k == DC - 1))
                    last.then_inc(hb_ps, 1)
                for q in range(GT):
                    if q == 0:
                        pe.wait_ge(ob_s, GT * g)
                    for f in range(FC):
                        if q == 0:
                            pe.wait_ge(hb_q, FC * g + f + 1)
                        last = pe.matmul(ps[:, 4 + q, 0:D], hq[:, f, q * P:(q + 1) * P], w2qT[:, f],
                                         start=(f == 0), stop=(f == FC - 1))
                    last.then_inc(ob_ps, 1)

        def ffn_act(act):
            for n in range(4):
                act.wait_ge(wt_ps, n + 1)
                dst = w1qT[:, n] if n < 2 else w2qT[:, FC // 2 * (n - 2):FC // 2 * (n - 1)].rearrange("p f d -> p (f d)")
                act.activation(dst, psb(n), ACT.Copy).then_inc(wt_cp, 1)
            act.wait_ge(wt_ps, 5)
            act.activation(rs2[:], ps[:, 4, 0:D], ACT.Copy).then_inc(wt_cp, 1)

            def transposed(g):
                act.wait_ge(yq_ps, g + 1)
                act.activation(yqT[:, :, g * GN:(g + 1) * GN], psb(5 + g % 2).rearrange("p (k n) -> p k n", k=DC),
                               ACT.Copy).then_inc(yq_T, 1)

            for g in range(GROUPS):
                act.wait_ge(yq_m, 2 * g + 2)
                if g >= 2:
                    act.wait_ge(yq_ps, g - 1)
                act.activation(yqn[:, (g % 2) * GT * D:(g % 2 + 1) * GT * D],
                               y[:, GT * g:GT * g + GT].rearrange("p q d -> p (q d)"), ACT.Relu,
                               bias=neg_magic[:]).then_inc(yq_n, 1)
                if g >= 1:
                    transposed(g - 1)
            transposed(GROUPS - 1)
            act.wait_ge(bq_ready, 1)
            with act.Fori(0, GROUPS) as g:
                for f in range(FC):
                    act.wait_ge(hb_ps, FC * g + f + 1)
                    act.wait_ge(hb_q, FC * g + max(f - 1, 0))
                    act.activation(v32[:, f % 2], ps[:, f % 4], ACT.Relu, scale=sc1[:, f:f + 1],
                                   bias=fb1[:, f:f + 1]).then_inc(hb_h, 1)

        pool_steps = [0]

        def then_pool(pool, ins):
            pool_steps[0] += 1
            ins.then_inc(pool_step, 1)
            pool.wait_ge(pool_step, pool_steps[0])

        def round_bias(dve, b, scale, r):
            link(dve, dve.reciprocal(r, scale))
            link(dve, dve.tensor_tensor(b, b, r, ALU.mult))
            link(dve, dve.tensor_scalar(b, b, MAGIC, MAGIC, ALU.add, ALU.subtract))
            return dve.tensor_tensor(b, b, scale, ALU.mult)

        def ffn_dve(dve):
            dve.wait_ge(ymax_in, GROUPS)
            link(dve, dve.memset(neg_magic[:], -MAGIC))
            dve.tensor_reduce(pmax[:, 0:1], ymax[:], AX.X, ALU.max).then_inc(mx_in, 1)
            dve.wait_ge(mx_out, 1)
            link(dve, dve.reciprocal(inv[:, 0:1], gmax[:, 0:1]))
            link(dve, dve.tensor_scalar(inv[:, 0:1], inv[:, 0:1], 1.0 / 3.0, None, ALU.mult))
            for g in range(GROUPS):
                yg = y[:, GT * g:GT * g + GT].rearrange("p q d -> p (q d)")
                dve.tensor_scalar(yg, yg, inv[:, 0:1], 255.0, ALU.mult, ALU.min).then_inc(yq_m, 1)
                dve.wait_ge(yq_m, 2 * g + 1)
                dve.tensor_scalar(yg, yg, MAGIC, None, ALU.add).then_inc(yq_m, 1)
            link(dve, dve.tensor_scalar(sc1[:], sw[:, 0:FC], gmax[:, 0:1], None, ALU.mult))
            round_bias(dve, fb1[:], sc1[:], vs[:, 0, 0:FC]).then_inc(bq_ready, 1)

            def row_max(f):
                for n in range(4):
                    dve.wait_ge(ia_ps, 4 * f + n + 1)
                    dve.tensor_reduce(imax[:, f, n:n + 1], ps[:, 2 * n:2 * n + 2].rearrange("p b n -> p (b n)"),
                                      AX.X, ALU.max).then_inc(ia_mx, 1)

            with dve.Fori(0, FC) as f:
                row_max(f)
            dve.wait_ge(ia_mx, 4 * FC)
            dve.wait_ge(bq_ready, 1)
            link(dve, dve.tensor_reduce(hmax[:], imax[:], AX.X, ALU.max))
            link(dve, dve.tensor_tensor(hmax[:], hmax[:], sc1[:], ALU.mult))
            link(dve, dve.tensor_tensor(hmax[:], hmax[:], fb1[:], ALU.add))
            dve.tensor_reduce(pmax[:, 1:2], hmax[:], AX.X, ALU.max).then_inc(mx_in, 1)
            dve.wait_ge(mx_out, 2)
            link(dve, dve.reciprocal(inv[:, 1:2], gmax[:, 1:2]))
            dve.wait_ge(wt_cp, 5)
            link(dve, dve.tensor_scalar(rs2[:], rs2[:], gmax[:, 1:2], None, ALU.mult))
            round_bias(dve, bq2[:], rs2[:], vs[:, 0, 0:D]).then_inc(bq_ready, 1)
            with dve.Fori(0, GROUPS) as g:
                for f in range(FC):
                    dve.wait_ge(hb_h, FC * g + f + 1)
                    dve.tensor_scalar(v32[:, f % 2], v32[:, f % 2], inv[:, 1:2], 255.0, ALU.mult, ALU.min)\
                       .then_inc(hb_s, 1)
                    if f == 0:
                        dve.wait_ge(ob_ps, GT * g)
                    dve.wait_ge(hb_s, FC * g + f + 1)
                    dve.tensor_scalar(hq[:, f], v32[:, f % 2], MAGIC, MAGIC, ALU.add, ALU.subtract).then_inc(hb_q, 1)
                for q in range(GT):
                    dve.wait_ge(ob_ps, GT * g + q + 1)
                    dve.tensor_tensor(vs[:, q % 3, 0:D], ps[:, 4 + q, 0:D], rs2[:], ALU.mult).then_inc(ob_s, 1)
                    if q == 0:
                        dve.wait_ge(xb_ready, g + 1)
                    dve.wait_ge(ob_s, GT * g + q + 1)
                    dve.tensor_tensor(x1[:, GT * g + q], x1[:, GT * g + q], vs[:, q % 3, 0:D], ALU.add).then_inc(ob, 1)

        def ffn_pool(pool):
            pool.wait_ge(wm_ready, 1)
            for m in range(2):
                c = (FC, DC)[m]
                st = stage1[:, 2048 * m:2048 * m + 2048].rearrange("p (c n) -> p c n", c=c)
                for k in range(c):
                    then_pool(pool, pool.tensor_scalar(st[:, k], st[:, k], swr[:, FC * m + k:FC * m + k + 1], None,
                                                       ALU.mult))
                st = stage1[:, 2048 * m:2048 * m + 2048]
                then_pool(pool, pool.tensor_scalar(st, st, -128.0, 127.0, ALU.max, ALU.min))
                then_pool(pool, pool.tensor_scalar(st, st, MAGIC, None, ALU.add))
                then_pool(pool, pool.tensor_scalar(wq_n[:, m], st, MAGIC, None, ALU.subtract))
            for c in range(DC - 1):
                then_pool(pool, pool.tensor_scalar(diag[:, c], ident[:], sw[:, FC + c:FC + c + 1], None, ALU.mult))
            pool.tensor_scalar(diag[:, DC - 1], ident[:], sw[:, FC + DC - 1:FC + DC], None, ALU.mult)\
                .then_inc(l1w_used, 1)

            pool.wait_ge(mx_in, 1)
            then_pool(pool, pool.partition_all_reduce(gmax[:, 0:1], pmax[:, 0:1], P, RMAX))
            then_pool(pool, pool.tensor_scalar(gmax[:, 0:1], gmax[:, 0:1], 1.0 / 3.0, EPS_QUANT, ALU.mult, ALU.max))
            pool.tensor_scalar(gmax[:, 0:1], gmax[:, 0:1], 1.0 / 255.0, None, ALU.mult).then_inc(mx_out, 1)
            pool.wait_ge(mx_in, 2)
            then_pool(pool, pool.partition_all_reduce(gmax[:, 1:2], pmax[:, 1:2], P, RMAX))
            pool.tensor_scalar(gmax[:, 1:2], gmax[:, 1:2], EPS_QUANT, 1.0 / 255.0, ALU.max, ALU.mult).then_inc(mx_out, 1)
            pool.wait_ge(bq_ready, 2)
            wide = bq2[:].rearrange("p (a d) -> p a d", a=1).broadcast_to([P, GT, D])
            with pool.Fori(0, GROUPS) as g:
                xg = x1[:, bass.ds(GT * g, GT)]
                pool.tensor_tensor(xg, xg, wide, ALU.add).then_inc(xb_ready, 1)

        block = ctx.enter_context(nc.Block())

        @block.sync
        def _(sp):
            sp.dma_start(stage[:, 0:1024].rearrange("p (c n) -> p c n", c=4), WT).then_inc(w_in, 16)
            sp.dma_start(h0[:], h0T).then_inc(w_in, 16)
            sp.dma_start(alpha[:], alphaT).then_inc(w_in, 16)
            sp.wait_ge(const0, 1)
            sp.dma_start(b_mat[0:1, :], b_row).then_inc(w_in, 16)
            for j in range(RING):
                sp.dma_start(z[:, j], zT[:, j]).then_inc(z_in[j], 16)
            sp.dma_start(gw[:], gate_wT).then_inc(small_in, 16)
            sp.dma_start(gb_row[:], gate_b.broadcast_to([P, E])).then_inc(small_in, 16)
            sp.dma_start(b1s[:], b1T).then_inc(small_in, 16)
            sp.dma_start(b2stage[0:1], b2).then_inc(small_in, 16)
            sp.dma_start(b2stage[32:33], b2).then_inc(small_in, 16)
            sp.dma_start(x1[:], xn).then_inc(x_in, 16)
            sp.dma_start(rw[:], rwT).then_inc(small_in, 16)
            sp.dma_start(rtw[:], rtwT).then_inc(small_in, 16)
            sp.dma_start(rb_row[:], rbias.broadcast_to([P, E])).then_inc(small_in, 16)
            sp.dma_start(fb1[:], fb1T).then_inc(small_in, 16)
            sp.dma_start(bq2[:], fb2.broadcast_to([P, D])).then_inc(small_in, 16)
            sp.dma_start(stage1[:].rearrange("p (m c n) -> p m c n", m=2, c=8)[:, 0], fw1n).then_inc(l1w_in, 16)
            sp.dma_start(stage1[:].rearrange("p (m c n) -> p m c n", m=2, c=2)[:, 1], fw2n).then_inc(l1w_in, 16)

            def keep_tile(i, j):
                sp.wait_ge(lo_ready, 32 * i + 8 * j + 9)
                sp.dma_start(HT[:, RING * i + j], hring[:, j % 2]).then_inc(ring_out[j % 2], 16)

            with sp.Fori(0, TILES // RING - 1) as i:
                for j in range(RING):
                    keep_tile(i, j)
                    sp.dma_start(z[:, j], zT[:, RING * i + j + RING]).then_inc(z_in[j], 16)
            for j in range(RING):
                keep_tile(TILES // RING - 1, j)
            for q in range(2):
                sp.wait_ge(ring_out[q], 16 * TILES // 2)

            def l1_weights(e):
                if e == 2:
                    sp.wait_ge(l1w_used, 1)
                    sp.dma_start(stage1[:, 0:1024].rearrange("p (c n) -> p c n", c=DC), sw1T).then_inc(l1w_in, 16)
                    sp.dma_start(stage1[:, 1024:2048].rearrange("p (c n) -> p c n", c=DC), sw3T).then_inc(l1w_in, 16)
                    sp.dma_start(stage1[:, 2048:3072].rearrange("p (c n) -> p c n", c=HSC), sw2T).then_inc(l1w_in, 16)
                if e == 4:
                    sp.wait_ge(l1w_used, 2)
                    sp.dma_start(stage1[:, 0:2048].rearrange("p (c n) -> p c n", c=DC), rw1T).then_inc(l1w_in, 16)
                    sp.dma_start(stage1[:, 2048:4096].rearrange("p (c n) -> p c n", c=E), rw2T).then_inc(l1w_in, 16)

            for e in range(E):
                if e == 0:
                    sp.wait_ge(vchain, 5)
                else:
                    sp.wait_ge(ew_split, 4 * e)
                l1_weights(e)
                sp.dma_start(stage[:, 0:2048], w1T[e]).then_inc(ew_in, 16)
                sp.dma_start(stage[:, 2048:4096], w2T[e]).then_inc(ew_in, 16)

            with sp.Fori(0, GROUPS) as g:
                sp.wait_ge(ob, GT * g + GT)
                sp.dma_start(out[:, bass.ds(GT * g, GT)], x1[:, bass.ds(GT * g, GT)]).then_inc(out_done, 16)
            sp.wait_ge(out_done, 16 * GROUPS)

        @block.gpsimd
        def _(pool):
            pool.memset(b_mat[:], 0.0).then_inc(const0, 1)
            pool.memset(b2s[:], 0.0).then_inc(idents, 1)
            pool.memset(a_ones[:], A_SCALE).then_inc(idents, 1)
            for e in range(E):
                pool.memset(prio[:, e:e + 1], float(E - e)).then_inc(idents, 1)
            pool.memset(ident[:], 0.0).then_inc(idents, 1)
            pool.wait_ge(idents, 11)
            pool.affine_select(out=ident[:], in_=ident[:], compare_op=ALU.not_equal, fill=1.0, base=0,
                               pattern=[[-1, P]], channel_multiplier=1).then_inc(idents, 1)
            pool.wait_ge(idents, 12)
            pool.tensor_copy(identb[:], ident[:]).then_inc(idents, 1)
            pool.tensor_copy(identh[:], ident[:]).then_inc(idents, 1)
            ffn_pool(pool)

        @block.scalar
        def _(act):
            def step(i, s):
                j, c = s // STEPS_PER_TILE, (s % STEPS_PER_TILE) * BATCH
                act.wait_ge(pre_ready, 32 * i + s + 1)
                act.activation(gate[:], ps[:, 2 * (j % 2):2 * (j % 2) + 2, c:c + BATCH], ACT.Tanh,
                               scale=0.5 / PRE_SCALE).then_inc(gate_ready, 1)
                act.wait_ge(u_ready, 32 * i + s + 1)
                if s % STEPS_PER_TILE == 0:
                    act.wait_ge(ring_out[j % 2], 32 * i + 16 * (j // 2))
                act.activation(hring[:, j % 2, 0, :, c:c + BATCH], u[:], ACT.Tanh, scale=0.5).then_inc(hi_ready, 1)
                act.activation(h32[:], u[:], ACT.Tanh, scale=0.5).then_inc(h32_ready, 1)

            with act.Fori(0, TILES // RING) as i:
                for s in range(RING * STEPS_PER_TILE):
                    step(i, s)

            for e in range(E):
                with act.Fori(0, GROUPS) as g:
                    for f in range(FC):
                        n = FC * GROUPS * e + f
                        act.wait_ge(l1_psum, n + FC * g + 1)
                        act.wait_ge(l1_hid, FC * g + max(n - 1, 0))
                        act.activation(v32[:, f % 2], ps[:, f % 4], ACT.Relu, bias=b1s[:, e, f:f + 1],
                                       scale=A_SCALE / W_SCALE).then_inc(l1_v, 1)
            mixture_act(act)
            ffn_act(act)

        @block.vector
        def _(dve):
            dve.memset(ones[:], 1.0).then_inc(prep, 1)
            dve.memset(leak[:], 1.0).then_inc(prep, 1)
            dve.wait_ge(w_in, 64)
            dve.wait_ge(prep, 2)
            wst = stage[:, 0:1024].rearrange("p (c n) -> p c n", c=4)
            dve.tensor_scalar(wh_hi[:], wst[:, 0:2], W_SCALE, None, ALU.mult).then_inc(prep, 1)
            dve.tensor_scalar(wz[:], wst[:, 2:4], PRE_SCALE, None, ALU.mult).then_inc(prep, 1)
            dve.tensor_scalar(b_mat[:], b_mat[:], PRE_SCALE, None, ALU.mult).then_inc(prep, 1)
            dve.tensor_scalar(alpha[:], alpha[:], -2.0, 2.0, ALU.mult, ALU.add).then_inc(prep, 1)
            dve.wait_ge(prep, 6)
            dve.scalar_tensor_tensor(wh_lo[:], wst[:, 0:2], W_SCALE, wh_hi[:], ALU.mult, ALU.subtract).then_inc(prep, 1)
            for c in range(DC):
                dve.tensor_scalar(leak[:, c], leak[:, c], alpha[:, c:c + 1], None, ALU.mult).then_inc(prep, 1)
            dve.wait_ge(prep, 9)
            h_hi, h_lo = hring[:, 1, 0, :, P - BATCH:P], hring[:, 1, 1, :, P - BATCH:P]
            dve.tensor_copy(h_hi, h0[:]).then_inc(prep, 1)
            dve.tensor_tensor(hleak[:], h0[:], leak[:], ALU.mult).then_inc(hleak_ready, 1)
            dve.wait_ge(prep, 10)
            dve.tensor_tensor(h_lo, h0[:], h_hi, ALU.subtract).then_inc(lo_ready, 1)

            def step(i, s):
                j, c = s // STEPS_PER_TILE, (s % STEPS_PER_TILE) * BATCH
                if s % STEPS_PER_TILE == 0:
                    dve.wait_ge(z_in[j], 16 * i + 16)
                dve.wait_ge(gate_ready, 32 * i + s + 1)
                dve.scalar_tensor_tensor(gz[:], gate[:], 1.0, z[:, j, :, c:c + BATCH], ALU.add, ALU.mult)\
                   .then_inc(gz_ready, 1)
                dve.wait_ge(gz_ready, 32 * i + s + 1)
                dve.wait_ge(hleak_ready, 32 * i + s + 1)
                dve.tensor_tensor(u[:], gz[:], hleak[:], ALU.add).then_inc(u_ready, 1)
                dve.wait_ge(h32_ready, 32 * i + s + 1)
                dve.tensor_tensor(hring[:, j % 2, 1, :, c:c + BATCH], h32[:], hring[:, j % 2, 0, :, c:c + BATCH],
                                  ALU.subtract).then_inc(lo_ready, 1)
                dve.tensor_tensor(hleak[:], h32[:], leak[:], ALU.mult).then_inc(hleak_ready, 1)

            with dve.Fori(0, TILES // RING) as i:
                for s in range(RING * STEPS_PER_TILE):
                    step(i, s)

            dve.wait_ge(small_in, 160)
            dve.wait_ge(idents, 14)
            link(dve, dve.tensor_scalar(gw_s[:, 0], gw[:], W_SCALE, None, ALU.mult))
            link(dve, dve.scalar_tensor_tensor(gw_s[:, 1], gw[:], W_SCALE, gw_s[:, 0], ALU.mult, ALU.subtract))
            link(dve, dve.tensor_scalar(b2s[0:1], b2stage[0:1], W_SCALE, None, ALU.mult))
            link(dve, dve.tensor_scalar(b2s[32:33], b2stage[32:33], W_SCALE, None, ALU.mult))
            link(dve, dve.scalar_tensor_tensor(b2s[32:33], b2stage[32:33], W_SCALE, b2s[32:33], ALU.mult, ALU.subtract))
            dve.tensor_scalar(b1s[:], b1s[:], A_SCALE, None, ALU.mult).then_inc(prep, 1)
            dve.wait_ge(logits_ready, 1)
            lg = ps[:, 4, 0:TILES * E].rearrange("p (j e) -> p j e", e=E)
            gb = gb_row[:].rearrange("p (a e) -> p a e", a=1).broadcast_to([P, TILES, E])
            link(dve, dve.tensor_scalar(sel[:], lg, 1.0 / W_SCALE, None, ALU.mult))
            link(dve, dve.tensor_tensor(sel[:], sel[:], gb, ALU.add))
            top2(dve, TILES)
            link(dve, dve.tensor_scalar(mask[:], mask[:], 1.0 / (W_SCALE * A_SCALE), None, ALU.mult))
            dve.wait_ge(x_in, 16)

            def l1_prepare(e):
                if e == 0:
                    dve.wait_ge(l1w_in, 32)
                    for m in range(2):
                        c = (FC, DC)[m]
                        st = stage1[:, 2048 * m:2048 * m + 2048].rearrange("p (c n) -> p c n", c=c)
                        s_, a_ = sw[:, FC * m:FC * m + c], swr[:, FC * m:FC * m + c]
                        link(dve, dve.tensor_reduce(s_, st, AX.X, ALU.max))
                        link(dve, dve.tensor_reduce(a_, st, AX.X, ALU.min))
                        link(dve, dve.scalar_tensor_tensor(s_, a_, -1.0, s_, ALU.mult, ALU.max))
                    link(dve, dve.tensor_scalar(sw[:], sw[:], EPS_QUANT, 1.0 / 127.0, ALU.max, ALU.mult))
                    dve.reciprocal(swr[:], sw[:]).then_inc(wm_ready, 1)
                    for c in range(DC):
                        link(dve, dve.tensor_copy(
                            h0rep[:, c].rearrange("p (r b) -> p r b", b=BATCH),
                            h0[:, c:c + 1].broadcast_to([P, P // BATCH, BATCH])))
                    link(dve, dve.tensor_scalar(rw_s[:, 0], rw[:], W_SCALE, None, ALU.mult))
                    link(dve, dve.scalar_tensor_tensor(rw_s[:, 1], rw[:], W_SCALE, rw_s[:, 0], ALU.mult, ALU.subtract))
                if e in (3, 5):
                    a, n = (0, 3072) if e == 3 else (3072, 4096)
                    dve.wait_ge(l1w_in, 80 if e == 3 else 112)
                    link(dve, dve.tensor_scalar(l1w[:, 0, a:a + n], stage1[:, 0:n], W_SCALE, None, ALU.mult))
                    dve.scalar_tensor_tensor(l1w[:, 1, a:a + n], stage1[:, 0:n], W_SCALE, l1w[:, 0, a:a + n],
                                             ALU.mult, ALU.subtract).then_inc(l1w_used, 1)

            for e in range(E):
                dve.wait_ge(ew_in, 32 * (e + 1))
                if e >= 2:
                    dve.wait_ge(l2_psum, TILES * (e - 1))
                for m in range(2):
                    st = stage[:, 2048 * m:2048 * m + 2048]
                    dve.tensor_scalar(wsplit[:, e % 2, m, 0], st, W_SCALE, None, ALU.mult).then_inc(ew_split, 1)
                    dve.wait_ge(ew_split, 4 * e + 2 * m + 1)
                    dve.scalar_tensor_tensor(wsplit[:, e % 2, m, 1], st, W_SCALE, wsplit[:, e % 2, m, 0],
                                             ALU.mult, ALU.subtract).then_inc(ew_split, 1)
                with dve.Fori(0, GROUPS) as g:
                    for f in range(FC):
                        n = FC * GROUPS * e + f
                        dve.wait_ge(l1_v, n + FC * g + 1)
                        dve.wait_ge(l2_psum, GT * GROUPS * e + GT * g)
                        dve.tensor_copy(hid[:, 0, f], v32[:, f % 2]).then_inc(split0, 1)
                        dve.wait_ge(split0, n + FC * g + 1)
                        dve.tensor_tensor(hid[:, 1, f], v32[:, f % 2], hid[:, 0, f], ALU.subtract).then_inc(l1_hid, 1)
                    for q in range(GT):
                        dve.wait_ge(l2_psum, GT * GROUPS * e + GT * g + q + 1)
                        dve.scalar_tensor_tensor(x1[:, GT * g + q], ps[:, 4 + q % 4, 0:D], mask[:, GT * g + q, e:e + 1],
                                                 x1[:, GT * g + q], ALU.mult, ALU.add).then_inc(l2_acc, 1)
                l1_prepare(e)
            mixture_dve(dve)
            ffn_dve(dve)

        @block.tensor
        def _(pe):
            def z_part(slot, part):
                m, k = part // 3, part % 3
                dst = ps[:, 2 * (slot % 2) + m, 0:P]
                cols = slice(m * P, (m + 1) * P)
                if k < 2:
                    pe.matmul(dst, wz[:, k, cols], z[:, slot, k, :], start=(k == 0), stop=False, skip_group_check=True)
                else:
                    pe.matmul(dst, b_mat[:, cols], ones[:], start=False, stop=False, skip_group_check=True)

            def step(i, s, last_tile=False):
                j, c = s // STEPS_PER_TILE, (s % STEPS_PER_TILE) * BATCH
                half, b = j % 2, 2 * (j % 2)
                prev, pc = (half, c - BATCH) if s % STEPS_PER_TILE else (1 - half, P - BATCH)
                pe.wait_ge(hi_ready, 32 * i + s)
                for w in (wh_hi, wh_lo):
                    for m in range(DC):
                        for k in range(DC):
                            pe.matmul(ps[:, b + m, c:c + BATCH], w[:, k, m * P:(m + 1) * P],
                                      hring[:, prev, 0, k, pc:pc + BATCH], start=False, stop=False, skip_group_check=True)
                pe.wait_ge(lo_ready, 32 * i + s + 1)
                for m in range(DC):
                    for k in range(DC):
                        last = pe.matmul(ps[:, b + m, c:c + BATCH], wh_hi[:, k, m * P:(m + 1) * P],
                                         hring[:, prev, 1, k, pc:pc + BATCH], start=False, stop=(k == DC - 1),
                                         skip_group_check=True)
                last.then_inc(pre_ready, 1)
                part = s % STEPS_PER_TILE
                if part < 3 * DC and not last_tile:
                    if part == 0:
                        pe.wait_ge(z_in[(j + 1) % RING], 16 * i + (32 if j == RING - 1 else 16))
                    z_part((j + 1) % RING, part)

            pe.wait_ge(prep, 10)
            pe.wait_ge(z_in[0], 16)
            for part in range(3 * DC):
                z_part(0, part)
            steps = RING * STEPS_PER_TILE
            with pe.Fori(0, TILES // RING - 1) as i:
                for s in range(steps):
                    step(i, s)
            for s in range(steps):
                step(TILES // RING - 1, s, last_tile=s >= steps - STEPS_PER_TILE)

            pe.wait_ge(ring_out[0], 16 * TILES // 2)
            pe.wait_ge(ring_out[1], 16 * TILES // 2)
            pe.wait_ge(vchain, 2)
            for j in range(TILES):
                for n, (a, b) in enumerate(((0, 0), (0, 1), (1, 0))):
                    for k in range(DC):
                        last = pe.matmul(ps[:, 4, j * E:(j + 1) * E], HT[:, j, a, k], gw_s[:, b, k],
                                         start=(n == 0 and k == 0), stop=(n == 2 and k == DC - 1))
            last.then_inc(logits_ready, 1)
            pe.wait_ge(vchain, 5)
            pe.wait_ge(prep, 11)

            for e in range(E):
                w = wsplit[:, e % 2]
                w1 = w[:, 0].rearrange("p s (k f) -> p s k f", k=DC)
                w2 = w[:, 1].rearrange("p s (f d) -> p s f d", f=FC)
                pe.wait_ge(ew_split, 4 * (e + 1))
                with pe.Fori(0, GROUPS) as g:
                    for f in range(FC):
                        n = FC * GROUPS * e + f
                        pe.wait_ge(l1_v, FC * g + max(n - 3, 0))
                        for q, (a, b) in enumerate(((0, 0), (0, 1), (1, 0))):
                            for k in range(DC):
                                last = pe.matmul(ps[:, f % 4], w1[:, a, k, f * P:(f + 1) * P],
                                                 HT[:, bass.ds(GT * g, GT), b, k],
                                                 start=(q == 0 and k == 0), stop=(q == 2 and k == DC - 1))
                        last.then_inc(l1_psum, 1)
                    for q in range(GT):
                        if q == 0:
                            pe.wait_ge(l2_acc, GT * GROUPS * e + GT * g)
                        dst = ps[:, 4 + q, 0:D]
                        pe.matmul(dst, a_ones[:], b2s[:, e], start=True, stop=False)
                        for f in range(FC):
                            pe.wait_ge(l1_hid, FC * GROUPS * e + FC * g + f + 1) if q == 0 else None
                            for n, (a, b) in enumerate(((0, 0), (0, 1), (1, 0))):
                                last = pe.matmul(dst, hid[:, a, f, q * P:(q + 1) * P], w2[:, b, f],
                                                 start=False, stop=(n == 2 and f == FC - 1))
                        last.then_inc(l2_psum, 1)
            mixture_pe(pe)
            ffn_pe(pe)


_INS = ['zT', 'xn', 'h0T', 'WT', 'b_row', 'alphaT', 'gate_wT', 'gate_b', 'w1T', 'b1T', 'w2T', 'b2', 'rwT', 'rtwT', 'rbias',
        'sw1T', 'sw3T', 'sw2T', 'rw1T', 'rw2T', 'fw1n', 'fb1T', 'fw2n', 'fb2']


def kernel(x, cond_1024, L0_cond_W, L0_cond_b, L0_cond_alpha, L0_ffn_gate_w, L0_ffn_gate_b, L0_ffn_w1, L0_ffn_b1,
           L0_ffn_w2, L0_ffn_b2, L1_cond_router_w, L1_cond_router_t_w, L1_cond_router_bias, L1_cond_sw1, L1_cond_sw3,
           L1_cond_sw2, L1_cond_rw1, L1_cond_rw2, L1_ffn_w1, L1_ffn_b1, L1_ffn_w2, L1_ffn_b2):
    import numpy as np
    import concourse.bacc as bacc
    from concourse.bass_utils import run_bass_kernel_spmd as run

    def rows(a):
        return np.asarray(a).reshape(-1, P, a.shape[-1]).transpose(1, 0, 2)

    x = np.asarray(x)
    arrays = {
        "zT": x.transpose(2, 1, 0).reshape(DC, P, TILES, P).transpose(1, 2, 0, 3),
        "xn": x.transpose(1, 0, 2).reshape(TILES, P, D).transpose(1, 0, 2),
        "h0T": rows(np.asarray(cond_1024).T),
        "WT": rows(np.asarray(L0_cond_W).T),
        "b_row": np.asarray(L0_cond_b)[None],
        "alphaT": np.asarray(L0_cond_alpha).reshape(DC, P).T,
        "gate_wT": rows(L0_ffn_gate_w),
        "gate_b": np.asarray(L0_ffn_gate_b)[None],
        "w1T": np.asarray(L0_ffn_w1).reshape(E, DC, P, F).transpose(0, 2, 1, 3).reshape(E, P, DC * F),
        "b1T": np.asarray(L0_ffn_b1).reshape(E, FC, P).transpose(2, 0, 1),
        "w2T": np.asarray(L0_ffn_w2).reshape(E, FC, P, D).transpose(0, 2, 1, 3).reshape(E, P, FC * D),
        "b2": np.asarray(L0_ffn_b2)[None],
        "rwT": rows(np.asarray(L1_cond_router_w).T),
        "rtwT": rows(np.asarray(L1_cond_router_t_w).T),
        "rbias": np.asarray(L1_cond_router_bias)[None],
        "sw1T": rows(np.asarray(L1_cond_sw1).T),
        "sw3T": rows(np.asarray(L1_cond_sw3).T),
        "sw2T": rows(np.asarray(L1_cond_sw2).T),
        "rw1T": rows(np.asarray(L1_cond_rw1).transpose(2, 0, 1).reshape(D, E * P)),
        "rw2T": np.asarray(L1_cond_rw2).transpose(2, 0, 1),
        "fw1n": rows(L1_ffn_w1),
        "fb1T": np.asarray(L1_ffn_b1).reshape(FC, P).T,
        "fw2n": rows(L1_ffn_w2),
        "fb2": np.asarray(L1_ffn_b2)[None],
    }
    arrays = {k: np.ascontiguousarray(v) for k, v in arrays.items()}
    nc = bacc.Bacc("TRN2", target_bir_lowering=False, num_devices=1)
    args = [nc.dram_tensor(f"in_{n}", arrays[n].shape, F32, kind="ExternalInput").ap() for n in _INS]
    args.append(nc.dram_tensor("out", (P, TILES, D), F32, kind="ExternalOutput").ap())
    build_program(nc, *args)
    r = run(nc, [{f"in_{n}": arrays[n] for n in _INS}], core_ids=[0])
    got = r.results[0]["out"]
    return np.ascontiguousarray(got.transpose(1, 0, 2).reshape(STEPS, BATCH, D).transpose(1, 0, 2))
```

```python
from contextlib import ExitStack

import concourse.bass as bass
from concourse import mybir

P = 128
BATCH, STEPS, D = 16, 256, 256
N = BATCH * STEPS
TILES = N // P
STEPS_PER_TILE = P // BATCH
DC = D // P
E = 8
F = 1024
FC = F // P
HS = 512
HSC = HS // P
GT = 4
GROUPS = TILES // GT
GN = GT * P
RING = 4

W_SCALE = 256.0
A_SCALE = 16.0
PRE_SCALE = W_SCALE
MAGIC = 12582912.0
ST = 256
SQ = ST // P
PAIRS = 2 * N
SLOT_TILES = (PAIRS + E * (ST - 1)) // ST
BLOCKS = SLOT_TILES * SQ
JOBS = 9
EPS_GATE = 1e-9
EPS_QUANT = 1e-8
FAR = 1e30

ALU = mybir.AluOpType
ACT = mybir.ActivationFunctionType
AX = mybir.AxisListType
F32 = mybir.dt.float32
F16 = mybir.dt.float16
BF16 = mybir.dt.bfloat16
I32 = mybir.dt.int32
U32 = mybir.dt.uint32
RMAX = bass.bass_isa.ReduceOp.max

HC = HSC + E
U_SHARED, U_ROUTED = 1, 1 + 2 * HSC
U_NEXT = U_ROUTED + E
U_OUT = U_NEXT + DC
U_PAIR = U_OUT + GT
UNITS = U_PAIR + GT * E // 2
PRE_UNITS = 1 + DC
YG = GT * (1 + E)
MIX_SCALE = W_SCALE * A_SCALE
LINKS = 24
V_SCALE = 4.0
OUT_SCALE = W_SCALE * V_SCALE

C_LANE, C_BLOCK = 0, P
C_TILE = C_BLOCK + BLOCKS
C_PAD = C_TILE + 2 * TILES
C_PART = C_PAD + BLOCKS
C_SLOT_TILE = C_PART + 1
C_TRI = C_SLOT_TILE + SLOT_TILES
CONSTS = C_TRI + P


def build_program(nc, zT, xn, h0T, WT, b_row, alphaT, gate_wT, gate_b, w1T, b1T, w2T, b2, rwT, rtwT, rbias,
                  sw1T, sw3T, sw2T, rw1T, rw2T, fw1n, fb1T, fw2n, fb2, const, rows_d, pairs_d, out):
    ctx = ExitStack()
    with ctx:
        def sb(name, shape, dt):
            return ctx.enter_context(nc.sbuf_tensor(name, shape, dt))

        def sem(name):
            return ctx.enter_context(nc.semaphore(name))

        ps = ctx.enter_context(nc.psum_tensor("ps", [P, 8, 512], F32))
        W = sb("W", [P, 2, E, 2, 2048], F16)
        W1 = W[:, 0].rearrange("p e s (k f) -> p e s k f", k=DC)
        W2 = W[:, 1].rearrange("p e s (f d) -> p e s f d", f=FC)
        area = W[:].rearrange("p m e s n -> p (m e s n)").bitcast(F32)

        def carve(a):
            at = [0]

            def part(n, dt=F32):
                size = n if dt == F32 else n // 2
                piece = a[:, at[0]:at[0] + size]
                at[0] += size
                assert at[0] <= a.shape[-1], at
                return piece if dt == F32 else piece.bitcast(dt)
            return part

        part = carve(area)
        x1 = part(TILES * D).rearrange("p (j d) -> p j d", d=D)
        y = part(TILES * D).rearrange("p (j d) -> p j d", d=D)
        hid1_flat = part(2 * HC * GN, F16)
        hid1 = hid1_flat.rearrange("p (s c n) -> p s c n", s=2, c=HC)
        yqT = hid1_flat[:, 0:DC * N].bitcast(BF16).rearrange("p (k n) -> p k n", k=DC)
        xs = part(2 * 2 * DC * GN, F16).rearrange("p (b s k n) -> p b s k n", b=2, s=2, k=DC)
        xsn_flat = part(2 * GT * D, F16)
        xsn = xsn_flat.rearrange("p (s n) -> p s n", s=2)
        yqn = xsn_flat.bitcast(BF16)
        vs = part(3 * GN).rearrange("p (b n) -> p b n", b=3)
        o_in = part(2 * 2 * GT * D).rearrange("p (b k q d) -> p b k q d", b=2, k=2, d=D)
        diag = part(DC * P).rearrange("p (c n) -> p c n", c=DC)
        h0rep = part(DC * P).rearrange("p (c n) -> p c n", c=DC)
        rs2 = part(D)
        bq2 = part(D)

        work = sb("work", [P, 9216], F32)
        part = carve(work[:])
        l1w = part(2 * 7168, F16).rearrange("p (s n) -> p s n", s=2)
        sw1s = l1w[:, :, 0:1024].rearrange("p s (k h) -> p s k h", k=DC)
        sw3s = l1w[:, :, 1024:2048].rearrange("p s (k h) -> p s k h", k=DC)
        sw2s = l1w[:, :, 2048:3072].rearrange("p s (k d) -> p s k d", k=HSC)
        rw1s = l1w[:, :, 3072:5120].rearrange("p s (k h) -> p s k h", k=DC)
        rw2s = l1w[:, :, 5120:7168].rearrange("p s (e d) -> p s e d", e=E)
        wq_n = part(2 * 2048, BF16).rearrange("p (m n) -> p m n", m=2)
        w1qT = l1w[:, 0, 0:DC * F].bitcast(BF16).rearrange("p (k f) -> p k f", k=DC)
        w2qT = l1w[:, 1, 0:FC * D].bitcast(BF16).rearrange("p (f d) -> p f d", f=FC)
        part = carve(work[:])
        lane1h = part(2 * TILES * P, BF16).rearrange("p (t n) -> p t n", n=P)
        block1h = part(2 * TILES * 2 * BLOCKS, BF16).rearrange("p (t v n) -> p t v n", v=2, n=BLOCKS)
        part = carve(work[:])
        wst = part(4 * D).rearrange("p (c n) -> p c n", c=4)
        b2st = part(E * D).rearrange("p (e d) -> p e d", e=E)
        stage = sb("stage", [P, 2, 1024], F32)

        lane = sb("lane", [P, 6144], F32)
        part = carve(lane[:])
        z = part(RING * DC * P).rearrange("p (r c n) -> p r c n", r=RING, c=DC)
        hring = part(2 * 2 * DC * P, F16).rearrange("p (h s c n) -> p h s c n", h=2, s=2, c=DC)
        wh_hi = part(DC * D, F16).rearrange("p (c n) -> p c n", c=DC)
        wh_lo = part(DC * D, F16).rearrange("p (c n) -> p c n", c=DC)
        wz = part(DC * D).rearrange("p (c n) -> p c n", c=DC)
        b_mat = part(D)
        hrow = part(2 * 2 * D, F16).rearrange("p (h n) -> p h n", h=2)
        sel = part(TILES * E).rearrange("p (j e) -> p j e", e=E)
        t8 = part(TILES * E).rearrange("p (j e) -> p j e", e=E)
        chosen = part(2 * TILES * E).rearrange("p (k j e) -> p k j e", k=2, e=E)
        slotf = part(TILES * E).rearrange("p (j e) -> p j e", e=E)
        m16 = part((TILES + 1) * E, BF16).rearrange("p (j e) -> p j e", e=E)
        m1 = part(TILES).rearrange("p (j a) -> p j a", a=1)
        k1 = part(TILES).rearrange("p (j a) -> p j a", a=1)
        slot = part(2 * TILES).rearrange("p (k j) -> p k j", k=2)
        le_n = part(SLOT_TILES * (E - 1)).rearrange("p (n e) -> p n e", e=E - 1)
        eot_f = part(SLOT_TILES)
        cst = part(CONSTS)
        tri = part(P, BF16)
        ones16 = part(P, BF16)
        inv3 = part(3 * BLOCKS).rearrange("p (k n) -> p k n", k=3)
        part = carve(lane[:])
        xg = part(2 * SQ * 2 * D, F16).rearrange("p (b q n) -> p b q n", b=2, q=SQ)
        xT = part(2 * 2 * DC * ST, F16).rearrange("p (b s k n) -> p b s k n", b=2, s=2, k=DC)
        hid = part(2 * FC * ST, F16).rearrange("p (s f n) -> p s f n", s=2, f=FC)
        hq = hid.rearrange("p s f n -> p (s f n)").bitcast(BF16).rearrange("p (f n) -> p f n", f=FC)
        v_flat = part(4 * ST)
        v4 = v_flat.rearrange("p (b n) -> p b n", b=4)
        v32 = v_flat.rearrange("p (b n) -> p b n", b=2)
        obuf = part(2 * SQ * D).rearrange("p (b q d) -> p b q d", b=2, q=SQ)

        ones = sb("ones", [P, P], F32)
        h0 = sb("h0", [P, DC, BATCH], F32)
        alpha = sb("alpha", [P, DC], F32)
        leak = sb("leak", [P, DC, BATCH], F32)
        gate = sb("gate", [P, DC, BATCH], F32)
        gz = sb("gz", [P, DC, BATCH], F32)
        u = sb("u", [P, DC, BATCH], F32)
        h32 = sb("h32", [P, DC, BATCH], F32)
        hleak = sb("hleak", [P, DC, BATCH], F32)
        cst16 = sb("cst16", [P, P + BLOCKS + 2 * TILES], BF16)
        sums = sb("sums", [P, 4, 2 * E], F32)
        first = sb("first", [P, E], F32)
        hi16 = sb("hi16", [P, 2 * TILES], BF16)
        lo16 = sb("lo16", [P, 2 * TILES], BF16)
        row_of = sb("row_of", [P, BLOCKS], U32)
        pair_of = sb("pair_of", [P, BLOCKS], U32)
        expert_of = sb("expert_of", [P, SLOT_TILES], I32)
        row_now = sb("row_now", [P, 2, SQ], U32)
        pair_now = sb("pair_now", [P, 2, SQ], U32)
        b1_now = sb("b1_now", [P, 2, FC], F32)
        w_scale = sb("w_scale", [P, 1], F32)
        inv = sb("inv", [P, 2], F32)
        neg_magic = sb("neg_magic", [P, 1], F32)
        sw = sb("sw", [P, FC + DC], F32)
        swr = sb("swr", [P, FC + DC], F32)
        fb1 = sb("fb1", [P, FC], F32)
        sc1 = sb("sc1", [P, FC], F32)
        imax = sb("imax", [P, FC, 4], F32)
        ymax = sb("ymax", [P, GROUPS], F32)
        pmax = sb("pmax", [P, 2], F32)
        gmax = sb("gmax", [P, 2], F32)
        hmax = sb("hmax", [P, FC], F32)
        rtw = sb("rtw", [P, DC, E], F32)
        rw = sb("rw", [P, DC, E], F32)
        rw_s = sb("rw_s", [P, 2, DC, E], F16)
        rb_row = sb("rb_row", [P, E], F32)
        t_bias = sb("t_bias", [P, E], F32)
        score = sb("score", [P, GT, E], F32)
        r_sel = sb("r_sel", [P, GT, E], F32)
        r_t8 = sb("r_t8", [P, GT, E], F32)
        r_one = sb("r_one", [P, GT, E], F32)
        r_mask = sb("r_mask", [P, GT, E], F32)
        r_m1 = sb("r_m1", [P, GT, 1], F32)
        r_k1 = sb("r_k1", [P, GT, 1], F32)
        comb = sb("comb", [P, GT, E], F32)
        gw = sb("gw", [P, DC, E], F32)
        gw_s = sb("gw_s", [P, 2, DC, E], F16)
        gb_row = sb("gb_row", [P, E], F32)
        b1s = sb("b1s", [P, E, FC], F32)
        b2s = sb("b2s", [P, E, D], F16)
        a_ones = sb("a_ones", [P, P], F16)
        prio = sb("prio", [P, E], F32)
        ident = sb("ident", [P, P], F32)
        identb = sb("identb", [P, P], BF16)
        identh = sb("identh", [P, P], F16)

        w_in = sem("w_in")
        small_in = sem("small_in")
        const0 = sem("const0")
        idents = sem("idents")
        z_in = [sem(f"z_in{i}") for i in range(RING)]
        prep = sem("prep")
        row_ps = sem("row_ps")
        row_cp = sem("row_cp")
        row_out = [sem(f"row_out{i}") for i in range(2)]
        logits_ready = sem("logits_ready")
        piece_in = [sem(f"piece_in{i}") for i in range(2)]
        w_split = sem("w_split")
        b2_ready = sem("b2_ready")
        gw_in = sem("gw_in")
        chosen_ready = sem("chosen_ready")
        pos_ready = sem("pos_ready")
        onehots = sem("onehots")
        slots_ready = sem("slots_ready")
        route_done = sem("route_done")
        row_idx = sem("row_idx")
        pair_idx = sem("pair_idx")
        b1_ready = sem("b1_ready")
        xg_in = [sem(f"xg_in{i}") for i in range(2)]
        xT_ps = sem("xT_ps")
        xT_ready = sem("xT_ready")
        out_ready = sem("out_ready")
        pairs_out = [sem(f"pairs_out{i}") for i in range(2)]
        mw_in = [sem(f"mw_in{i}") for i in range(2)]
        mw_used = sem("mw_used")
        x_in = [sem(f"x_in{i}") for i in range(2)]
        o_arrived = [sem(f"o_arrived{i}") for i in range(2)]
        x1_step = sem("x1_step")
        x1_ready = sem("x1_ready")
        mix_start = sem("mix_start")
        diag_ready = sem("diag_ready")
        bq2_in = sem("bq2_in")
        pre_ready = sem("pre_ready")
        gate_ready = sem("gate_ready")
        gz_ready = sem("gz_ready")
        u_ready = sem("u_ready")
        hi_ready = sem("hi_ready")
        h32_ready = sem("h32_ready")
        lo_ready = sem("lo_ready")
        hleak_ready = sem("hleak_ready")
        vchain = sem("vchain")
        l1_psum = sem("l1_psum")
        l1_v = sem("l1_v")
        split0 = sem("split0")
        l1_hid = sem("l1_hid")
        l2_psum = sem("l2_psum")
        out_done = sem("out_done")
        xn_hi = sem("xn_hi")
        xn_lo = sem("xn_lo")
        xs_T = sem("xs_T")
        unit = sem("unit")
        sa_used = sem("sa_used")
        tb_ready = sem("tb_ready")
        router_step = sem("router_step")
        ymax_in = sem("ymax_in")
        wm_ready = sem("wm_ready")
        pool_step = sem("pool_step")
        bq_ready = sem("bq_ready")
        xb_ready = sem("xb_ready")
        rt_in = sem("rt_in")
        rt_sig = sem("rt_sig")
        th_ready = sem("th_ready")
        vs_ready = sem("vs_ready")
        vr_ready = sem("vr_ready")
        hi1 = sem("hi1")
        lo1 = sem("lo1")
        y_acc = sem("y_acc")
        mx_in = sem("mx_in")
        mx_out = sem("mx_out")
        wt_ps = sem("wt_ps")
        wt_cp = sem("wt_cp")
        yq_m = sem("yq_m")
        yq_n = sem("yq_n")
        yq_ps = sem("yq_ps")
        yq_T = sem("yq_T")
        ia_ps = sem("ia_ps")
        ia_mx = sem("ia_mx")
        hb_ps = sem("hb_ps")
        hb_h = sem("hb_h")
        hb_q = sem("hb_q")
        hb_s = sem("hb_s")
        ob_ps = sem("ob_ps")
        ob_s = sem("ob_s")
        ob = sem("ob")

        count = {"v": 0}

        def link(dve, ins):
            count["v"] += 1
            ins.then_inc(vchain, 1)
            dve.wait_ge(vchain, count["v"])

        def route(dve):
            wide = [P, TILES, E]
            dve.wait_ge(logits_ready, 1)
            lg = ps[:, 5, E:(TILES + 1) * E].rearrange("p (j e) -> p j e", e=E)
            gb = gb_row[:].rearrange("p (a e) -> p a e", a=1).broadcast_to(wide)
            pr = prio[:].rearrange("p (a e) -> p a e", a=1).broadcast_to(wide)
            link(dve, dve.tensor_scalar(sel, lg, 1.0 / W_SCALE, None, ALU.mult))
            link(dve, dve.tensor_tensor(sel, sel, gb, ALU.add))
            for k in range(2):
                link(dve, dve.tensor_reduce(m1, sel, AX.X, ALU.max))
                link(dve, dve.tensor_tensor(t8, sel, m1.broadcast_to(wide), ALU.is_equal))
                link(dve, dve.tensor_tensor(t8, t8, pr, ALU.mult))
                link(dve, dve.tensor_reduce(k1, t8, AX.X, ALU.max))
                link(dve, dve.tensor_tensor(chosen[:, k], t8, k1.broadcast_to(wide), ALU.is_equal))
                if k == 0:
                    link(dve, dve.scalar_tensor_tensor(sel, chosen[:, k], -FAR, sel, ALU.mult, ALU.add))
            link(dve, dve.memset(m16[:, TILES], 0.0))
            dve.tensor_tensor(m16[:, 0:TILES], chosen[:, 0], chosen[:, 1], ALU.add).then_inc(chosen_ready, 1)
            dve.wait_ge(pos_ready, 1)
            s = lambda n, a: sums[:, n, E - a:2 * E - a]
            link(dve, dve.tensor_scalar(s(0, 0), ps[:, 4, TILES * E:(TILES + 1) * E], 1.0 / ST, (ST - 1) / 2 / ST,
                                        ALU.mult, ALU.add))
            link(dve, dve.tensor_scalar(s(0, 0), s(0, 0), MAGIC, MAGIC, ALU.add, ALU.subtract))
            for n in range(3):
                link(dve, dve.tensor_tensor(s(n + 1, 0), s(n, 0), s(n, 1 << n), ALU.add))
            link(dve, dve.tensor_tensor(first[:], s(3, 0), s(0, 0), ALU.subtract))
            link(dve, dve.tensor_scalar(first[:], first[:], float(ST), None, ALU.mult))
            link(dve, dve.tensor_tensor(slotf, ps[:, 4, 0:TILES * E].rearrange("p (j e) -> p j e", e=E),
                                        first[:].rearrange("p (a e) -> p a e", a=1).broadcast_to(wide), ALU.add))
            for k in range(2):
                link(dve, dve.tensor_tensor(t8, chosen[:, k], slotf, ALU.mult))
                link(dve, dve.tensor_reduce(slot[:, k].rearrange("p (j a) -> p j a", a=1), t8, AX.X, ALU.add))
            slots = slot.rearrange("p k j -> p (k j)")
            h32_ = inv3[:, 0, 0:2 * TILES]
            link(dve, dve.tensor_scalar(h32_, slots, 1.0 / P, (P - 1) / 2 / P, ALU.mult, ALU.subtract))
            link(dve, dve.tensor_scalar(hi16[:], h32_, MAGIC, MAGIC, ALU.add, ALU.subtract))
            link(dve, dve.scalar_tensor_tensor(lo16[:], hi16[:], -float(P), slots, ALU.mult, ALU.add))
            quarter = TILES // 2
            for c in range(4):
                r = slice(c * quarter, (c + 1) * quarter)
                wl, wb = [P, quarter, P], [P, quarter, BLOCKS]
                lanes = cst16[:, 0:P].rearrange("p (a n) -> p a n", a=1).broadcast_to(wl)
                blocks = cst16[:, P:P + BLOCKS].rearrange("p (a n) -> p a n", a=1).broadcast_to(wb)
                tiles = cst16[:, P + BLOCKS:].rearrange("p (t a) -> p t a", a=1)[:, r].broadcast_to(wb)
                lo_b = lo16[:].rearrange("p (t a) -> p t a", a=1)[:, r].broadcast_to(wl)
                hi_b = hi16[:].rearrange("p (t a) -> p t a", a=1)[:, r].broadcast_to(wb)
                b0, b1 = block1h[:, r, 0], block1h[:, r, 1]
                link(dve, dve.tensor_tensor(b0, blocks, hi_b, ALU.is_equal))
                link(dve, dve.tensor_scalar(b1, b0, cst[:, C_PART:C_PART + 1], None, ALU.mult))
                link(dve, dve.tensor_tensor(b0, b0, tiles, ALU.mult))
                dve.tensor_tensor(lane1h[:, r], lanes, lo_b, ALU.is_equal).then_inc(onehots, 1)
            ends = sums[:, 3, E:2 * E - 1].rearrange("p (a e) -> p a e", a=1).broadcast_to([P, SLOT_TILES, E - 1])
            at = cst[:, C_SLOT_TILE:C_TRI].rearrange("p (n a) -> p n a", a=1).broadcast_to([P, SLOT_TILES, E - 1])
            link(dve, dve.tensor_tensor(le_n, ends, at, ALU.is_le))
            link(dve, dve.tensor_reduce(eot_f.rearrange("p (n a) -> p n a", a=1), le_n, AX.X, ALU.add))
            link(dve, dve.tensor_copy(expert_of[:], eot_f))
            dve.wait_ge(slots_ready, 1)
            a, b = ps[:, 7, 0:BLOCKS], ps[:, 7, BLOCKS:2 * BLOCKS]
            r, s1, s2 = (inv3[:, k] for k in range(3))
            link(dve, dve.tensor_copy(s1, b))
            link(dve, dve.scalar_tensor_tensor(r, a, float(P), s1, ALU.mult, ALU.add))
            link(dve, dve.tensor_scalar(s1, a, TILES + 0.5, -float(N), ALU.is_gt, ALU.mult))
            link(dve, dve.tensor_tensor(row_of[:], r, s1, ALU.add))
            link(dve, dve.tensor_scalar(s2, a, 0.5, None, ALU.is_lt))
            link(dve, dve.tensor_tensor(s2, s2, cst[:, C_PAD:C_PAD + BLOCKS], ALU.mult))
            dve.scalar_tensor_tensor(pair_of[:], r, -float(P), s2, ALU.add, ALU.add).then_inc(route_done, 1)

        def is_tile(n, k):
            return isinstance(n, int) and n == k

        def psh(b):
            return ps[:, b].bitcast(F16)

        def bank_of(u):
            return u % 8

        def mix_groups(eng, mix):
            mix(0, 0)
            with eng.Fori(0, GROUPS // 2 - 1) as i:
                mix(2 * i + 1, 1)
                mix(2 * i + 2, 0)
            mix(GROUPS - 1, 1)

        def is_last(g):
            return isinstance(g, int) and g == GROUPS - 1

        def acc_index(p, q, j):
            return GT + 2 * GT * p + 4 * (q // 2) + 2 * j + q % 2

        def mixture_pe(pe):
            def split_matmul(dst, lhs, rhs, ks):
                for n, (a, b) in enumerate(((0, 0), (0, 1), (1, 0))):
                    for k in ks:
                        last = pe.matmul(dst, lhs(a, k), rhs(b, k), start=(n == 0 and k == ks[0]),
                                         stop=(n == 2 and k == ks[-1]))
                return last

            def reader_done(g, u):
                if u >= 8:
                    h, v = g, u - 8
                    if is_last(g) and U_NEXT <= v < U_OUT:
                        v -= 8
                elif isinstance(g, int) and g == 0:
                    return
                else:
                    h, v = g - 1, (u + 32 if u + 32 < UNITS else u + 24)
                if v == 0:
                    pe.wait_ge(rt_in, h + 1)
                elif v < U_ROUTED:
                    c = (v - U_SHARED) // 2
                    pe.wait_ge(vs_ready if (v - U_SHARED) % 2 else sa_used, HSC * h + c + 1)
                elif v < U_NEXT:
                    pe.wait_ge(vr_ready, E * h + v - U_ROUTED + 1)
                elif v < U_OUT:
                    pe.wait_ge(xs_T, 2 * h + 2 + v - U_NEXT + 1)
                elif v < U_PAIR:
                    pe.wait_ge(y_acc, YG * h + v - U_OUT + 1)
                else:
                    p, q = (v - U_PAIR) // GT, (v - U_PAIR) % GT
                    pe.wait_ge(y_acc, YG * h + acc_index(p, q, 1) + 1)

            def transposes(g, s):
                pe.wait_ge(xn_lo if s else xn_hi, g + 1)
                for k in range(DC):
                    for q in range(GT):
                        last = pe.transpose(psh(bank_of(U_NEXT + s))[:, k * GN + q * P:k * GN + (q + 1) * P],
                                            xsn[:, s, q * D + k * P:q * D + (k + 1) * P], identh[:])
                last.then_inc(unit, 1)

            pe.wait_ge(out_ready, SLOT_TILES)
            pe.wait_ge(mix_start, 1)
            for k in range(DC):
                last = pe.matmul(ps[:, 0, 0:E], h0rep[:, k], rtw[:, k], start=(k == 0), stop=(k == DC - 1))
            last.then_inc(unit, 1)
            for s in range(2):
                transposes(0, s)

            def mix(g, buf):
                xh = lambda s, k: xs[:, buf, s, k]
                if isinstance(g, int) and g == 0:
                    pe.wait_ge(tb_ready, 1)
                reader_done(g, 0)
                pe.wait_ge(xs_T, 2 * g + 2)
                for q in range(GT):
                    last = split_matmul(ps[:, 0, q * E:(q + 1) * E], lambda s, k: xs[:, buf, s, k, q * P:(q + 1) * P],
                                        lambda s, k: rw_s[:, s, k], range(DC))
                last.then_inc(unit, 1)
                for c in range(HSC):
                    for m, w in enumerate((sw1s, sw3s)):
                        u = U_SHARED + 2 * c + m
                        reader_done(g, u)
                        split_matmul(ps[:, bank_of(u)], lambda s, k: w[:, s, k, c * P:(c + 1) * P], xh,
                                     range(DC)).then_inc(unit, 1)
                for e in range(E):
                    u = U_ROUTED + e
                    reader_done(g, u)
                    split_matmul(ps[:, bank_of(u)], lambda s, k: rw1s[:, s, k, e * P:(e + 1) * P], xh,
                                 range(DC)).then_inc(unit, 1)
                if not is_last(g):
                    for s in range(2):
                        reader_done(g, U_NEXT + s)
                        transposes(g + 1, s)
                for q in range(GT):
                    u = U_OUT + q
                    reader_done(g, u)
                    if q == 0:
                        pe.wait_ge(lo1, HC * g + HSC)
                    split_matmul(ps[:, bank_of(u), 0:D], lambda s, k: hid1[:, s, k, q * P:(q + 1) * P],
                                 lambda s, k: sw2s[:, s, k], range(HSC)).then_inc(unit, 1)
                for p in range(E // 2):
                    for q in range(GT):
                        u = U_PAIR + GT * p + q
                        reader_done(g, u)
                        if q == 0:
                            pe.wait_ge(lo1, HC * g + HSC + 2 * p + 2)
                        for j in range(2):
                            last = split_matmul(ps[:, bank_of(u), j * D:(j + 1) * D],
                                                lambda s, k: hid1[:, s, HSC + 2 * p + j, q * P:(q + 1) * P],
                                                lambda s, k: rw2s[:, s, 2 * p + j], range(1))
                        last.then_inc(unit, 1)

            mix_groups(pe, mix)

        def mixture_act(act):
            def input_hi(g):
                act.wait_ge(x1_ready, g + 1)
                act.activation(xsn[:, 0], x1[:, bass.ds(GT * g, GT)].rearrange("p q d -> p (q d)"), ACT.Copy,
                               scale=A_SCALE).then_inc(xn_hi, 1)

            def input_T(buf, s):
                act.activation(xs[:, buf, s].rearrange("p k n -> p (k n)"), psh(bank_of(U_NEXT + s)), ACT.Copy)\
                   .then_inc(xs_T, 1)

            input_hi(0)
            for s in range(2):
                act.wait_ge(unit, 2 + s)
                input_T(0, s)

            def mix(g, buf):
                base = PRE_UNITS + UNITS * g
                act.wait_ge(rt_in, g + 1)
                act.activation(score[:], r_sel[:], ACT.Tanh, scale=0.5).then_inc(rt_sig, 1)
                if not is_last(g):
                    act.wait_ge(xs_T, 2 * g + 2)
                    input_hi(g + 1)

                def hi_part(c):
                    if c < HSC:
                        act.wait_ge(vs_ready, HSC * g + c + 1)
                    else:
                        act.wait_ge(vr_ready, E * g + c - HSC + 1)
                    act.activation(hid1[:, 0, c], vs[:, c % 3], ACT.Copy,
                                   scale=V_SCALE / (2 * MIX_SCALE) if c < HSC else V_SCALE).then_inc(hi1, 1)

                for c in range(HC):
                    u = U_SHARED + 2 * c if c < HSC else U_ROUTED + c - HSC
                    act.wait_ge(unit, base + u + 1)
                    if c < HSC:
                        act.wait_ge(sa_used, HSC * g + max(c - 1, 0))
                        act.activation(v32[:, c % 2], ps[:, bank_of(u)], ACT.Tanh, scale=0.5 / MIX_SCALE)\
                           .then_inc(th_ready, 1)
                    else:
                        act.wait_ge(lo1, HC * g + c - 2)
                        act.activation(vs[:, c % 3], ps[:, bank_of(u)], ACT.Gelu, scale=1.0 / MIX_SCALE)\
                           .then_inc(vr_ready, 1)
                    if c >= 1:
                        hi_part(c - 1)
                hi_part(HC - 1)
                if not is_last(g):
                    for s in range(2):
                        act.wait_ge(unit, base + U_NEXT + s + 1)
                        input_T(1 - buf, s)

            mix_groups(act, mix)

        def mixture_dve(dve):
            dve.wait_ge(l2_psum, SLOT_TILES)
            rep_b = [P, P // BATCH, BATCH]
            link(dve, dve.tensor_copy(h0rep[:, 0].rearrange("p (r b) -> p r b", b=BATCH), h0[:, 0:1].broadcast_to(rep_b)))
            dve.tensor_copy(h0rep[:, 1].rearrange("p (r b) -> p r b", b=BATCH), h0[:, 1:2].broadcast_to(rep_b))\
               .then_inc(mix_start, 1)
            dve.wait_ge(unit, 1)
            dve.tensor_copy(t_bias[:], ps[:, 0, 0:E]).then_inc(tb_ready, 1)

            def input_lo(g):
                dve.wait_ge(xn_hi, g + 1)
                dve.scalar_tensor_tensor(xsn[:, 1], x1[:, bass.ds(GT * g, GT)].rearrange("p q d -> p (q d)"), A_SCALE,
                                         xsn[:, 0], ALU.mult, ALU.subtract).then_inc(xn_lo, 1)

            input_lo(0)
            wide = [P, GT, E]
            rb = rb_row[:].rearrange("p (a e) -> p a e", a=1).broadcast_to(wide)
            tb = t_bias[:].rearrange("p (a e) -> p a e", a=1).broadcast_to(wide)
            pr = prio[:].rearrange("p (a e) -> p a e", a=1).broadcast_to(wide)
            s, t, o, mk, a, b = r_sel[:], r_t8[:], r_one[:], r_mask[:], r_m1[:], r_k1[:]

            def mix(g, buf):
                base = PRE_UNITS + UNITS * g
                made = [0]

                def then(ins):
                    made[0] += 1
                    ins.then_inc(router_step, 1)
                    dve.wait_ge(router_step, LINKS * g + made[0])

                dve.wait_ge(unit, base + 1)
                if isinstance(g, int) and g == 0:
                    dve.wait_ge(tb_ready, 1)
                dve.scalar_tensor_tensor(s, ps[:, 0, 0:GT * E].rearrange("p (q e) -> p q e", e=E),
                                         1.0 / MIX_SCALE, tb, ALU.mult, ALU.add).then_inc(rt_in, 1)
                dve.wait_ge(rt_sig, g + 1)
                then(dve.tensor_scalar(score[:], score[:], 0.5, 0.5, ALU.mult, ALU.add))
                then(dve.tensor_tensor(s, score[:], rb, ALU.add))
                for k in range(2):
                    dst = mk if k else o
                    then(dve.tensor_reduce(a, s, AX.X, ALU.max))
                    then(dve.tensor_tensor(t, s, a.broadcast_to(wide), ALU.is_equal))
                    then(dve.tensor_tensor(t, t, pr, ALU.mult))
                    then(dve.tensor_reduce(b, t, AX.X, ALU.max))
                    then(dve.tensor_tensor(dst, t, b.broadcast_to(wide), ALU.is_equal))
                    if k == 0:
                        then(dve.scalar_tensor_tensor(s, dst, -FAR, s, ALU.mult, ALU.add))
                then(dve.tensor_tensor(mk, mk, o, ALU.add))
                then(dve.tensor_tensor(t, score[:], mk, ALU.mult))
                then(dve.tensor_reduce(a, t, AX.X, ALU.add))
                then(dve.tensor_scalar(b, a, EPS_GATE, 1.0 / OUT_SCALE, ALU.is_gt, ALU.mult))
                then(dve.tensor_scalar(a, a, EPS_GATE, None, ALU.add))
                then(dve.reciprocal(a, a))
                then(dve.tensor_tensor(t, t, a.broadcast_to(wide), ALU.mult))
                then(dve.tensor_tensor(t, t, b.broadcast_to(wide), ALU.mult))
                then(dve.tensor_scalar(b, b, -0.5, 0.5 / OUT_SCALE, ALU.mult, ALU.add))
                then(dve.tensor_tensor(mk, mk, b.broadcast_to(wide), ALU.mult))
                then(dve.tensor_tensor(comb[:], t, mk, ALU.add))
                assert made[0] == LINKS
                if not is_last(g):
                    input_lo(g + 1)

                def lo_part(c):
                    dve.wait_ge(hi1, HC * g + c + 1)
                    dve.scalar_tensor_tensor(hid1[:, 1, c], vs[:, c % 3],
                                             V_SCALE / (2 * MIX_SCALE) if c < HSC else V_SCALE, hid1[:, 0, c],
                                             ALU.mult, ALU.subtract).then_inc(lo1, 1)

                for c in range(HSC):
                    dve.wait_ge(th_ready, HSC * g + c + 1)
                    dve.scalar_tensor_tensor(vs[:, c % 3], v32[:, c % 2], 1.0, ps[:, bank_of(U_SHARED + 2 * c)],
                                             ALU.add, ALU.mult).then_inc(sa_used, 1)
                    dve.wait_ge(sa_used, HSC * g + c + 1)
                    dve.wait_ge(unit, base + U_SHARED + 2 * c + 2)
                    dve.scalar_tensor_tensor(vs[:, c % 3], ps[:, bank_of(U_SHARED + 2 * c + 1)], 1.0 / MIX_SCALE,
                                             vs[:, c % 3], ALU.mult, ALU.mult).then_inc(vs_ready, 1)
                    if c >= 1:
                        lo_part(c - 1)
                for c in range(HSC, HC):
                    lo_part(c - 1)
                lo_part(HC - 1)
                if is_last(g):
                    base -= 2
                for q in range(GT):
                    dve.wait_ge(unit, base + U_OUT + q + 1)
                    dve.tensor_scalar(y[:, GT * g + q], ps[:, bank_of(U_OUT + q), 0:D], 1.0 / OUT_SCALE, None,
                                      ALU.mult).then_inc(y_acc, 1)
                for p in range(E // 2):
                    for q2 in range(0, GT, 2):
                        for j in range(2):
                            for q in (q2, q2 + 1):
                                if j == 0:
                                    dve.wait_ge(unit, base + U_PAIR + GT * p + q + 1)
                                before = acc_index(p, q, 0) if j else (acc_index(p - 1, q, 1) if p else q)
                                dve.wait_ge(y_acc, YG * g + before + 1)
                                dve.scalar_tensor_tensor(
                                    y[:, GT * g + q], ps[:, bank_of(U_PAIR + GT * p + q), j * D:(j + 1) * D],
                                    comb[:, q, 2 * p + j:2 * p + j + 1], y[:, GT * g + q], ALU.mult, ALU.add)\
                                   .then_inc(y_acc, 1)
                dve.wait_ge(y_acc, YG * g + YG)
                dve.tensor_reduce(ymax[:, bass.ds(g, 1)], y[:, bass.ds(GT * g, GT)].rearrange("p q d -> p (q d)"),
                                  AX.X, ALU.max).then_inc(ymax_in, 1)

            mix_groups(dve, mix)

        def psb(b, n=1):
            return ps[:, b:b + n].rearrange("p b n -> p (b n)").bitcast(BF16)

        def ffn_pe(pe):
            pe.wait_ge(y_acc, YG * GROUPS)
            pe.wait_ge(mw_used, 11)
            for k in range(DC):
                for c in range(FC):
                    last = pe.transpose(psb(k)[:, c * P:(c + 1) * P],
                                        wq_n[:, 0, c * D + k * P:c * D + (k + 1) * P], identb[:])
                last.then_inc(wt_ps, 1)
            for h in range(2):
                for c in range(FC // 2):
                    for k in range(DC):
                        f = FC // 2 * h + c
                        last = pe.transpose(psb(2 + h)[:, c * D + k * P:c * D + (k + 1) * P],
                                            wq_n[:, 1, k * F + f * P:k * F + (f + 1) * P], identb[:])
                last.then_inc(wt_ps, 1)
            pe.wait_ge(diag_ready, DC)
            for k in range(DC):
                last = pe.matmul(ps[:, 4, k * P:(k + 1) * P], ones[:], diag[:, k], start=True, stop=True)
            last.then_inc(wt_ps, 1)
            for g in range(GROUPS):
                pe.wait_ge(yq_n, g + 1)
                if g >= 2:
                    pe.wait_ge(yq_T, g - 1)
                for k in range(DC):
                    for q in range(GT):
                        last = pe.transpose(psb(5 + g % 2)[:, k * GN + q * P:k * GN + (q + 1) * P],
                                            yqn[:, (g % 2) * GT * D + q * D + k * P:(g % 2) * GT * D + q * D + (k + 1) * P],
                                            identb[:])
                last.then_inc(yq_ps, 1)
            pe.wait_ge(wt_cp, 5)
            pe.wait_ge(yq_T, GROUPS)

            def row_max(f):
                for n in range(4):
                    if not (isinstance(f, int) and f == 0):
                        pe.wait_ge(ia_mx, 4 * (f - 1) + n + 1)
                    for m in range(2):
                        for k in range(DC):
                            last = pe.matmul(ps[:, 2 * n + m], w1qT[:, k, bass.ds(f * P, P)],
                                             yqT[:, k, (2 * n + m) * GN:(2 * n + m + 1) * GN],
                                             start=(k == 0), stop=(k == DC - 1))
                    last.then_inc(ia_ps, 1)

            row_max(0)
            with pe.Fori(1, FC) as f:
                row_max(f)
            pe.wait_ge(ia_mx, 4 * FC)

            def group(g):
                for f in range(FC):
                    if not (is_tile(g, 0) and f < 4):
                        pe.wait_ge(hb_h, FC * g + f - 3)
                    for k in range(DC):
                        last = pe.matmul(ps[:, f % 4], w1qT[:, k, f * P:(f + 1) * P], yqT[:, k, bass.ds(GN * g, GN)],
                                         start=(k == 0), stop=(k == DC - 1))
                    last.then_inc(hb_ps, 1)
                for q in range(GT):
                    if q == 0 and not is_tile(g, 0):
                        pe.wait_ge(ob_s, GT * g)
                    for f in range(FC):
                        if q == 0:
                            pe.wait_ge(hb_q, FC * g + f + 1)
                        last = pe.matmul(ps[:, 4 + q, 0:D], hq[:, f, q * P:(q + 1) * P], w2qT[:, f],
                                         start=(f == 0), stop=(f == FC - 1))
                    last.then_inc(ob_ps, 1)

            group(0)
            with pe.Fori(1, GROUPS) as g:
                group(g)

        def ffn_act(act):
            for n in range(4):
                act.wait_ge(wt_ps, n + 1)
                dst = w1qT[:, n] if n < 2 else w2qT[:, FC // 2 * (n - 2):FC // 2 * (n - 1)].rearrange("p f d -> p (f d)")
                act.activation(dst, psb(n), ACT.Copy).then_inc(wt_cp, 1)
            act.wait_ge(wt_ps, 5)
            act.activation(rs2, ps[:, 4, 0:D], ACT.Copy).then_inc(wt_cp, 1)

            def transposed(g):
                act.wait_ge(yq_ps, g + 1)
                act.activation(yqT[:, :, g * GN:(g + 1) * GN], psb(5 + g % 2).rearrange("p (k n) -> p k n", k=DC),
                               ACT.Copy).then_inc(yq_T, 1)

            for g in range(GROUPS):
                act.wait_ge(yq_m, 2 * g + 2)
                if g >= 2:
                    act.wait_ge(yq_ps, g - 1)
                act.activation(yqn[:, (g % 2) * GT * D:(g % 2 + 1) * GT * D],
                               y[:, GT * g:GT * g + GT].rearrange("p q d -> p (q d)"), ACT.Relu,
                               bias=neg_magic[:]).then_inc(yq_n, 1)
                if g >= 1:
                    transposed(g - 1)
            transposed(GROUPS - 1)
            act.wait_ge(bq_ready, 1)

            def group(g):
                for f in range(FC):
                    act.wait_ge(hb_ps, FC * g + f + 1)
                    if not (is_tile(g, 0) and f < 2):
                        act.wait_ge(hb_q, FC * g + f - 1)
                    act.activation(v32[:, f % 2], ps[:, f % 4], ACT.Relu, scale=sc1[:, f:f + 1],
                                   bias=fb1[:, f:f + 1]).then_inc(hb_h, 1)

            group(0)
            with act.Fori(1, GROUPS) as g:
                group(g)

        pool_steps = [0]

        def then_pool(pool, ins):
            pool_steps[0] += 1
            ins.then_inc(pool_step, 1)
            pool.wait_ge(pool_step, pool_steps[0])

        def round_bias(dve, b, scale, r):
            link(dve, dve.reciprocal(r, scale))
            link(dve, dve.tensor_tensor(b, b, r, ALU.mult))
            link(dve, dve.tensor_scalar(b, b, MAGIC, MAGIC, ALU.add, ALU.subtract))
            return dve.tensor_tensor(b, b, scale, ALU.mult)

        def ffn_dve(dve):
            dve.wait_ge(ymax_in, GROUPS)
            link(dve, dve.memset(neg_magic[:], -MAGIC))
            dve.tensor_reduce(pmax[:, 0:1], ymax[:], AX.X, ALU.max).then_inc(mx_in, 1)
            dve.wait_ge(mx_out, 1)
            link(dve, dve.reciprocal(inv[:, 0:1], gmax[:, 0:1]))
            link(dve, dve.tensor_scalar(inv[:, 0:1], inv[:, 0:1], 1.0 / 3.0, None, ALU.mult))
            for g in range(GROUPS):
                yg = y[:, GT * g:GT * g + GT].rearrange("p q d -> p (q d)")
                dve.tensor_scalar(yg, yg, inv[:, 0:1], 255.0, ALU.mult, ALU.min).then_inc(yq_m, 1)
                dve.wait_ge(yq_m, 2 * g + 1)
                dve.tensor_scalar(yg, yg, MAGIC, None, ALU.add).then_inc(yq_m, 1)
            link(dve, dve.tensor_scalar(sc1[:], sw[:, 0:FC], gmax[:, 0:1], None, ALU.mult))
            round_bias(dve, fb1[:], sc1[:], vs[:, 0, 0:FC]).then_inc(bq_ready, 1)

            def row_max(f):
                for n in range(4):
                    dve.wait_ge(ia_ps, 4 * f + n + 1)
                    dve.tensor_reduce(imax[:, f, n:n + 1], ps[:, 2 * n:2 * n + 2].rearrange("p b n -> p (b n)"),
                                      AX.X, ALU.max).then_inc(ia_mx, 1)

            with dve.Fori(0, FC) as f:
                row_max(f)
            dve.wait_ge(ia_mx, 4 * FC)
            dve.wait_ge(bq_ready, 1)
            link(dve, dve.tensor_reduce(hmax[:], imax[:], AX.X, ALU.max))
            link(dve, dve.tensor_tensor(hmax[:], hmax[:], sc1[:], ALU.mult))
            link(dve, dve.tensor_tensor(hmax[:], hmax[:], fb1[:], ALU.add))
            dve.tensor_reduce(pmax[:, 1:2], hmax[:], AX.X, ALU.max).then_inc(mx_in, 1)
            dve.wait_ge(mx_out, 2)
            link(dve, dve.reciprocal(inv[:, 1:2], gmax[:, 1:2]))
            dve.wait_ge(wt_cp, 5)
            link(dve, dve.tensor_scalar(rs2, rs2, gmax[:, 1:2], None, ALU.mult))
            dve.wait_ge(bq2_in, 16)
            round_bias(dve, bq2, rs2, vs[:, 0, 0:D]).then_inc(bq_ready, 1)

            def group(g):
                for f in range(FC):
                    dve.wait_ge(hb_h, FC * g + f + 1)
                    dve.tensor_scalar(v32[:, f % 2], v32[:, f % 2], inv[:, 1:2], 255.0, ALU.mult, ALU.min)\
                       .then_inc(hb_s, 1)
                    if f == 0 and not is_tile(g, 0):
                        dve.wait_ge(ob_ps, GT * g)
                    dve.wait_ge(hb_s, FC * g + f + 1)
                    dve.tensor_scalar(hq[:, f], v32[:, f % 2], MAGIC, MAGIC, ALU.add, ALU.subtract).then_inc(hb_q, 1)
                for q in range(GT):
                    dve.wait_ge(ob_ps, GT * g + q + 1)
                    dve.tensor_tensor(vs[:, q % 3, 0:D], ps[:, 4 + q, 0:D], rs2, ALU.mult).then_inc(ob_s, 1)
                    if q == 0:
                        dve.wait_ge(xb_ready, g + 1)
                    dve.wait_ge(ob_s, GT * g + q + 1)
                    dve.tensor_tensor(x1[:, GT * g + q], x1[:, GT * g + q], vs[:, q % 3, 0:D], ALU.add).then_inc(ob, 1)

            group(0)
            with dve.Fori(1, GROUPS) as g:
                group(g)

        def ffn_pool(pool):
            def add_results(g, h, p):
                pool.wait_ge(x_in[p], 16 * h + 16)
                pool.wait_ge(o_arrived[p], 32 * h + 32)
                pool.tensor_tensor(o_in[:, p, 0], o_in[:, p, 0], o_in[:, p, 1], ALU.add).then_inc(x1_step, 1)
                pool.wait_ge(x1_step, g + 1)
                xg_ = x1[:, bass.ds(GT * g, GT)]
                pool.tensor_tensor(xg_, xg_, o_in[:, p, 0], ALU.add).then_inc(x1_ready, 1)

            for p in range(2):
                add_results(p, 0, p)
            for c in range(DC):
                pool.tensor_scalar(diag[:, c], ident[:], sw[:, FC + c:FC + c + 1], None, ALU.mult)\
                    .then_inc(diag_ready, 1)
            with pool.Fori(1, GROUPS // 2) as h:
                for p in range(2):
                    add_results(2 * h + p, h, p)

            pool.wait_ge(mx_in, 1)
            then_pool(pool, pool.partition_all_reduce(gmax[:, 0:1], pmax[:, 0:1], P, RMAX))
            then_pool(pool, pool.tensor_scalar(gmax[:, 0:1], gmax[:, 0:1], 1.0 / 3.0, EPS_QUANT, ALU.mult, ALU.max))
            pool.tensor_scalar(gmax[:, 0:1], gmax[:, 0:1], 1.0 / 255.0, None, ALU.mult).then_inc(mx_out, 1)
            pool.wait_ge(mx_in, 2)
            then_pool(pool, pool.partition_all_reduce(gmax[:, 1:2], pmax[:, 1:2], P, RMAX))
            pool.tensor_scalar(gmax[:, 1:2], gmax[:, 1:2], EPS_QUANT, 1.0 / 255.0, ALU.max, ALU.mult).then_inc(mx_out, 1)
            pool.wait_ge(bq_ready, 2)
            wide = bq2.rearrange("p (a d) -> p a d", a=1).broadcast_to([P, GT, D])
            with pool.Fori(0, GROUPS) as g:
                xg = x1[:, bass.ds(GT * g, GT)]
                pool.tensor_tensor(xg, xg, wide, ALU.add).then_inc(xb_ready, 1)

        def slot_tiles(eng, tile):
            for n in range(JOBS):
                tile(n, n // 2, n % 2)
            with eng.Fori(0, (SLOT_TILES - 2 - JOBS) // 2) as i:
                tile(2 * i + JOBS, i + JOBS // 2, 1)
                tile(2 * i + JOBS + 1, i + JOBS // 2 + 1, 0)
            for n in range(SLOT_TILES - 2, SLOT_TILES):
                tile(n, n // 2, n % 2)

        def experts_pe(pe):
            def transposes(n, m, p):
                pe.wait_ge(xg_in[p], 32 * m + 32)
                for s in range(2):
                    for k in range(DC):
                        for q in range(SQ):
                            c = (s * DC + k) * ST + q * P
                            last = pe.transpose(psh(6)[:, c:c + P], xg[:, p, q, (s * DC + k) * P:(s * DC + k + 1) * P],
                                                identh[:])
                last.then_inc(xT_ps, 1)

            pe.wait_ge(w_split, 96)
            pe.wait_ge(route_done, 1)
            transposes(0, 0, 0)

            def tile(n, m, p):
                e = pe.value_load(expert_of[0:1, bass.ds(n, 1)], min_val=0, max_val=E - 1)
                of_e = lambda a: a.rearrange("p a n -> p (a n)")
                pe.wait_ge(xT_ready, n + 1)
                for f in range(FC):
                    if not (is_tile(n, 0) and f < 4):
                        pe.wait_ge(l1_v, FC * n + f - 3)
                    for i, (a, b) in enumerate(((0, 0), (0, 1), (1, 0))):
                        for k in range(DC):
                            last = pe.matmul(ps[:, f % 4, 0:ST],
                                             of_e(W1[:, bass.ds(e, 1), a, k, f * P:(f + 1) * P]), xT[:, p, b, k],
                                             start=(i == 0 and k == 0), stop=(i == 2 and k == DC - 1))
                    last.then_inc(l1_psum, 1)
                if not is_tile(n, SLOT_TILES - 1):
                    transposes(n + 1, m + p, 1 - p)
                if not is_tile(n, 0):
                    pe.wait_ge(out_ready, n)
                for q in range(SQ):
                    pe.matmul(ps[:, 4 + q, 0:D], a_ones[:], of_e(b2s[:, bass.ds(e, 1)]), start=True, stop=False)
                for f in range(FC):
                    pe.wait_ge(l1_hid, FC * n + f + 1)
                    for i, (a, b) in enumerate(((0, 0), (1, 0), (0, 1))):
                        for q in range(SQ):
                            last = pe.matmul(ps[:, 4 + q, 0:D], hid[:, a, f, q * P:(q + 1) * P],
                                             of_e(W2[:, bass.ds(e, 1), b, f]), start=False,
                                             stop=(i == 2 and f == FC - 1))
                last.then_inc(l2_psum, 1)

            slot_tiles(pe, tile)

        def experts_act(act):
            def transposed(n, p):
                act.wait_ge(xT_ps, n + 1)
                act.activation(xT[:, p].rearrange("p s k n -> p (s k n)"), psh(6), ACT.Copy).then_inc(xT_ready, 1)

            def results(n, m, p):
                act.wait_ge(l2_psum, n + 1)
                if not is_tile(m, 0):
                    act.wait_ge(pairs_out[p], 32 * m)
                act.activation(obuf[:, p], ps[:, 4:4 + SQ, 0:D], ACT.Copy, scale=1.0 / (W_SCALE * A_SCALE))\
                   .then_inc(out_ready, 1)

            transposed(0, 0)

            def tile(n, m, p):
                if not is_tile(n, 0):
                    results(n - 1, m - 1 + p, 1 - p)
                for f in range(FC):
                    act.wait_ge(l1_psum, FC * n + f + 1)
                    if f == 0:
                        act.wait_ge(b1_ready, n + 1)
                    if not (is_tile(n, 0) and f < 4):
                        act.wait_ge(l1_hid, FC * n + f - 3)
                    act.activation(v4[:, f % 4], ps[:, f % 4, 0:ST], ACT.Relu, bias=b1_now[:, p, f:f + 1],
                                   scale=A_SCALE / W_SCALE).then_inc(l1_v, 1)
                if not is_tile(n, SLOT_TILES - 1):
                    transposed(n + 1, 1 - p)

            slot_tiles(act, tile)
            results(SLOT_TILES - 1, SLOT_TILES // 2, 0)

        def split_piece(dve, c):
            dve.wait_ge(mw_in[c % 2], 16 * (c // 2) + 16)
            hi, lo = l1w[:, 0, 1024 * c:1024 * (c + 1)], l1w[:, 1, 1024 * c:1024 * (c + 1)]
            link(dve, dve.tensor_scalar(hi, stage[:, c % 2], W_SCALE, None, ALU.mult))
            dve.scalar_tensor_tensor(lo, stage[:, c % 2], W_SCALE, hi, ALU.mult, ALU.subtract).then_inc(mw_used, 1)

        def ffn_rows(c):
            a, n = (4 * c, 4) if c < 2 else (FC + c - 2, 1)
            return slice(a, a + n), stage[:, (7 + c) % 2].rearrange("p (c n) -> p c n", c=n)

        def scale_piece(dve, c):
            dve.wait_ge(mw_in[(7 + c) % 2], 16 * ((7 + c) // 2) + 16)
            r, st = ffn_rows(c)
            link(dve, dve.tensor_reduce(sw[:, r], st, AX.X, ALU.max))
            link(dve, dve.tensor_reduce(swr[:, r], st, AX.X, ALU.min))
            link(dve, dve.scalar_tensor_tensor(sw[:, r], swr[:, r], -1.0, sw[:, r], ALU.mult, ALU.max))
            link(dve, dve.tensor_scalar(sw[:, r], sw[:, r], EPS_QUANT, 1.0 / 127.0, ALU.max, ALU.mult))
            dve.reciprocal(swr[:, r], sw[:, r]).then_inc(wm_ready, 1)

        def quantise_piece(pool, c):
            pool.wait_ge(wm_ready, c + 1)
            r, st = ffn_rows(c)
            for k in range(r.stop - r.start):
                then_pool(pool, pool.tensor_scalar(st[:, k], st[:, k], swr[:, r.start + k:r.start + k + 1], None, ALU.mult))
            st = stage[:, (7 + c) % 2]
            then_pool(pool, pool.tensor_scalar(st, st, -128.0, 127.0, ALU.max, ALU.min))
            then_pool(pool, pool.tensor_scalar(st, st, MAGIC, None, ALU.add))
            pool.tensor_scalar(wq_n[:, c // 2, 1024 * (c % 2):1024 * (c % 2) + 1024], st, MAGIC, None, ALU.subtract)\
                .then_inc(mw_used, 1)
            pool.wait_ge(mw_used, 7 + c + 1)

        def experts_dve(dve):
            def tile(n, m, p):
                for f in range(FC):
                    dve.wait_ge(l1_v, FC * n + f + 1)
                    if f == 0 and not is_tile(n, 0):
                        dve.wait_ge(l2_psum, n)
                    dve.tensor_copy(hid[:, 0, f], v4[:, f % 4]).then_inc(split0, 1)
                    dve.wait_ge(split0, FC * n + f + 1)
                    dve.tensor_tensor(hid[:, 1, f], v4[:, f % 4], hid[:, 0, f], ALU.subtract).then_inc(l1_hid, 1)
                if isinstance(n, int):
                    if n < 4:
                        for c in range(2 * n, min(2 * n + 2, 7)):
                            split_piece(dve, c)
                    elif n < 8:
                        scale_piece(dve, n - 4)
                    if n == 3:
                        link(dve, dve.tensor_scalar(rw_s[:, 0], rw[:], W_SCALE, None, ALU.mult))
                        link(dve, dve.scalar_tensor_tensor(rw_s[:, 1], rw[:], W_SCALE, rw_s[:, 0], ALU.mult,
                                                           ALU.subtract))

            slot_tiles(dve, tile)

        def experts_pool(pool):
            def row_indices(n, m, p):
                if not is_tile(m, 0):
                    pool.wait_ge(xg_in[p], 32 * m)
                    pool.wait_ge(xT_ps, n - 1)
                pool.tensor_copy(row_now[:, p], row_of[:, bass.ds(SQ * n, SQ)]).then_inc(row_idx, 1)
                pool.wait_ge(row_idx, n + 1)

            def gather(p):
                for q in range(SQ):
                    pool.indirect_dma_start(out=xg[:, p, q], out_offset=None, in_=rows_d,
                                            in_offset=bass.IndirectOffsetOnAxis(ap=row_now[:, p, q:q + 1], axis=0))\
                        .then_inc(xg_in[p], 16)

            def pair_indices(n, m, p):
                if not is_tile(m, 0):
                    pool.wait_ge(pairs_out[p], 32 * m)
                pool.tensor_copy(pair_now[:, p], pair_of[:, bass.ds(SQ * n, SQ)]).then_inc(pair_idx, 1)
                pool.wait_ge(pair_idx, n + 1)
                pool.wait_ge(out_ready, n + 1)

            def scatter(p):
                for q in range(SQ):
                    pool.indirect_dma_start(out=pairs_d, in_=obuf[:, p, q], in_offset=None,
                                            out_offset=bass.IndirectOffsetOnAxis(ap=pair_now[:, p, q:q + 1], axis=0))\
                        .then_inc(pairs_out[p], 16)

            def expert(n):
                return pool.value_load(expert_of[0:1, bass.ds(n, 1)], min_val=0, max_val=E - 1)

            def bias(n, p, e):
                if not is_tile(n, 0) and not is_tile(n, 1):
                    pool.wait_ge(l1_v, FC * n - FC)
                pool.tensor_copy(b1_now[:, p], b1s[:, bass.ds(e, 1)].rearrange("p a n -> p (a n)")).then_inc(b1_ready, 1)
                pool.wait_ge(b1_ready, n + 1)

            pool.wait_ge(route_done, 1)
            pool.wait_ge(row_out[0], 16 * (TILES // 2 + 1) + 1)
            pool.wait_ge(row_out[1], 16 * TILES // 2 + 1)
            for n in range(2):
                row_indices(n, 0, n)
                gather(n)
            bias(0, 0, expert(0))

            def tile(n, m, p):
                more = not (isinstance(n, int) and n >= SLOT_TILES - 2)
                if more:
                    row_indices(n + 2, m + 1, p)
                if not is_tile(n, 0):
                    pair_indices(n - 1, m - 1 + p, 1 - p)
                if not is_tile(n, SLOT_TILES - 1):
                    e = expert(n + 1)
                if more:
                    gather(p)
                if not is_tile(n, 0):
                    scatter(1 - p)
                if not is_tile(n, SLOT_TILES - 1):
                    bias(n + 1, 1 - p, e)
                if isinstance(n, int) and 5 <= n < JOBS:
                    quantise_piece(pool, n - 5)

            slot_tiles(pool, tile)
            pair_indices(SLOT_TILES - 1, SLOT_TILES // 2, 0)
            scatter(0)

        block = ctx.enter_context(nc.Block())

        @block.sync
        def _(sp):
            sp.dma_start(wst, WT).then_inc(w_in, 16)
            sp.dma_start(h0[:], h0T).then_inc(w_in, 16)
            sp.dma_start(alpha[:], alphaT).then_inc(w_in, 16)
            sp.wait_ge(const0, 1)
            sp.dma_start(b_mat[0:1, :], b_row).then_inc(w_in, 16)
            for j in range(RING):
                sp.dma_start(z[:, j], zT[:, j]).then_inc(z_in[j], 16)
            sp.dma_start(gw[:], gate_wT).then_inc(gw_in, 16)
            sp.dma_start(b2st[0:1], b2).then_inc(small_in, 16)
            sp.dma_start(b2st[32:33], b2).then_inc(small_in, 16)
            sp.dma_start(gb_row[:], gate_b.broadcast_to([P, E])).then_inc(small_in, 16)
            sp.dma_start(b1s[:], b1T).then_inc(small_in, 16)
            sp.dma_start(rw[:], rwT).then_inc(small_in, 16)
            sp.dma_start(rtw[:], rtwT).then_inc(small_in, 16)
            sp.dma_start(rb_row[:], rbias.broadcast_to([P, E])).then_inc(small_in, 16)
            sp.dma_start(fb1[:], fb1T).then_inc(small_in, 16)
            sp.dma_start(cst, const).then_inc(small_in, 16)

            def keep_rows(i, j):
                sp.wait_ge(row_cp, 2 * RING * i + 2 * j + 2)
                sp.dma_start(rows_d[bass.ds(P * RING * i + P * j, P)], hrow[:, j % 2]).then_inc(row_out[j % 2], 16)

            def next_z(i, j):
                sp.wait_ge(u_ready, 32 * i + 8 * j + 8)
                sp.dma_start(z[:, j], zT[:, RING * i + j + RING]).then_inc(z_in[j], 16)

            with sp.Fori(0, TILES // RING - 1) as i:
                for j in range(RING):
                    keep_rows(i, j)
                    next_z(i, j)
            for j in range(RING):
                keep_rows(TILES // RING - 1, j)
            keep_rows(TILES // RING, 0)

            pieces = [sw1T, sw3T, sw2T, rw1T[:, 0:1], rw1T[:, 1:2], rw2T[:, 0:E // 2], rw2T[:, E // 2:],
                      fw1n[:, 0:FC // 2], fw1n[:, FC // 2:], fw2n[:, 0:1], fw2n[:, 1:2]]
            sp.wait_ge(w_split, 96)
            for c, piece in enumerate(pieces):
                if c >= 2:
                    sp.wait_ge(mw_used, c - 1)
                sp.dma_start(stage[:, c % 2].rearrange("p (c n) -> p c n", c=piece.shape[1]), piece)\
                  .then_inc(mw_in[c % 2], 16)

            pairs_in = pairs_d[0:PAIRS].rearrange("(k j p) d -> p k j d", k=2, p=P)
            sp.wait_ge(l2_psum, SLOT_TILES)
            sp.dma_start(x1[:, 0:GT], xn[:, 0:GT]).then_inc(x_in[0], 16)
            sp.wait_ge(pairs_out[0], 16 * (SLOT_TILES + 1))
            sp.wait_ge(pairs_out[1], 16 * (SLOT_TILES - 1))

            def results(g, p):
                for k in range(2):
                    sp.dma_start(o_in[:, p, k], pairs_in[:, k, bass.ds(GT * g, GT)]).then_inc(o_arrived[p], 16)

            results(0, 0)
            sp.dma_start(x1[:, GT:2 * GT], xn[:, GT:2 * GT]).then_inc(x_in[1], 16)
            results(1, 1)
            sp.dma_start(bq2, fb2.broadcast_to([P, D])).then_inc(bq2_in, 16)
            with sp.Fori(1, GROUPS // 2) as h:
                for p in range(2):
                    sp.wait_ge(x1_ready, 2 * h + p - 1)
                    sp.dma_start(x1[:, bass.ds(2 * GT * h + GT * p, GT)], xn[:, bass.ds(2 * GT * h + GT * p, GT)])\
                      .then_inc(x_in[p], 16)
                    results(2 * h + p, p)

            with sp.Fori(0, GROUPS) as g:
                sp.wait_ge(ob, GT * g + GT)
                sp.dma_start(out[:, bass.ds(GT * g, GT)], x1[:, bass.ds(GT * g, GT)]).then_inc(out_done, 16)
            sp.wait_ge(out_done, 16 * GROUPS)

        @block.gpsimd
        def _(pool):
            pool.memset(b_mat, 0.0).then_inc(const0, 1)
            pool.memset(hring[:, 1], 0.0).then_inc(const0, 1)
            for h in range(2):
                pool.memset(hrow[:, h], 0.0).then_inc(row_out[h], 1)
            pool.memset(b2s[:], 0.0).then_inc(idents, 1)
            pool.memset(a_ones[:], A_SCALE).then_inc(idents, 1)
            for e in range(E):
                pool.memset(prio[:, e:e + 1], float(E - e)).then_inc(idents, 1)
            pool.memset(ident[:], 0.0).then_inc(idents, 1)
            pool.wait_ge(idents, 11)
            pool.affine_select(out=ident[:], in_=ident[:], compare_op=ALU.not_equal, fill=1.0, base=0,
                               pattern=[[-1, P]], channel_multiplier=1).then_inc(idents, 1)
            pool.wait_ge(idents, 12)
            pool.tensor_copy(identh[:], ident[:]).then_inc(idents, 1)
            pool.tensor_copy(identb[:], ident[:]).then_inc(idents, 1)
            pool.memset(sums[:], 0.0).then_inc(idents, 1)
            pool.memset(w_scale[:], W_SCALE).then_inc(idents, 1)
            pool.memset(ones16, 1.0).then_inc(idents, 1)

            def load(e, c):
                src = (w1T, w2T)[c // 2][bass.ds(e, 1)].rearrange("a p n -> p (a n)")
                pool.dma_start(stage[:, c % 2], src[:, 1024 * (c % 2):1024 * (c % 2) + 1024]).then_inc(piece_in[c % 2], 16)

            def split(e, c):
                st, n = stage[:, c % 2], slice(1024 * (c % 2), 1024 * (c % 2) + 1024)
                hi, lo = (W[:, c // 2, bass.ds(e, 1), s, n].rearrange("p a n -> p (a n)") for s in range(2))
                done = 12 * e + 3 * c
                pool.wait_ge(piece_in[c % 2], 32 * e + 16 * (c // 2) + 16)
                pool.tensor_tensor(st, st, w_scale[:].broadcast_to([P, 1024]), ALU.mult).then_inc(w_split, 1)
                pool.wait_ge(w_split, done + 1)
                pool.tensor_copy(hi, st).then_inc(w_split, 1)
                pool.wait_ge(w_split, done + 2)
                pool.tensor_tensor(lo, st, hi, ALU.subtract).then_inc(w_split, 1)
                pool.wait_ge(w_split, done + 3)

            pool.wait_ge(idents, 17)
            load(0, 0)
            load(0, 1)
            with pool.Fori(0, E - 1) as e:
                for c in range(4):
                    split(e, c)
                    load(e + c // 2, (c + 2) % 4)
            for c in range(4):
                split(E - 1, c)
                if c < 2:
                    load(E - 1, c + 2)
            pool.wait_ge(small_in, 144)
            for n, r in enumerate((0, 32)):
                pool.tensor_scalar(b2st[r:r + 1], b2st[r:r + 1], W_SCALE, None, ALU.mult).then_inc(b2_ready, 1)
                pool.wait_ge(b2_ready, 2 * n + 1)
                pool.tensor_copy(b2s[r:r + 1], b2st[r:r + 1]).then_inc(b2_ready, 1)
                pool.wait_ge(b2_ready, 2 * n + 2)
            pool.tensor_tensor(b2s[32:33], b2st[32:33], b2s[32:33], ALU.subtract).then_inc(b2_ready, 1)
            pool.wait_ge(b2_ready, 5)
            pool.tensor_copy(tri, cst[:, C_TRI:CONSTS]).then_inc(b2_ready, 1)
            pool.wait_ge(b2_ready, 6)
            pool.tensor_copy(cst16[:], cst[:, 0:C_PAD]).then_inc(b2_ready, 1)
            pool.wait_ge(b2_ready, 7)
            pool.tensor_scalar(b1s[:], b1s[:], A_SCALE, None, ALU.mult).then_inc(b2_ready, 1)
            pool.wait_ge(b2_ready, 8)
            experts_pool(pool)
            ffn_pool(pool)

        @block.scalar
        def _(act):
            def rows_copy(J2, j, s):
                if s == 0:
                    act.wait_ge(row_out[j % 2], 16 * J2 + 1)
                act.activation(hrow[:, j % 2, s * D:(s + 1) * D], psh(4)[:, s * D:(s + 1) * D], ACT.Copy)\
                   .then_inc(row_cp, 1)

            def step(i, s):
                j, c = s // STEPS_PER_TILE, (s % STEPS_PER_TILE) * BATCH
                act.wait_ge(pre_ready, 32 * i + s + 1)
                act.activation(gate[:], ps[:, 2 * (j % 2):2 * (j % 2) + 2, c:c + BATCH], ACT.Tanh,
                               scale=0.5 / PRE_SCALE).then_inc(gate_ready, 1)
                act.wait_ge(u_ready, 32 * i + s + 1)
                act.activation(hring[:, j % 2, 0, :, c:c + BATCH], u[:], ACT.Tanh, scale=0.5).then_inc(hi_ready, 1)
                act.activation(h32[:], u[:], ACT.Tanh, scale=0.5).then_inc(h32_ready, 1)
                part = s % STEPS_PER_TILE
                if part in (3, 4):
                    if part == 3:
                        act.wait_ge(row_ps, RING * i + j + 1)
                    rows_copy(2 * i + j // 2, j, part - 3)

            with act.Fori(0, TILES // RING) as i:
                for s in range(RING * STEPS_PER_TILE):
                    step(i, s)
            act.wait_ge(row_ps, TILES + 1)
            for s in range(2):
                rows_copy(TILES // 2, 0, s)
            experts_act(act)
            mixture_act(act)
            ffn_act(act)

        @block.vector
        def _(dve):
            dve.memset(ones[:], 1.0).then_inc(prep, 1)
            dve.memset(leak[:], 1.0).then_inc(prep, 1)
            dve.wait_ge(w_in, 64)
            dve.wait_ge(prep, 2)
            dve.tensor_scalar(wh_hi, wst[:, 0:2], W_SCALE, None, ALU.mult).then_inc(prep, 1)
            dve.tensor_scalar(wz, wst[:, 2:4], PRE_SCALE, None, ALU.mult).then_inc(prep, 1)
            dve.tensor_scalar(b_mat, b_mat, PRE_SCALE, None, ALU.mult).then_inc(prep, 1)
            dve.tensor_scalar(alpha[:], alpha[:], -2.0, 2.0, ALU.mult, ALU.add).then_inc(prep, 1)
            dve.wait_ge(prep, 6)
            dve.scalar_tensor_tensor(wh_lo, wst[:, 0:2], W_SCALE, wh_hi, ALU.mult, ALU.subtract).then_inc(prep, 1)
            for c in range(DC):
                dve.tensor_scalar(leak[:, c], leak[:, c], alpha[:, c:c + 1], None, ALU.mult).then_inc(prep, 1)
            dve.wait_ge(gw_in, 16)
            dve.tensor_scalar(gw_s[:, 0], gw[:], W_SCALE, None, ALU.mult).then_inc(prep, 1)
            dve.wait_ge(prep, 10)
            dve.scalar_tensor_tensor(gw_s[:, 1], gw[:], W_SCALE, gw_s[:, 0], ALU.mult, ALU.subtract).then_inc(prep, 1)
            h_hi, h_lo = hring[:, 1, 0, :, P - BATCH:P], hring[:, 1, 1, :, P - BATCH:P]
            dve.wait_ge(const0, 2)
            dve.tensor_copy(h_hi, h0[:]).then_inc(hi_ready, 1)
            dve.tensor_tensor(hleak[:], h0[:], leak[:], ALU.mult).then_inc(hleak_ready, 1)
            dve.wait_ge(hi_ready, 1)
            dve.tensor_tensor(h_lo, h0[:], h_hi, ALU.subtract).then_inc(lo_ready, 1)

            def step(i, s):
                j, c = s // STEPS_PER_TILE, (s % STEPS_PER_TILE) * BATCH
                if s % STEPS_PER_TILE == 0:
                    dve.wait_ge(z_in[j], 16 * i + 16)
                dve.wait_ge(gate_ready, 32 * i + s + 1)
                dve.scalar_tensor_tensor(gz[:], gate[:], 1.0, z[:, j, :, c:c + BATCH], ALU.add, ALU.mult)\
                   .then_inc(gz_ready, 1)
                dve.wait_ge(gz_ready, 32 * i + s + 1)
                dve.wait_ge(hleak_ready, 32 * i + s + 1)
                dve.tensor_tensor(u[:], gz[:], hleak[:], ALU.add).then_inc(u_ready, 1)
                dve.wait_ge(h32_ready, 32 * i + s + 1)
                dve.tensor_tensor(hring[:, j % 2, 1, :, c:c + BATCH], h32[:], hring[:, j % 2, 0, :, c:c + BATCH],
                                  ALU.subtract).then_inc(lo_ready, 1)
                dve.tensor_tensor(hleak[:], h32[:], leak[:], ALU.mult).then_inc(hleak_ready, 1)

            with dve.Fori(0, TILES // RING) as i:
                for s in range(RING * STEPS_PER_TILE):
                    step(i, s)
            dve.wait_ge(b2_ready, 8)
            route(dve)
            experts_dve(dve)
            mixture_dve(dve)
            ffn_dve(dve)

        @block.tensor
        def _(pe):
            def z_part(slot, part):
                m, k = part // 3, part % 3
                dst = ps[:, 2 * (slot % 2) + m, 0:P]
                cols = slice(m * P, (m + 1) * P)
                if k < 2:
                    pe.matmul(dst, wz[:, k, cols], z[:, slot, k, :], start=(k == 0), stop=False, skip_group_check=True)
                else:
                    pe.matmul(dst, b_mat[:, cols], ones[:], start=False, stop=False, skip_group_check=True)

            def rows(half):
                for s in range(2):
                    for k in range(DC):
                        last = pe.transpose(psh(4)[:, (s * DC + k) * P:(s * DC + k + 1) * P], hring[:, half, s, k],
                                            identh[:])
                last.then_inc(row_ps, 1)

            def logits(half, col):
                for n, (a, b) in enumerate(((0, 0), (0, 1), (1, 0))):
                    for k in range(DC):
                        last = pe.matmul(ps[:, 5, bass.ds(col, E)], hring[:, half, a, k], gw_s[:, b, k],
                                         start=(n == 0 and k == 0), stop=(n == 2 and k == DC - 1))
                return last

            def step(i, s, last_tile=False):
                j, c = s // STEPS_PER_TILE, (s % STEPS_PER_TILE) * BATCH
                half, b = j % 2, 2 * (j % 2)
                part = s % STEPS_PER_TILE
                prev, pc = (half, c - BATCH) if part else (1 - half, P - BATCH)
                pe.wait_ge(hi_ready, 32 * i + s + 1)
                for w in (wh_hi, wh_lo):
                    for m in range(DC):
                        for k in range(DC):
                            pe.matmul(ps[:, b + m, c:c + BATCH], w[:, k, m * P:(m + 1) * P],
                                      hring[:, prev, 0, k, pc:pc + BATCH], start=False, stop=False, skip_group_check=True)
                pe.wait_ge(lo_ready, 32 * i + s + 1)
                for m in range(DC):
                    for k in range(DC):
                        last = pe.matmul(ps[:, b + m, c:c + BATCH], wh_hi[:, k, m * P:(m + 1) * P],
                                         hring[:, prev, 1, k, pc:pc + BATCH], start=False, stop=(k == DC - 1),
                                         skip_group_check=True)
                last.then_inc(pre_ready, 1)
                if part < 3 * DC and not last_tile:
                    if part == 0:
                        pe.wait_ge(z_in[(j + 1) % RING], 16 * i + (32 if j == RING - 1 else 16))
                    z_part((j + 1) % RING, part)
                if part == 1:
                    rows(1 - half)
                if part == 6:
                    logits(1 - half, E * RING * i + E * j)

            pe.wait_ge(prep, 11)
            pe.wait_ge(z_in[0], 16)
            pe.wait_ge(idents, 13)
            for part in range(3 * DC):
                z_part(0, part)
            steps = RING * STEPS_PER_TILE
            with pe.Fori(0, TILES // RING - 1) as i:
                for s in range(steps):
                    step(i, s)
            for s in range(steps):
                step(TILES // RING - 1, s, last_tile=s >= steps - STEPS_PER_TILE)
            pe.wait_ge(lo_ready, STEPS + 1)
            logits(1, E * TILES).then_inc(logits_ready, 1)
            rows(1)

            pe.wait_ge(chosen_ready, 1)
            pe.wait_ge(b2_ready, 8)
            pe.wait_ge(row_cp, 2 * TILES + 2)
            flat = m16.rearrange("p j e -> p (j e)")
            pe.matmul(ps[:, 4, 0:(TILES + 1) * E], tri, flat, start=True, stop=False, skip_group_check=True)
            for j in range(TILES):
                last = pe.matmul(ps[:, 4, (j + 1) * E:(TILES + 1) * E], ones16,
                                 m16[:, j:j + 1].broadcast_to([P, TILES - j, E]), start=False, stop=(j == TILES - 1),
                                 skip_group_check=True)
            last.then_inc(pos_ready, 1)
            for t in range(2 * TILES):
                if t % (TILES // 2) == 0:
                    pe.wait_ge(onehots, t // (TILES // 2) + 1)
                last = pe.matmul(ps[:, 7, 0:2 * BLOCKS], lane1h[:, t], block1h[:, t].rearrange("p v n -> p (v n)"),
                                 start=(t == 0), stop=(t == 2 * TILES - 1))
            last.then_inc(slots_ready, 1)
            experts_pe(pe)
            mixture_pe(pe)
            ffn_pe(pe)


_INS = ['zT', 'xn', 'h0T', 'WT', 'b_row', 'alphaT', 'gate_wT', 'gate_b', 'w1T', 'b1T', 'w2T', 'b2', 'rwT', 'rtwT', 'rbias',
        'sw1T', 'sw3T', 'sw2T', 'rw1T', 'rw2T', 'fw1n', 'fb1T', 'fw2n', 'fb2', 'const']


def kernel(x, cond_1024, L0_cond_W, L0_cond_b, L0_cond_alpha, L0_ffn_gate_w, L0_ffn_gate_b, L0_ffn_w1, L0_ffn_b1,
           L0_ffn_w2, L0_ffn_b2, L1_cond_router_w, L1_cond_router_t_w, L1_cond_router_bias, L1_cond_sw1, L1_cond_sw3,
           L1_cond_sw2, L1_cond_rw1, L1_cond_rw2, L1_ffn_w1, L1_ffn_b1, L1_ffn_w2, L1_ffn_b2):
    import numpy as np
    import concourse.bacc as bacc
    from concourse.bass_utils import run_bass_kernel_spmd as run

    def rows(a):
        return np.asarray(a).reshape(-1, P, a.shape[-1]).transpose(1, 0, 2)

    x = np.asarray(x)
    arrays = {
        "zT": x.transpose(2, 1, 0).reshape(DC, P, TILES, P).transpose(1, 2, 0, 3),
        "xn": x.transpose(1, 0, 2).reshape(TILES, P, D).transpose(1, 0, 2),
        "h0T": rows(np.asarray(cond_1024).T),
        "WT": rows(np.asarray(L0_cond_W).T),
        "b_row": np.asarray(L0_cond_b)[None],
        "alphaT": np.asarray(L0_cond_alpha).reshape(DC, P).T,
        "gate_wT": rows(L0_ffn_gate_w),
        "gate_b": np.asarray(L0_ffn_gate_b)[None],
        "w1T": np.asarray(L0_ffn_w1).reshape(E, DC, P, F).transpose(0, 2, 1, 3).reshape(E, P, DC * F),
        "b1T": np.asarray(L0_ffn_b1).reshape(E, FC, P).transpose(2, 0, 1),
        "w2T": np.asarray(L0_ffn_w2).reshape(E, FC, P, D).transpose(0, 2, 1, 3).reshape(E, P, FC * D),
        "b2": np.asarray(L0_ffn_b2)[None],
        "rwT": rows(np.asarray(L1_cond_router_w).T),
        "rtwT": rows(np.asarray(L1_cond_router_t_w).T),
        "rbias": np.asarray(L1_cond_router_bias)[None],
        "sw1T": rows(np.asarray(L1_cond_sw1).T),
        "sw3T": rows(np.asarray(L1_cond_sw3).T),
        "sw2T": rows(np.asarray(L1_cond_sw2).T),
        "rw1T": rows(np.asarray(L1_cond_rw1).transpose(2, 0, 1).reshape(D, E * P)),
        "rw2T": np.asarray(L1_cond_rw2).transpose(2, 0, 1),
        "fw1n": rows(L1_ffn_w1),
        "fb1T": np.asarray(L1_ffn_b1).reshape(FC, P).T,
        "fw2n": rows(L1_ffn_w2),
        "fb2": np.asarray(L1_ffn_b2)[None],
    }
    p, b = np.arange(P), np.arange(BLOCKS)
    const = np.zeros((P, CONSTS), np.float32)
    const[:, C_LANE:C_LANE + P] = p
    const[:, C_BLOCK:C_BLOCK + BLOCKS] = b
    const[:, C_TILE:C_TILE + 2 * TILES] = np.arange(2 * TILES) + 1
    const[:, C_PAD:C_PAD + BLOCKS] = P + PAIRS + P * b[None] + p[:, None]
    const[:, C_PART] = p
    const[:, C_SLOT_TILE:C_SLOT_TILE + SLOT_TILES] = np.arange(SLOT_TILES)
    const[:, C_TRI:C_TRI + P] = p[:, None] < p[None]
    arrays["const"] = const
    arrays = {k: np.ascontiguousarray(v) for k, v in arrays.items()}
    nc = bacc.Bacc("TRN2", target_bir_lowering=False, num_devices=1)
    args = [nc.dram_tensor(f"in_{n}", arrays[n].shape, F32, kind="ExternalInput").ap() for n in _INS]
    args.append(nc.dram_tensor("rows", (N + P, 2 * D), F16).ap())
    args.append(nc.dram_tensor("pairs", (PAIRS + SLOT_TILES * ST, D), F32).ap())
    args.append(nc.dram_tensor("out", (P, TILES, D), F32, kind="ExternalOutput").ap())
    build_program(nc, *args)
    r = run(nc, [{f"in_{n}": arrays[n] for n in _INS}], core_ids=[0])
    got = r.results[0]["out"]
    return np.ascontiguousarray(got.transpose(1, 0, 2).reshape(STEPS, BATCH, D).transpose(1, 0, 2))
```

```python
from contextlib import ExitStack

import concourse.bass as bass
from concourse import mybir

P = 128
BATCH, STEPS, D = 16, 256, 256
N = BATCH * STEPS
TILES = N // P
STEPS_PER_TILE = P // BATCH
DC = D // P
E = 8
F = 1024
FC = F // P
HS = 512
HSC = HS // P
GT = 4
GROUPS = TILES // GT
GN = GT * P
RING = 4

W_SCALE = 256.0
A_SCALE = 16.0
PRE_SCALE = W_SCALE
MAGIC = 12582912.0
ST = 256
SQ = ST // P
PAIRS = 2 * N
SLOT_TILES = (PAIRS + E * (ST - 1)) // ST
BLOCKS = SLOT_TILES * SQ
JOBS = 9
EPS_GATE = 1e-9
EPS_QUANT = 1e-8
FAR = 1e30

ALU = mybir.AluOpType
ACT = mybir.ActivationFunctionType
AX = mybir.AxisListType
F32 = mybir.dt.float32
F16 = mybir.dt.float16
BF16 = mybir.dt.bfloat16
I32 = mybir.dt.int32
U32 = mybir.dt.uint32
RMAX = bass.bass_isa.ReduceOp.max

HC = HSC + E
U_SHARED, U_ROUTED = 1, 1 + 2 * HSC
U_NEXT = U_ROUTED + E
U_OUT = U_NEXT + DC
U_PAIR = U_OUT + GT
UNITS = U_PAIR + GT * E // 2
PRE_UNITS = 1 + DC
YG = GT * (1 + E)
MIX_SCALE = W_SCALE * A_SCALE
LINKS = 24
V_SCALE = 4.0
OUT_SCALE = W_SCALE * V_SCALE

C_LANE, C_BLOCK = 0, P
C_TILE = C_BLOCK + BLOCKS
C_PAD = C_TILE + TILES // 2
C_SLOT_TILE = C_PAD + BLOCKS
C_TRI = C_SLOT_TILE + SLOT_TILES
CONSTS = C_TRI + P


def build_program(nc, zT, xn, h0T, WT, b_row, alphaT, gate_wT, gate_b, w1T, b1T, w2T, b2, rwT, rtwT, rbias,
                  sw1T, sw3T, sw2T, rw1T, rw2T, fw1n, fb1T, fw2n, fb2, const, rows_d, pairs_d, out):
    ctx = ExitStack()
    with ctx:
        def sb(name, shape, dt):
            return ctx.enter_context(nc.sbuf_tensor(name, shape, dt))

        def sem(name):
            return ctx.enter_context(nc.semaphore(name))

        ps = ctx.enter_context(nc.psum_tensor("ps", [P, 8, 512], F32))
        W = sb("W", [P, 2, E, 2, 2048], F16)
        W1 = W[:, 0].rearrange("p e s (k f) -> p e s k f", k=DC)
        W2 = W[:, 1].rearrange("p e s (f d) -> p e s f d", f=FC)
        area = W[:].rearrange("p m e s n -> p (m e s n)").bitcast(F32)

        def carve(a):
            at = [0]

            def part(n, dt=F32):
                size = n if dt == F32 else n // 2
                piece = a[:, at[0]:at[0] + size]
                at[0] += size
                assert at[0] <= a.shape[-1], at
                return piece if dt == F32 else piece.bitcast(dt)
            return part

        part = carve(area)
        x1 = part(TILES * D).rearrange("p (j d) -> p j d", d=D)
        y = part(TILES * D).rearrange("p (j d) -> p j d", d=D)
        hid1_flat = part(2 * HC * GN, F16)
        hid1 = hid1_flat.rearrange("p (s c n) -> p s c n", s=2, c=HC)
        yqT = hid1_flat[:, 0:DC * N].bitcast(BF16).rearrange("p (k n) -> p k n", k=DC)
        vq = hid1_flat[:, DC * N:].bitcast(F32).rearrange("p (b n) -> p b n", b=4)
        xs_flat = part(2 * 2 * DC * GN, F16)
        xs = xs_flat.rearrange("p (b s k n) -> p b s k n", b=2, s=2, k=DC)
        xsn_flat = part(2 * GT * D, F16)
        xsn = xsn_flat.rearrange("p (s n) -> p s n", s=2)
        yqn = xsn_flat.bitcast(BF16)
        vs_flat = part(3 * GN)
        vs = vs_flat.rearrange("p (b n) -> p b n", b=3)
        ov = vs_flat[:, 0:GT * D].rearrange("p (b q d) -> p b q d", b=2, q=2)
        o_in = part(2 * 2 * GT * D).rearrange("p (b k q d) -> p b k q d", b=2, k=2, d=D)
        diag = part(DC * P).rearrange("p (c n) -> p c n", c=DC)
        h0rep = part(DC * P).rearrange("p (c n) -> p c n", c=DC)
        rs2 = part(D)
        bq2 = part(D)

        work = sb("work", [P, 9216], F32)
        part = carve(work[:])
        l1w = part(2 * 7168, F16).rearrange("p (s n) -> p s n", s=2)
        sw1s = l1w[:, :, 0:1024].rearrange("p s (k h) -> p s k h", k=DC)
        sw3s = l1w[:, :, 1024:2048].rearrange("p s (k h) -> p s k h", k=DC)
        sw2s = l1w[:, :, 2048:3072].rearrange("p s (k d) -> p s k d", k=HSC)
        rw1s = l1w[:, :, 3072:5120].rearrange("p s (k h) -> p s k h", k=DC)
        rw2s = l1w[:, :, 5120:7168].rearrange("p s (e d) -> p s e d", e=E)
        wq_n = part(2 * 2048, BF16).rearrange("p (m n) -> p m n", m=2)
        w1qT = l1w[:, 0, 0:DC * F].bitcast(BF16).rearrange("p (k f) -> p k f", k=DC)
        w2qT = l1w[:, 1, 0:FC * D].bitcast(BF16).rearrange("p (f d) -> p f d", f=FC)
        part = carve(work[:])
        lane1h = part(2 * TILES * P, F16).rearrange("p (t n) -> p t n", n=P)
        block1h = part(2 * TILES * BLOCKS, F16).rearrange("p (t n) -> p t n", n=BLOCKS)
        part = carve(work[:])
        wst = part(4 * D).rearrange("p (c n) -> p c n", c=4)
        zs = part(2 * STEPS_PER_TILE * DC * BATCH * 2).rearrange("p (h s c b v) -> p h s c b v", h=2, s=STEPS_PER_TILE,
                                                                 c=DC, v=2)
        stage = sb("stage", [P, 2, 1024], F32)

        lane = sb("lane", [P, 6144], F32)
        part = carve(lane[:])
        z = part(RING * DC * P).rearrange("p (r c n) -> p r c n", r=RING, c=DC)
        hring = part(2 * 2 * DC * P, F16).rearrange("p (h s c n) -> p h s c n", h=2, s=2, c=DC)
        wh_hi = part(DC * D, F16).rearrange("p (c n) -> p c n", c=DC)
        wh_lo = part(DC * D, F16).rearrange("p (c n) -> p c n", c=DC)
        wz = part(DC * D).rearrange("p (c n) -> p c n", c=DC)
        b_mat = part(D)
        hrow = part(2 * 2 * D, F16).rearrange("p (h n) -> p h n", h=2)
        sel = part(TILES * E).rearrange("p (j e) -> p j e", e=E)
        t8 = part(TILES * E).rearrange("p (j e) -> p j e", e=E)
        chosen = part(2 * TILES * E).rearrange("p (k j e) -> p k j e", k=2, e=E)
        slotf = part(TILES * E).rearrange("p (j e) -> p j e", e=E)
        m16 = part((TILES + 1) * E, BF16).rearrange("p (j e) -> p j e", e=E)
        m1 = part(TILES).rearrange("p (j a) -> p j a", a=1)
        k1 = part(TILES).rearrange("p (j a) -> p j a", a=1)
        slot = part(2 * TILES).rearrange("p (k j) -> p k j", k=2)
        le_n = part(SLOT_TILES * (E - 1)).rearrange("p (n e) -> p n e", e=E - 1)
        eot_f = part(SLOT_TILES)
        cst = part(CONSTS)
        tri = part(P, BF16)
        ones16 = part(P, BF16)
        by_slot = part(2 * BLOCKS).rearrange("p (k n) -> p k n", k=2)
        part = carve(lane[:])
        xg = part(2 * SQ * 2 * D, F16).rearrange("p (b q n) -> p b q n", b=2, q=SQ)
        xT = part(2 * 2 * DC * ST, F16).rearrange("p (b s k n) -> p b s k n", b=2, s=2, k=DC)
        hid = part(2 * FC * ST, F16).rearrange("p (s f n) -> p s f n", s=2, f=FC)
        hq = [a.bitcast(BF16).rearrange("p (f n) -> p f n", f=FC)
              for a in (hid.rearrange("p s f n -> p (s f n)"), xs_flat)]
        v_flat = part(4 * ST)
        v4 = v_flat.rearrange("p (b n) -> p b n", b=4)
        v32 = v_flat.rearrange("p (b n) -> p b n", b=2)
        obuf = part(2 * SQ * D).rearrange("p (b q d) -> p b q d", b=2, q=SQ)

        ones = sb("ones", [P, P], F32)
        h0 = sb("h0", [P, DC, BATCH], F32)
        alpha = sb("alpha", [P, DC], F32)
        gate_rest = sb("gate_rest", [P, DC, BATCH, 2], F32)
        u = sb("u", [P, DC, BATCH, 2], F32)
        h32 = sb("h32", [P, DC, BATCH], F32)
        cst16 = sb("cst16", [P, P + BLOCKS], F16)
        sums = sb("sums", [P, 4, 2 * E], F32)
        first = sb("first", [P, E], F32)
        block_f = sb("block_f", [P, 2 * TILES], F32)
        lane_f = sb("lane_f", [P, 2 * TILES], F32)
        row_of = sb("row_of", [P, BLOCKS], U32)
        pair_of = sb("pair_of", [P, BLOCKS], U32)
        expert_of = sb("expert_of", [P, SLOT_TILES], I32)
        row_now = sb("row_now", [P, 2, SQ], U32)
        pair_now = sb("pair_now", [P, 2, SQ], U32)
        b1_now = sb("b1_now", [P, 2, FC], F32)
        b2_now = sb("b2_now", [P, 2, D], F32)
        w_scale = sb("w_scale", [P, 1], F32)
        inv = sb("inv", [P, 2], F32)
        neg_magic = sb("neg_magic", [P, 1], F32)
        magic = sb("magic", [P, 1], F32)
        sw = sb("sw", [P, FC + DC], F32)
        swr = sb("swr", [P, FC + DC], F32)
        fb1 = sb("fb1", [P, FC], F32)
        sc1 = sb("sc1", [P, FC], F32)
        imax = sb("imax", [P, FC, 4], F32)
        ymax = sb("ymax", [P, GROUPS], F32)
        pmax = sb("pmax", [P, 2], F32)
        gmax = sb("gmax", [P, 2], F32)
        hmax = sb("hmax", [P, FC], F32)
        rtw = sb("rtw", [P, DC, E], F32)
        rw = sb("rw", [P, DC, E], F32)
        rw_s = sb("rw_s", [P, 2, DC, E], F16)
        rb_row = sb("rb_row", [P, E], F32)
        t_bias = sb("t_bias", [P, E], F32)
        score = sb("score", [P, GT, E], F32)
        r_sel = sb("r_sel", [P, GT, E], F32)
        r_t8 = sb("r_t8", [P, GT, E], F32)
        r_one = sb("r_one", [P, GT, E], F32)
        r_mask = sb("r_mask", [P, GT, E], F32)
        r_m1 = sb("r_m1", [P, GT, 1], F32)
        r_k1 = sb("r_k1", [P, GT, 1], F32)
        comb = sb("comb", [P, GT, E], F32)
        gw = sb("gw", [P, DC, E], F32)
        gw_s = sb("gw_s", [P, 2, DC, E], F16)
        gb_row = sb("gb_row", [P, E], F32)
        b1s = sb("b1s", [P, E, FC], F32)
        prio = sb("prio", [P, E], F32)
        ident = sb("ident", [P, P], F32)
        identb = sb("identb", [P, P], BF16)
        identh = sb("identh", [P, P], F16)

        w_in = sem("w_in")
        small_in = sem("small_in")
        const0 = sem("const0")
        idents = sem("idents")
        z_in = [sem(f"z_in{i}") for i in range(RING)]
        prep = sem("prep")
        row_ps = sem("row_ps")
        row_cp = sem("row_cp")
        row_out = [sem(f"row_out{i}") for i in range(2)]
        logits_ready = sem("logits_ready")
        piece_in = [sem(f"piece_in{i}") for i in range(2)]
        w_split = sem("w_split")
        cst_ready = sem("cst_ready")
        b2_in = [sem(f"b2_in{i}") for i in range(2)]
        gw_in = sem("gw_in")
        chosen_ready = sem("chosen_ready")
        pos_ready = sem("pos_ready")
        lanes_ready = sem("lanes_ready")
        onehots = sem("onehots")
        pool_onehots = sem("pool_onehots")
        slots_ready = sem("slots_ready")
        route_done = sem("route_done")
        row_idx = sem("row_idx")
        pair_idx = sem("pair_idx")
        b1_ready = sem("b1_ready")
        xg_in = [sem(f"xg_in{i}") for i in range(2)]
        xT_ps = sem("xT_ps")
        xT_ready = sem("xT_ready")
        out_ready = sem("out_ready")
        pairs_out = [sem(f"pairs_out{i}") for i in range(2)]
        mw_in = [sem(f"mw_in{i}") for i in range(2)]
        mw_used = sem("mw_used")
        x_in = [sem(f"x_in{i}") for i in range(2)]
        o_arrived = [sem(f"o_arrived{i}") for i in range(2)]
        x1_first = sem("x1_first")
        x1_step = sem("x1_step")
        x1_ready = sem("x1_ready")
        mix_start = sem("mix_start")
        diag_ready = sem("diag_ready")
        bq2_in = sem("bq2_in")
        pre_ready = sem("pre_ready")
        gate_ready = sem("gate_ready")
        u_ready = sem("u_ready")
        hi_ready = sem("hi_ready")
        h32_ready = sem("h32_ready")
        lo_ready = sem("lo_ready")
        rest_ready = sem("rest_ready")
        zs_ready = sem("zs_ready")
        vchain = sem("vchain")
        l1_psum = sem("l1_psum")
        l1_v = sem("l1_v")
        split0 = sem("split0")
        l1_hid = sem("l1_hid")
        l2_psum = sem("l2_psum")
        out_done = sem("out_done")
        xn_hi = sem("xn_hi")
        xn_lo = sem("xn_lo")
        xs_T = sem("xs_T")
        unit = sem("unit")
        sa_used = sem("sa_used")
        tb_ready = sem("tb_ready")
        router_step = sem("router_step")
        ymax_in = sem("ymax_in")
        pool_step = sem("pool_step")
        bq_ready = sem("bq_ready")
        xb_ready = sem("xb_ready")
        rt_in = sem("rt_in")
        rt_sig = sem("rt_sig")
        th_ready = sem("th_ready")
        vs_ready = sem("vs_ready")
        vr_ready = sem("vr_ready")
        hi1 = sem("hi1")
        lo1 = sem("lo1")
        y_acc = sem("y_acc")
        mx_in = sem("mx_in")
        mx_out = sem("mx_out")
        wt_ps = sem("wt_ps")
        wt_cp = sem("wt_cp")
        yq_m = sem("yq_m")
        yq_n = sem("yq_n")
        yq_ps = sem("yq_ps")
        yq_T = sem("yq_T")
        ia_ps = sem("ia_ps")
        ia_mx = sem("ia_mx")
        hb_ps = sem("hb_ps")
        hb_h = sem("hb_h")
        hb_qa = sem("hb_qa")
        hb_qp = sem("hb_qp")
        hb_qd = sem("hb_qd")
        hb_s = sem("hb_s")
        ob_ps = sem("ob_ps")
        ob_s = sem("ob_s")
        ob = sem("ob")

        count = {"v": 0}

        def link(dve, ins):
            count["v"] += 1
            ins.then_inc(vchain, 1)
            dve.wait_ge(vchain, count["v"])

        def block_onehot(eng, t):
            number = C_TILE + t % (TILES // 2)
            return eng.tensor_scalar(block1h[:, t], cst16[:, P:P + BLOCKS], block_f[:, t:t + 1], cst[:, number:number + 1],
                                     ALU.is_equal, ALU.mult)

        def lane_onehot(eng, t):
            return eng.tensor_scalar(lane1h[:, t], cst16[:, 0:P], lane_f[:, t:t + 1], None, ALU.is_equal)

        DVE_PAIRS = (0, TILES // 2, TILES, 3 * TILES // 2, 3 * TILES // 2 + 4)
        POOL_PAIRS = range(DVE_PAIRS[-1], 2 * TILES)

        def route(dve):
            wide = [P, TILES, E]
            dve.wait_ge(logits_ready, 1)
            lg = ps[:, 5, E:(TILES + 1) * E].rearrange("p (j e) -> p j e", e=E)
            gb = gb_row[:].rearrange("p (a e) -> p a e", a=1).broadcast_to(wide)
            pr = prio[:].rearrange("p (a e) -> p a e", a=1).broadcast_to(wide)
            link(dve, dve.tensor_scalar(sel, lg, 1.0 / W_SCALE, None, ALU.mult))
            link(dve, dve.tensor_tensor(sel, sel, gb, ALU.add))
            for k in range(2):
                link(dve, dve.tensor_reduce(m1, sel, AX.X, ALU.max))
                link(dve, dve.tensor_tensor(t8, sel, m1.broadcast_to(wide), ALU.is_equal))
                link(dve, dve.tensor_tensor(t8, t8, pr, ALU.mult))
                link(dve, dve.tensor_reduce(k1, t8, AX.X, ALU.max))
                link(dve, dve.tensor_tensor(chosen[:, k], t8, k1.broadcast_to(wide), ALU.is_equal))
                if k == 0:
                    link(dve, dve.scalar_tensor_tensor(sel, chosen[:, k], -FAR, sel, ALU.mult, ALU.add))
            link(dve, dve.memset(m16[:, TILES], 0.0))
            dve.tensor_tensor(m16[:, 0:TILES], chosen[:, 0], chosen[:, 1], ALU.add).then_inc(chosen_ready, 1)
            dve.wait_ge(pos_ready, 1)
            s = lambda n, a: sums[:, n, E - a:2 * E - a]
            link(dve, dve.tensor_scalar(s(0, 0), ps[:, 4, TILES * E:(TILES + 1) * E], 1.0 / ST, (ST - 1) / 2 / ST,
                                        ALU.mult, ALU.add))
            link(dve, dve.tensor_scalar(s(0, 0), s(0, 0), MAGIC, MAGIC, ALU.add, ALU.subtract))
            for n in range(3):
                link(dve, dve.tensor_tensor(s(n + 1, 0), s(n, 0), s(n, 1 << n), ALU.add))
            link(dve, dve.tensor_tensor(first[:], s(3, 0), s(0, 0), ALU.subtract))
            link(dve, dve.tensor_scalar(first[:], first[:], float(ST), None, ALU.mult))
            link(dve, dve.tensor_tensor(slotf, ps[:, 4, 0:TILES * E].rearrange("p (j e) -> p j e", e=E),
                                        first[:].rearrange("p (a e) -> p a e", a=1).broadcast_to(wide), ALU.add))
            for k in range(2):
                link(dve, dve.tensor_tensor(t8, chosen[:, k], slotf, ALU.mult))
                link(dve, dve.tensor_reduce(slot[:, k].rearrange("p (j a) -> p j a", a=1), t8, AX.X, ALU.add))
            slots = slot.rearrange("p k j -> p (k j)")
            link(dve, dve.tensor_scalar(block_f[:], slots, 1.0 / P, (P - 1) / 2 / P, ALU.mult, ALU.subtract))
            link(dve, dve.tensor_scalar(block_f[:], block_f[:], MAGIC, MAGIC, ALU.add, ALU.subtract))
            dve.scalar_tensor_tensor(lane_f[:], block_f[:], -float(P), slots, ALU.mult, ALU.add)\
               .then_inc(lanes_ready, 1)
            dve.wait_ge(lanes_ready, 1)
            quarter = TILES // 2
            for b in range(len(DVE_PAIRS) - 1):
                t, n = DVE_PAIRS[b], DVE_PAIRS[b + 1] - DVE_PAIRS[b]
                row = lambda a, m: a.rearrange("p (a n) -> p a n", a=1).broadcast_to([P, n, m])
                each = lambda a, m: a.rearrange("p (n a) -> p n a", a=1).broadcast_to([P, n, m])
                blk = block1h[:, t:t + n]
                dve.tensor_tensor(blk, row(cst16[:, P:], BLOCKS), each(block_f[:, t:t + n], BLOCKS), ALU.is_equal)\
                   .then_inc(onehots, 1)
                dve.tensor_tensor(lane1h[:, t:t + n], row(cst16[:, 0:P], P), each(lane_f[:, t:t + n], P), ALU.is_equal)
                dve.wait_ge(onehots, 2 * b + 1)
                dve.tensor_tensor(blk, blk, each(cst[:, C_TILE:C_TILE + n], BLOCKS), ALU.mult).then_inc(onehots, 1)
            ends = sums[:, 3, E:2 * E - 1].rearrange("p (a e) -> p a e", a=1).broadcast_to([P, SLOT_TILES, E - 1])
            at = cst[:, C_SLOT_TILE:C_TRI].rearrange("p (n a) -> p n a", a=1).broadcast_to([P, SLOT_TILES, E - 1])
            link(dve, dve.tensor_tensor(le_n, ends, at, ALU.is_le))
            link(dve, dve.tensor_reduce(eot_f.rearrange("p (n a) -> p n a", a=1), le_n, AX.X, ALU.add))
            link(dve, dve.tensor_copy(expert_of[:], eot_f))
            dve.wait_ge(slots_ready, 1)
            found = ps[:, 7, 0:4 * BLOCKS].rearrange("p (q n) -> p q n", q=4)
            s1, s2 = by_slot[:, 0], by_slot[:, 1]
            link(dve, dve.tensor_copy(s2, found[:, 0]))
            for q in range(1, 4):
                link(dve, dve.tensor_scalar(s1, found[:, q], 0.5, float(q * quarter * P), ALU.is_gt, ALU.mult))
                link(dve, dve.tensor_tensor(s1, s1, found[:, q], ALU.add))
                link(dve, dve.tensor_tensor(s2, s2, s1, ALU.add))
            link(dve, dve.tensor_scalar(s1, s2, N + 0.5, -float(N), ALU.is_gt, ALU.mult))
            link(dve, dve.scalar_tensor_tensor(s1, s2, P - 1.0, s1, ALU.add, ALU.add))
            link(dve, dve.tensor_copy(row_of[:], s1))
            link(dve, dve.tensor_scalar(s1, s2, 0.5, None, ALU.is_lt))
            link(dve, dve.tensor_tensor(s1, s1, cst[:, C_PAD:C_PAD + BLOCKS], ALU.mult))
            dve.scalar_tensor_tensor(pair_of[:], s2, -1.0, s1, ALU.add, ALU.add).then_inc(route_done, 1)

        def is_tile(n, k):
            return isinstance(n, int) and n == k

        def psh(b):
            return ps[:, b].bitcast(F16)

        def bank_of(u):
            return u % 8

        def mix_groups(eng, mix):
            mix(0, 0)
            with eng.Fori(0, GROUPS // 2 - 1) as i:
                mix(2 * i + 1, 1)
                mix(2 * i + 2, 0)
            mix(GROUPS - 1, 1)

        def is_last(g):
            return isinstance(g, int) and g == GROUPS - 1

        def acc_index(p, q, j):
            return GT + 2 * GT * p + 4 * (q // 2) + 2 * j + q % 2

        def mixture_pe(pe):
            def split_matmul(dst, lhs, rhs, ks):
                for n, (a, b) in enumerate(((0, 0), (0, 1), (1, 0))):
                    for k in ks:
                        last = pe.matmul(dst, lhs(a, k), rhs(b, k), start=(n == 0 and k == ks[0]),
                                         stop=(n == 2 and k == ks[-1]))
                return last

            def reader_done(g, u):
                if u >= 8:
                    h, v = g, u - 8
                    if is_last(g) and U_NEXT <= v < U_OUT:
                        v -= 8
                elif isinstance(g, int) and g == 0:
                    return
                else:
                    h, v = g - 1, (u + 32 if u + 32 < UNITS else u + 24)
                if v == 0:
                    pe.wait_ge(rt_in, h + 1)
                elif v < U_ROUTED:
                    c = (v - U_SHARED) // 2
                    pe.wait_ge(vs_ready if (v - U_SHARED) % 2 else sa_used, HSC * h + c + 1)
                elif v < U_NEXT:
                    pe.wait_ge(vr_ready, E * h + v - U_ROUTED + 1)
                elif v < U_OUT:
                    pe.wait_ge(xs_T, 2 * h + 2 + v - U_NEXT + 1)
                elif v < U_PAIR:
                    pe.wait_ge(y_acc, YG * h + v - U_OUT + 1)
                else:
                    p, q = (v - U_PAIR) // GT, (v - U_PAIR) % GT
                    pe.wait_ge(y_acc, YG * h + acc_index(p, q, 1) + 1)

            def transposes(g, s):
                pe.wait_ge(xn_lo if s else xn_hi, g + 1)
                for k in range(DC):
                    for q in range(GT):
                        last = pe.transpose(psh(bank_of(U_NEXT + s))[:, k * GN + q * P:k * GN + (q + 1) * P],
                                            xsn[:, s, q * D + k * P:q * D + (k + 1) * P], identh[:])
                last.then_inc(unit, 1)

            pe.wait_ge(out_ready, SLOT_TILES)
            pe.wait_ge(mix_start, 1)
            for k in range(DC):
                last = pe.matmul(ps[:, 0, 0:E], h0rep[:, k], rtw[:, k], start=(k == 0), stop=(k == DC - 1))
            last.then_inc(unit, 1)
            for s in range(2):
                transposes(0, s)

            def mix(g, buf):
                xh = lambda s, k: xs[:, buf, s, k]
                if isinstance(g, int) and g == 0:
                    pe.wait_ge(tb_ready, 1)
                reader_done(g, 0)
                pe.wait_ge(xs_T, 2 * g + 2)
                for q in range(GT):
                    last = split_matmul(ps[:, 0, q * E:(q + 1) * E], lambda s, k: xs[:, buf, s, k, q * P:(q + 1) * P],
                                        lambda s, k: rw_s[:, s, k], range(DC))
                last.then_inc(unit, 1)
                for c in range(HSC):
                    for m, w in enumerate((sw1s, sw3s)):
                        u = U_SHARED + 2 * c + m
                        reader_done(g, u)
                        split_matmul(ps[:, bank_of(u)], lambda s, k: w[:, s, k, c * P:(c + 1) * P], xh,
                                     range(DC)).then_inc(unit, 1)
                for e in range(E):
                    u = U_ROUTED + e
                    reader_done(g, u)
                    split_matmul(ps[:, bank_of(u)], lambda s, k: rw1s[:, s, k, e * P:(e + 1) * P], xh,
                                 range(DC)).then_inc(unit, 1)
                if not is_last(g):
                    for s in range(2):
                        reader_done(g, U_NEXT + s)
                        transposes(g + 1, s)
                for q in range(GT):
                    u = U_OUT + q
                    reader_done(g, u)
                    if q == 0:
                        pe.wait_ge(lo1, HC * g + HSC)
                    split_matmul(ps[:, bank_of(u), 0:D], lambda s, k: hid1[:, s, k, q * P:(q + 1) * P],
                                 lambda s, k: sw2s[:, s, k], range(HSC)).then_inc(unit, 1)
                for p in range(E // 2):
                    for q in range(GT):
                        u = U_PAIR + GT * p + q
                        reader_done(g, u)
                        if q == 0:
                            pe.wait_ge(lo1, HC * g + HSC + 2 * p + 2)
                        for j in range(2):
                            last = split_matmul(ps[:, bank_of(u), j * D:(j + 1) * D],
                                                lambda s, k: hid1[:, s, HSC + 2 * p + j, q * P:(q + 1) * P],
                                                lambda s, k: rw2s[:, s, 2 * p + j], range(1))
                        last.then_inc(unit, 1)

            mix_groups(pe, mix)

        def mixture_act(act):
            def input_hi(g):
                act.wait_ge(x1_ready, g + 1)
                act.activation(xsn[:, 0], x1[:, bass.ds(GT * g, GT)].rearrange("p q d -> p (q d)"), ACT.Copy,
                               scale=A_SCALE).then_inc(xn_hi, 1)

            def input_T(buf, s):
                act.activation(xs[:, buf, s].rearrange("p k n -> p (k n)"), psh(bank_of(U_NEXT + s)), ACT.Copy)\
                   .then_inc(xs_T, 1)

            input_hi(0)
            for s in range(2):
                act.wait_ge(unit, 2 + s)
                input_T(0, s)

            def mix(g, buf):
                base = PRE_UNITS + UNITS * g
                act.wait_ge(rt_in, g + 1)
                act.activation(score[:], r_sel[:], ACT.Tanh, scale=0.5).then_inc(rt_sig, 1)
                if not is_last(g):
                    act.wait_ge(xs_T, 2 * g + 2)
                    input_hi(g + 1)

                def hi_part(c):
                    if c < HSC:
                        act.wait_ge(vs_ready, HSC * g + c + 1)
                    else:
                        act.wait_ge(vr_ready, E * g + c - HSC + 1)
                    act.activation(hid1[:, 0, c], vs[:, c % 3], ACT.Copy,
                                   scale=V_SCALE / (2 * MIX_SCALE) if c < HSC else V_SCALE).then_inc(hi1, 1)

                for c in range(HC):
                    u = U_SHARED + 2 * c if c < HSC else U_ROUTED + c - HSC
                    act.wait_ge(unit, base + u + 1)
                    if c < HSC:
                        act.wait_ge(sa_used, HSC * g + max(c - 1, 0))
                        act.activation(v32[:, c % 2], ps[:, bank_of(u)], ACT.Tanh, scale=0.5 / MIX_SCALE)\
                           .then_inc(th_ready, 1)
                    else:
                        act.wait_ge(lo1, HC * g + c - 2)
                        act.activation(vs[:, c % 3], ps[:, bank_of(u)], ACT.Gelu, scale=1.0 / MIX_SCALE)\
                           .then_inc(vr_ready, 1)
                    if c >= 1:
                        hi_part(c - 1)
                hi_part(HC - 1)
                if not is_last(g):
                    for s in range(2):
                        act.wait_ge(unit, base + U_NEXT + s + 1)
                        input_T(1 - buf, s)

            mix_groups(act, mix)

        def mixture_dve(dve):
            dve.wait_ge(l2_psum, SLOT_TILES)
            rep_b = [P, P // BATCH, BATCH]
            link(dve, dve.tensor_copy(h0rep[:, 0].rearrange("p (r b) -> p r b", b=BATCH), h0[:, 0:1].broadcast_to(rep_b)))
            dve.tensor_copy(h0rep[:, 1].rearrange("p (r b) -> p r b", b=BATCH), h0[:, 1:2].broadcast_to(rep_b))\
               .then_inc(mix_start, 1)
            dve.wait_ge(o_arrived[0], 32)
            dve.tensor_tensor(o_in[:, 0, 0], o_in[:, 0, 0], o_in[:, 0, 1], ALU.add).then_inc(x1_first, 1)
            dve.wait_ge(x_in[0], 16)
            dve.wait_ge(x1_first, 1)
            dve.tensor_tensor(x1[:, 0:GT], x1[:, 0:GT], o_in[:, 0, 0], ALU.add).then_inc(x1_ready, 1)
            dve.wait_ge(unit, 1)
            dve.tensor_copy(t_bias[:], ps[:, 0, 0:E]).then_inc(tb_ready, 1)

            def input_lo(g):
                dve.wait_ge(xn_hi, g + 1)
                dve.scalar_tensor_tensor(xsn[:, 1], x1[:, bass.ds(GT * g, GT)].rearrange("p q d -> p (q d)"), A_SCALE,
                                         xsn[:, 0], ALU.mult, ALU.subtract).then_inc(xn_lo, 1)

            input_lo(0)
            wide = [P, GT, E]
            rb = rb_row[:].rearrange("p (a e) -> p a e", a=1).broadcast_to(wide)
            tb = t_bias[:].rearrange("p (a e) -> p a e", a=1).broadcast_to(wide)
            pr = prio[:].rearrange("p (a e) -> p a e", a=1).broadcast_to(wide)
            s, t, o, mk, a, b = r_sel[:], r_t8[:], r_one[:], r_mask[:], r_m1[:], r_k1[:]

            def mix(g, buf):
                base = PRE_UNITS + UNITS * g
                made = [0]

                def then(ins):
                    made[0] += 1
                    ins.then_inc(router_step, 1)
                    dve.wait_ge(router_step, LINKS * g + made[0])

                def lo_part(c):
                    dve.wait_ge(hi1, HC * g + c + 1)
                    dve.scalar_tensor_tensor(hid1[:, 1, c], vs[:, c % 3],
                                             V_SCALE / (2 * MIX_SCALE) if c < HSC else V_SCALE, hid1[:, 0, c],
                                             ALU.mult, ALU.subtract).then_inc(lo1, 1)

                def shared(c):
                    dve.wait_ge(th_ready, HSC * g + c + 1)
                    dve.scalar_tensor_tensor(vs[:, c % 3], v32[:, c % 2], 1.0, ps[:, bank_of(U_SHARED + 2 * c)],
                                             ALU.add, ALU.mult).then_inc(sa_used, 1)
                    dve.wait_ge(sa_used, HSC * g + c + 1)
                    dve.wait_ge(unit, base + U_SHARED + 2 * c + 2)
                    dve.scalar_tensor_tensor(vs[:, c % 3], ps[:, bank_of(U_SHARED + 2 * c + 1)], 1.0 / MIX_SCALE,
                                             vs[:, c % 3], ALU.mult, ALU.mult).then_inc(vs_ready, 1)
                    if c >= 1:
                        lo_part(c - 1)

                def gates(part):
                    if part == 0:
                        then(dve.tensor_tensor(mk, mk, o, ALU.add))
                        then(dve.tensor_tensor(t, score[:], mk, ALU.mult))
                        then(dve.tensor_reduce(a, t, AX.X, ALU.add))
                    elif part == 1:
                        then(dve.tensor_scalar(b, a, EPS_GATE, 1.0 / OUT_SCALE, ALU.is_gt, ALU.mult))
                        then(dve.tensor_scalar(a, a, EPS_GATE, None, ALU.add))
                        then(dve.reciprocal(a, a))
                    elif part == 2:
                        then(dve.tensor_tensor(t, t, a.broadcast_to(wide), ALU.mult))
                        then(dve.tensor_tensor(t, t, b.broadcast_to(wide), ALU.mult))
                    else:
                        then(dve.tensor_scalar(b, b, -0.5, 0.5 / OUT_SCALE, ALU.mult, ALU.add))
                        then(dve.tensor_tensor(mk, mk, b.broadcast_to(wide), ALU.mult))
                        then(dve.tensor_tensor(comb[:], t, mk, ALU.add))

                dve.wait_ge(unit, base + 1)
                if isinstance(g, int) and g == 0:
                    dve.wait_ge(tb_ready, 1)
                dve.scalar_tensor_tensor(s, ps[:, 0, 0:GT * E].rearrange("p (q e) -> p q e", e=E),
                                         1.0 / MIX_SCALE, tb, ALU.mult, ALU.add).then_inc(rt_in, 1)
                dve.wait_ge(rt_sig, g + 1)
                then(dve.tensor_scalar(score[:], score[:], 0.5, 0.5, ALU.mult, ALU.add))
                then(dve.tensor_tensor(s, score[:], rb, ALU.add))
                for k in range(2):
                    dst = mk if k else o
                    then(dve.tensor_reduce(a, s, AX.X, ALU.max))
                    then(dve.tensor_tensor(t, s, a.broadcast_to(wide), ALU.is_equal))
                    then(dve.tensor_tensor(t, t, pr, ALU.mult))
                    then(dve.tensor_reduce(b, t, AX.X, ALU.max))
                    then(dve.tensor_tensor(dst, t, b.broadcast_to(wide), ALU.is_equal))
                    if k == 0:
                        then(dve.scalar_tensor_tensor(s, dst, -FAR, s, ALU.mult, ALU.add))
                    shared(k)
                if not is_last(g):
                    input_lo(g + 1)

                for c in range(2, HSC):
                    shared(c)
                for c in range(HSC, HC):
                    lo_part(c - 1)
                    if 1 <= c - HSC < 5:
                        gates(c - HSC - 1)
                assert made[0] == LINKS
                lo_part(HC - 1)
                if is_last(g):
                    base -= 2
                for q in range(GT):
                    dve.wait_ge(unit, base + U_OUT + q + 1)
                    dve.tensor_scalar(y[:, GT * g + q], ps[:, bank_of(U_OUT + q), 0:D], 1.0 / OUT_SCALE, None,
                                      ALU.mult).then_inc(y_acc, 1)
                for p in range(E // 2):
                    for q2 in range(0, GT, 2):
                        for j in range(2):
                            for q in (q2, q2 + 1):
                                if j == 0:
                                    dve.wait_ge(unit, base + U_PAIR + GT * p + q + 1)
                                before = acc_index(p, q, 0) if j else (acc_index(p - 1, q, 1) if p else q)
                                dve.wait_ge(y_acc, YG * g + before + 1)
                                dve.scalar_tensor_tensor(
                                    y[:, GT * g + q], ps[:, bank_of(U_PAIR + GT * p + q), j * D:(j + 1) * D],
                                    comb[:, q, 2 * p + j:2 * p + j + 1], y[:, GT * g + q], ALU.mult, ALU.add)\
                                   .then_inc(y_acc, 1)
                dve.wait_ge(y_acc, YG * g + YG)
                dve.tensor_reduce(ymax[:, bass.ds(g, 1)], y[:, bass.ds(GT * g, GT)].rearrange("p q d -> p (q d)"),
                                  AX.X, ALU.max).then_inc(ymax_in, 1)

            mix_groups(dve, mix)

        def psb(b, n=1):
            return ps[:, b:b + n].rearrange("p b n -> p (b n)").bitcast(BF16)

        DVE_CHUNKS, ACT_CHUNKS, POOL_CHUNKS = (0, 3, 6), (1, 4), (2, 5, 7)

        def ffn_groups(eng, group):
            for g in (0, 1):
                group(g, g)
            with eng.Fori(1, GROUPS // 2 - 1) as i:
                group(2 * i, 0)
                group(2 * i + 1, 1)
            for g in (GROUPS - 2, GROUPS - 1):
                group(g, g % 2)

        def wait_rounded(eng, g, f):
            for chunks, done in ((DVE_CHUNKS, hb_qd), (ACT_CHUNKS, hb_qa), (POOL_CHUNKS, hb_qp)):
                if f in chunks:
                    eng.wait_ge(done, len(chunks) * g + chunks.index(f) + 1)

        def ffn_pe(pe):
            pe.wait_ge(y_acc, YG * GROUPS)
            pe.wait_ge(mw_used, 11)
            for k in range(DC):
                for c in range(FC):
                    last = pe.transpose(psb(k)[:, c * P:(c + 1) * P],
                                        wq_n[:, 0, c * D + k * P:c * D + (k + 1) * P], identb[:])
                last.then_inc(wt_ps, 1)
            for h in range(2):
                for c in range(FC // 2):
                    for k in range(DC):
                        f = FC // 2 * h + c
                        last = pe.transpose(psb(2 + h)[:, c * D + k * P:c * D + (k + 1) * P],
                                            wq_n[:, 1, k * F + f * P:k * F + (f + 1) * P], identb[:])
                last.then_inc(wt_ps, 1)
            pe.wait_ge(diag_ready, DC)
            for k in range(DC):
                last = pe.matmul(ps[:, 4, k * P:(k + 1) * P], ones[:], diag[:, k], start=True, stop=True)
            last.then_inc(wt_ps, 1)
            def transposes(g):
                pe.wait_ge(yq_n, g + 1)
                if g >= 2:
                    pe.wait_ge(yq_T, g - 1)
                for k in range(DC):
                    for q in range(GT):
                        at = (g % 2) * GT * D + q * D + k * P
                        last = pe.transpose(psb(5 + g % 2)[:, k * GN + q * P:k * GN + (q + 1) * P], yqn[:, at:at + P],
                                            identb[:])
                last.then_inc(yq_ps, 1)

            def row_max(n):
                pe.wait_ge(yq_T, 2 * n + 2)
                for f in range(FC):
                    if FC * n + f >= 2:
                        pe.wait_ge(ia_mx, FC * n + f - 1)
                    for m in range(2):
                        for k in range(DC):
                            last = pe.matmul(ps[:, 2 * (f % 2) + m], w1qT[:, k, f * P:(f + 1) * P],
                                             yqT[:, k, (2 * n + m) * GN:(2 * n + m + 1) * GN],
                                             start=(k == 0), stop=(k == DC - 1))
                    last.then_inc(ia_ps, 1)

            pe.wait_ge(wt_cp, 5)
            for n, groups in enumerate((range(0, 3), range(3, 6), range(6, 8), ())):
                for g in groups:
                    transposes(g)
                row_max(n)
            pe.wait_ge(ia_mx, FC * GROUPS // 2)

            def hidden(g):
                for f in range(FC):
                    if not (is_tile(g, 0) and f < 4):
                        pe.wait_ge(hb_h, FC * g + f - 3)
                    for k in range(DC):
                        last = pe.matmul(ps[:, f % 4], w1qT[:, k, f * P:(f + 1) * P], yqT[:, k, bass.ds(GN * g, GN)],
                                         start=(k == 0), stop=(k == DC - 1))
                    last.then_inc(hb_ps, 1)

            def group(g, buf):
                if not is_last(g):
                    hidden(g + 1)
                if not is_tile(g, 0) and not is_tile(g, 1):
                    pe.wait_ge(ob_s, 2 * (g - 1))
                for q in range(GT):
                    for f in range(FC):
                        if q == 0:
                            wait_rounded(pe, g, f)
                        last = pe.matmul(ps[:, 4 + 2 * buf + q // 2, (q % 2) * D:(q % 2 + 1) * D],
                                         hq[buf][:, f, q * P:(q + 1) * P], w2qT[:, f], start=(f == 0), stop=(f == FC - 1))
                    if q % 2:
                        last.then_inc(ob_ps, 1)

            hidden(0)
            ffn_groups(pe, group)

        def ffn_act(act):
            for n in range(4):
                act.wait_ge(wt_ps, n + 1)
                dst = w1qT[:, n] if n < 2 else w2qT[:, FC // 2 * (n - 2):FC // 2 * (n - 1)].rearrange("p f d -> p (f d)")
                act.activation(dst, psb(n), ACT.Copy).then_inc(wt_cp, 1)
            act.wait_ge(wt_ps, 5)
            act.activation(rs2, ps[:, 4, 0:D], ACT.Copy).then_inc(wt_cp, 1)

            def transposed(g):
                act.wait_ge(yq_ps, g + 1)
                act.activation(yqT[:, :, g * GN:(g + 1) * GN], psb(5 + g % 2).rearrange("p (k n) -> p k n", k=DC),
                               ACT.Copy).then_inc(yq_T, 1)

            for g in range(GROUPS):
                act.wait_ge(yq_m, 2 * g + 2)
                if g >= 2:
                    act.wait_ge(yq_ps, g - 1)
                act.activation(yqn[:, (g % 2) * GT * D:(g % 2 + 1) * GT * D],
                               y[:, GT * g:GT * g + GT].rearrange("p q d -> p (q d)"), ACT.Relu,
                               bias=neg_magic[:]).then_inc(yq_n, 1)
                if g >= 1:
                    transposed(g - 1)
            transposed(GROUPS - 1)
            act.wait_ge(bq_ready, 2)

            def group(g, buf):
                for f in range(FC + 2):
                    if f < FC:
                        act.wait_ge(hb_ps, FC * g + f + 1)
                        if f >= 4:
                            wait_rounded(act, g, f - 4)
                        elif not is_tile(g, 0):
                            wait_rounded(act, g - 1, f + 4)
                        act.activation(vq[:, f % 4], ps[:, f % 4], ACT.Relu, scale=sc1[:, f:f + 1],
                                       bias=fb1[:, f:f + 1]).then_inc(hb_h, 1)
                    if f - 2 in ACT_CHUNKS:
                        if f - 2 == ACT_CHUNKS[0] and not is_tile(g, 0) and not is_tile(g, 1):
                            act.wait_ge(ob_ps, 2 * (g - 1))
                        act.wait_ge(hb_s, FC * g + f - 1)
                        act.activation(hq[buf][:, f - 2], vq[:, (f - 2) % 4], ACT.Relu, bias=neg_magic[:])\
                           .then_inc(hb_qa, 1)

            ffn_groups(act, group)

        pool_steps = [0]

        def then_pool(pool, ins):
            pool_steps[0] += 1
            ins.then_inc(pool_step, 1)
            pool.wait_ge(pool_step, pool_steps[0])

        def round_bias(dve, b, scale, r):
            link(dve, dve.reciprocal(r, scale))
            link(dve, dve.tensor_tensor(b, b, r, ALU.mult))
            link(dve, dve.tensor_scalar(b, b, MAGIC, MAGIC, ALU.add, ALU.subtract))
            return dve.tensor_tensor(b, b, scale, ALU.mult)

        def ffn_dve(dve):
            dve.wait_ge(ymax_in, GROUPS)
            link(dve, dve.memset(neg_magic[:], -MAGIC))
            dve.tensor_reduce(pmax[:, 0:1], ymax[:], AX.X, ALU.max).then_inc(mx_in, 1)
            dve.wait_ge(mx_out, 1)
            link(dve, dve.reciprocal(inv[:, 0:1], gmax[:, 0:1]))
            link(dve, dve.tensor_scalar(inv[:, 0:1], inv[:, 0:1], 1.0 / 3.0, None, ALU.mult))

            def round_y(g):
                yg = y[:, GT * g:GT * g + GT].rearrange("p q d -> p (q d)")
                dve.tensor_scalar(yg, yg, inv[:, 0:1], 255.0, ALU.mult, ALU.min).then_inc(yq_m, 1)
                dve.wait_ge(yq_m, 2 * g + 1)
                dve.tensor_scalar(yg, yg, MAGIC, None, ALU.add).then_inc(yq_m, 1)

            for g in range(6):
                round_y(g)
            link(dve, dve.tensor_scalar(sc1[:], sw[:, 0:FC], gmax[:, 0:1], None, ALU.mult))
            round_bias(dve, fb1[:], sc1[:], vs[:, 0, 0:FC]).then_inc(bq_ready, 1)

            for n in range(GROUPS // 2):
                if n == 1:
                    for g in range(6, GROUPS):
                        round_y(g)
                for f in range(FC):
                    dve.wait_ge(ia_ps, FC * n + f + 1)
                    dve.tensor_reduce(imax[:, f, n:n + 1],
                                      ps[:, 2 * (f % 2):2 * (f % 2) + 2].rearrange("p b n -> p (b n)"),
                                      AX.X, ALU.max).then_inc(ia_mx, 1)
            dve.wait_ge(ia_mx, FC * GROUPS // 2)
            dve.wait_ge(bq_ready, 1)
            link(dve, dve.tensor_reduce(hmax[:], imax[:], AX.X, ALU.max))
            link(dve, dve.tensor_tensor(hmax[:], hmax[:], sc1[:], ALU.mult))
            link(dve, dve.tensor_tensor(hmax[:], hmax[:], fb1[:], ALU.add))
            dve.tensor_reduce(pmax[:, 1:2], hmax[:], AX.X, ALU.max).then_inc(mx_in, 1)
            dve.wait_ge(mx_out, 2)
            link(dve, dve.reciprocal(inv[:, 1:2], gmax[:, 1:2]))
            link(dve, dve.tensor_scalar(sc1[:], sc1[:], inv[:, 1:2], None, ALU.mult))
            dve.tensor_scalar(fb1[:], fb1[:], inv[:, 1:2], None, ALU.mult).then_inc(bq_ready, 1)

            def outputs(g, buf, half, part):
                if part == 0:
                    dve.wait_ge(ob_ps, 2 * g + half + 1)
                    if not is_tile(g, 0):
                        dve.wait_ge(ob, 2 * g)
                    dve.tensor_tensor(ov[:, half], ps[:, 4 + 2 * buf + half].rearrange("p (q d) -> p q d", q=2),
                                      rs2.rearrange("p (a d) -> p a d", a=1).broadcast_to([P, 2, D]), ALU.mult)\
                       .then_inc(ob_s, 1)
                else:
                    if half == 0:
                        dve.wait_ge(xb_ready, g + 1)
                    dve.wait_ge(ob_s, 2 * g + half + 1)
                    xh = x1[:, bass.ds(GT * g + 2 * half, 2)]
                    dve.tensor_tensor(xh, xh, ov[:, half], ALU.add).then_inc(ob, 1)

            def hidden(g, buf, between=None):
                for f in range(FC):
                    dve.wait_ge(hb_h, FC * g + f + 1)
                    dve.tensor_scalar(vq[:, f % 4], vq[:, f % 4], 255.0, MAGIC, ALU.min, ALU.add).then_inc(hb_s, 1)
                    if f - 1 in DVE_CHUNKS:
                        if f - 1 == DVE_CHUNKS[0] and not is_tile(g, 0) and not is_tile(g, 1):
                            dve.wait_ge(ob_ps, 2 * (g - 1))
                        dve.wait_ge(hb_s, FC * g + f)
                        dve.tensor_scalar(hq[buf][:, f - 1], vq[:, (f - 1) % 4], MAGIC, None, ALU.subtract)\
                           .then_inc(hb_qd, 1)
                    if between and f % 2:
                        outputs(*between, f // 4, f % 4 // 2)

            def group(g, buf):
                if not is_last(g):
                    hidden(g + 1, 1 - buf, None if is_tile(g, 0) else (g - 1, 1 - buf))

            hidden(0, 0)
            dve.wait_ge(wt_cp, 5)
            link(dve, dve.tensor_scalar(rs2, rs2, gmax[:, 1:2], None, ALU.mult))
            dve.wait_ge(bq2_in, 16)
            round_bias(dve, bq2, rs2, vs[:, 0, 0:D]).then_inc(bq_ready, 1)
            ffn_groups(dve, group)
            for g in (GROUPS - 2, GROUPS - 1):
                for n in range(4):
                    outputs(g, g % 2, n // 2, n % 2)

        def ffn_pool(pool):
            def add_results(g, h, p):
                pool.wait_ge(x_in[p], 16 * h + 16)
                pool.wait_ge(o_arrived[p], 32 * h + 32)
                pool.tensor_tensor(o_in[:, p, 0], o_in[:, p, 0], o_in[:, p, 1], ALU.add).then_inc(x1_step, 1)
                pool.wait_ge(x1_step, g)
                pool.wait_ge(x1_ready, g)
                xg_ = x1[:, bass.ds(GT * g, GT)]
                pool.tensor_tensor(xg_, xg_, o_in[:, p, 0], ALU.add).then_inc(x1_ready, 1)

            add_results(1, 0, 1)
            for c in range(DC):
                pool.tensor_scalar(diag[:, c], ident[:], sw[:, FC + c:FC + c + 1], None, ALU.mult)\
                    .then_inc(diag_ready, 1)
            with pool.Fori(1, GROUPS // 2) as h:
                for p in range(2):
                    add_results(2 * h + p, h, p)

            pool.wait_ge(mx_in, 1)
            then_pool(pool, pool.partition_all_reduce(gmax[:, 0:1], pmax[:, 0:1], P, RMAX))
            then_pool(pool, pool.tensor_scalar(gmax[:, 0:1], gmax[:, 0:1], 1.0 / 3.0, EPS_QUANT, ALU.mult, ALU.max))
            pool.tensor_scalar(gmax[:, 0:1], gmax[:, 0:1], 1.0 / 255.0, None, ALU.mult).then_inc(mx_out, 1)
            pool.wait_ge(mx_in, 2)
            then_pool(pool, pool.partition_all_reduce(gmax[:, 1:2], pmax[:, 1:2], P, RMAX))
            pool.tensor_scalar(gmax[:, 1:2], gmax[:, 1:2], EPS_QUANT, 1.0 / 255.0, ALU.max, ALU.mult).then_inc(mx_out, 1)
            wide = bq2.rearrange("p (a d) -> p a d", a=1).broadcast_to([P, GT, D])
            def group(g, buf):
                for n, f in enumerate(POOL_CHUNKS):
                    if n == 0 and not is_tile(g, 0) and not is_tile(g, 1):
                        pool.wait_ge(ob_ps, 2 * (g - 1))
                    pool.wait_ge(hb_s, FC * g + f + 1)
                    pool.tensor_tensor(hq[buf][:, f], vq[:, f % 4], magic[:].broadcast_to([P, GN]), ALU.subtract)\
                        .then_inc(hb_qp, 1)
                    pool.wait_ge(hb_qp, len(POOL_CHUNKS) * g + n + 1)
                pool.wait_ge(bq_ready, 3)
                xg_ = x1[:, bass.ds(GT * g, GT)]
                pool.tensor_tensor(xg_, xg_, wide, ALU.add).then_inc(xb_ready, 1)
                pool.wait_ge(xb_ready, g + 1)

            ffn_groups(pool, group)

        def slot_tiles(eng, tile):
            for n in range(JOBS):
                tile(n, n // 2, n % 2)
            with eng.Fori(0, (SLOT_TILES - 2 - JOBS) // 2) as i:
                tile(2 * i + JOBS, i + JOBS // 2, 1)
                tile(2 * i + JOBS + 1, i + JOBS // 2 + 1, 0)
            for n in range(SLOT_TILES - 2, SLOT_TILES):
                tile(n, n // 2, n % 2)

        def experts_pe(pe):
            def transposes(n, m, p):
                pe.wait_ge(xg_in[p], 32 * m + 32)
                for s in range(2):
                    for k in range(DC):
                        for q in range(SQ):
                            c = (s * DC + k) * ST + q * P
                            last = pe.transpose(psh(6)[:, c:c + P], xg[:, p, q, (s * DC + k) * P:(s * DC + k + 1) * P],
                                                identh[:])
                last.then_inc(xT_ps, 1)

            pe.wait_ge(w_split, 96)
            pe.wait_ge(route_done, 1)
            transposes(0, 0, 0)

            def tile(n, m, p):
                e = pe.value_load(expert_of[0:1, bass.ds(n, 1)], min_val=0, max_val=E - 1)
                of_e = lambda a: a.rearrange("p a n -> p (a n)")
                pe.wait_ge(xT_ready, n + 1)
                for f in range(FC):
                    if not (is_tile(n, 0) and f < 4):
                        pe.wait_ge(l1_v, FC * n + f - 3)
                    for i, (a, b) in enumerate(((0, 0), (0, 1), (1, 0))):
                        for k in range(DC):
                            last = pe.matmul(ps[:, f % 4, 0:ST],
                                             of_e(W1[:, bass.ds(e, 1), a, k, f * P:(f + 1) * P]), xT[:, p, b, k],
                                             start=(i == 0 and k == 0), stop=(i == 2 and k == DC - 1))
                    last.then_inc(l1_psum, 1)
                if not is_tile(n, SLOT_TILES - 1):
                    transposes(n + 1, m + p, 1 - p)
                if not is_tile(n, 0):
                    pe.wait_ge(out_ready, n)
                for f in range(FC):
                    pe.wait_ge(l1_hid, FC * n + f + 1)
                    for i, (a, b) in enumerate(((0, 0), (1, 0), (0, 1))):
                        for q in range(SQ):
                            last = pe.matmul(ps[:, 4 + q, 0:D], hid[:, a, f, q * P:(q + 1) * P],
                                             of_e(W2[:, bass.ds(e, 1), b, f]), start=(i == 0 and f == 0),
                                             stop=(i == 2 and f == FC - 1))
                last.then_inc(l2_psum, 1)

            slot_tiles(pe, tile)

        def experts_act(act):
            def transposed(n, p):
                act.wait_ge(xT_ps, n + 1)
                act.activation(xT[:, p].rearrange("p s k n -> p (s k n)"), psh(6), ACT.Copy).then_inc(xT_ready, 1)

            transposed(0, 0)

            def tile(n, m, p):
                for f in range(FC):
                    act.wait_ge(l1_psum, FC * n + f + 1)
                    if f == 0:
                        act.wait_ge(b1_ready, n + 1)
                    if not (is_tile(n, 0) and f < 4):
                        act.wait_ge(l1_hid, FC * n + f - 3)
                    act.activation(v4[:, f % 4], ps[:, f % 4, 0:ST], ACT.Relu, bias=b1_now[:, p, f:f + 1],
                                   scale=A_SCALE / W_SCALE).then_inc(l1_v, 1)
                if not is_tile(n, SLOT_TILES - 1):
                    transposed(n + 1, 1 - p)

            slot_tiles(act, tile)

        def split_piece(dve, c):
            dve.wait_ge(mw_in[c % 2], 16 * (c // 2) + 16)
            hi, lo = l1w[:, 0, 1024 * c:1024 * (c + 1)], l1w[:, 1, 1024 * c:1024 * (c + 1)]
            link(dve, dve.tensor_scalar(hi, stage[:, c % 2], W_SCALE, None, ALU.mult))
            dve.scalar_tensor_tensor(lo, stage[:, c % 2], W_SCALE, hi, ALU.mult, ALU.subtract).then_inc(mw_used, 1)

        def ffn_rows(c):
            a, n = (4 * c, 4) if c < 2 else (FC + c - 2, 1)
            return slice(a, a + n), stage[:, (7 + c) % 2].rearrange("p (c n) -> p c n", c=n)

        def scale_piece(dve, c):
            dve.wait_ge(mw_in[(7 + c) % 2], 16 * ((7 + c) // 2) + 16)
            r, st = ffn_rows(c)
            link(dve, dve.tensor_reduce(sw[:, r], st, AX.X, ALU.max))
            link(dve, dve.tensor_reduce(swr[:, r], st, AX.X, ALU.min))
            link(dve, dve.scalar_tensor_tensor(sw[:, r], swr[:, r], -1.0, sw[:, r], ALU.mult, ALU.max))
            link(dve, dve.tensor_scalar(sw[:, r], sw[:, r], EPS_QUANT, 1.0 / 127.0, ALU.max, ALU.mult))
            link(dve, dve.reciprocal(swr[:, r], sw[:, r]))

        def quantise_piece(dve, c):
            r, st = ffn_rows(c)
            for k in range(r.stop - r.start):
                link(dve, dve.tensor_scalar(st[:, k], st[:, k], swr[:, r.start + k:r.start + k + 1], -128.0,
                                            ALU.mult, ALU.max))
            st = stage[:, (7 + c) % 2]
            link(dve, dve.tensor_scalar(st, st, 127.0, MAGIC, ALU.min, ALU.add))
            dve.tensor_scalar(wq_n[:, c // 2, 1024 * (c % 2):1024 * (c % 2) + 1024], st, MAGIC, None, ALU.subtract)\
               .then_inc(mw_used, 1)

        def experts_dve(dve):
            def results(n, m, p):
                dve.wait_ge(l2_psum, n + 1)
                dve.wait_ge(b2_in[p], 16 * m + 16)
                if not is_tile(m, 0):
                    dve.wait_ge(pairs_out[p], 32 * m)
                b2_ = b2_now[:, p].rearrange("p (a d) -> p a d", a=1).broadcast_to([P, SQ, D])
                dve.scalar_tensor_tensor(obuf[:, p], ps[:, 4:4 + SQ, 0:D], 1.0 / (W_SCALE * A_SCALE), b2_,
                                         ALU.mult, ALU.add).then_inc(out_ready, 1)

            def tile(n, m, p):
                if not is_tile(n, 0):
                    results(n - 1, m - 1 + p, 1 - p)
                for f in range(FC):
                    dve.wait_ge(l1_v, FC * n + f + 1)
                    if f == 0 and not is_tile(n, 0):
                        dve.wait_ge(l2_psum, n)
                    dve.tensor_copy(hid[:, 0, f], v4[:, f % 4]).then_inc(split0, 1)
                    dve.wait_ge(split0, FC * n + f + 1)
                    dve.tensor_tensor(hid[:, 1, f], v4[:, f % 4], hid[:, 0, f], ALU.subtract).then_inc(l1_hid, 1)
                if isinstance(n, int):
                    if n < 4:
                        for c in range(2 * n, min(2 * n + 2, 7)):
                            split_piece(dve, c)
                    if 4 <= n < 8:
                        scale_piece(dve, n - 4)
                    if 5 <= n < 9:
                        quantise_piece(dve, n - 5)
                    if n == 3:
                        link(dve, dve.tensor_scalar(rw_s[:, 0], rw[:], W_SCALE, None, ALU.mult))
                        link(dve, dve.scalar_tensor_tensor(rw_s[:, 1], rw[:], W_SCALE, rw_s[:, 0], ALU.mult,
                                                           ALU.subtract))

            slot_tiles(dve, tile)
            results(SLOT_TILES - 1, SLOT_TILES // 2, 0)

        def experts_pool(pool):
            def row_indices(n, m, p):
                if not is_tile(m, 0):
                    pool.wait_ge(xg_in[p], 32 * m)
                    pool.wait_ge(xT_ps, n - 1)
                pool.tensor_copy(row_now[:, p], row_of[:, bass.ds(SQ * n, SQ)]).then_inc(row_idx, 1)
                pool.wait_ge(row_idx, n + 1)

            def gather(p):
                for q in range(SQ):
                    pool.indirect_dma_start(out=xg[:, p, q], out_offset=None, in_=rows_d,
                                            in_offset=bass.IndirectOffsetOnAxis(ap=row_now[:, p, q:q + 1], axis=0))\
                        .then_inc(xg_in[p], 16)

            def pair_indices(n, m, p):
                if not is_tile(m, 0):
                    pool.wait_ge(pairs_out[p], 32 * m)
                pool.tensor_copy(pair_now[:, p], pair_of[:, bass.ds(SQ * n, SQ)]).then_inc(pair_idx, 1)
                pool.wait_ge(pair_idx, n + 1)
                pool.wait_ge(out_ready, n + 1)

            def scatter(p):
                for q in range(SQ):
                    pool.indirect_dma_start(out=pairs_d, in_=obuf[:, p, q], in_offset=None,
                                            out_offset=bass.IndirectOffsetOnAxis(ap=pair_now[:, p, q:q + 1], axis=0))\
                        .then_inc(pairs_out[p], 16)

            def expert(n):
                return pool.value_load(expert_of[0:1, bass.ds(n, 1)], min_val=0, max_val=E - 1)

            def bias(n, p, e):
                if not is_tile(n, 0) and not is_tile(n, 1):
                    pool.wait_ge(l1_v, FC * n - FC)
                pool.tensor_copy(b1_now[:, p], b1s[:, bass.ds(e, 1)].rearrange("p a n -> p (a n)")).then_inc(b1_ready, 1)
                pool.wait_ge(b1_ready, n + 1)

            pool.wait_ge(lanes_ready, 1)
            for n, t in enumerate(POOL_PAIRS):
                block_onehot(pool, t).then_inc(pool_onehots, 1)
                pool.wait_ge(pool_onehots, 2 * n + 1)
                lane_onehot(pool, t).then_inc(pool_onehots, 1)
                pool.wait_ge(pool_onehots, 2 * n + 2)
            pool.wait_ge(route_done, 1)
            pool.wait_ge(row_out[0], 16 * (TILES // 2 + 1) + 1)
            pool.wait_ge(row_out[1], 16 * TILES // 2 + 1)
            for n in range(2):
                row_indices(n, 0, n)
                gather(n)
            bias(0, 0, expert(0))

            def tile(n, m, p):
                more = not (isinstance(n, int) and n >= SLOT_TILES - 2)
                if more:
                    row_indices(n + 2, m + 1, p)
                if not is_tile(n, 0):
                    pair_indices(n - 1, m - 1 + p, 1 - p)
                if not is_tile(n, SLOT_TILES - 1):
                    e = expert(n + 1)
                if more:
                    gather(p)
                if not is_tile(n, 0):
                    scatter(1 - p)
                if not is_tile(n, SLOT_TILES - 1):
                    bias(n + 1, 1 - p, e)

            slot_tiles(pool, tile)
            pair_indices(SLOT_TILES - 1, SLOT_TILES // 2, 0)
            scatter(0)

        block = ctx.enter_context(nc.Block())

        @block.sync
        def _(sp):
            sp.dma_start(wst, WT).then_inc(w_in, 16)
            sp.dma_start(h0[:], h0T).then_inc(w_in, 16)
            sp.dma_start(alpha[:], alphaT).then_inc(w_in, 16)
            sp.wait_ge(const0, 1)
            sp.dma_start(b_mat[0:1, :], b_row).then_inc(w_in, 16)
            for j in range(RING):
                sp.dma_start(z[:, j], zT[:, j]).then_inc(z_in[j], 16)
            sp.dma_start(gw[:], gate_wT).then_inc(gw_in, 16)
            sp.dma_start(gb_row[:], gate_b.broadcast_to([P, E])).then_inc(small_in, 16)
            sp.dma_start(b1s[:], b1T).then_inc(small_in, 16)
            sp.dma_start(rw[:], rwT).then_inc(small_in, 16)
            sp.dma_start(rtw[:], rtwT).then_inc(small_in, 16)
            sp.dma_start(rb_row[:], rbias.broadcast_to([P, E])).then_inc(small_in, 16)
            sp.dma_start(fb1[:], fb1T).then_inc(small_in, 16)
            sp.dma_start(cst, const).then_inc(small_in, 16)

            def keep_rows(i, j):
                sp.wait_ge(row_cp, 2 * RING * i + 2 * j + 2)
                sp.dma_start(rows_d[bass.ds(P * RING * i + P * j, P)], hrow[:, j % 2]).then_inc(row_out[j % 2], 16)

            def next_z(i, j):
                sp.wait_ge(rest_ready, 64 * i + 16 * j + 16)
                sp.dma_start(z[:, j], zT[:, RING * i + j + RING]).then_inc(z_in[j], 16)

            with sp.Fori(0, TILES // RING - 1) as i:
                for j in range(RING):
                    keep_rows(i, j)
                    next_z(i, j)
            for j in range(RING):
                keep_rows(TILES // RING - 1, j)
            keep_rows(TILES // RING, 0)

            pieces = [sw1T, sw3T, sw2T, rw1T[:, 0:1], rw1T[:, 1:2], rw2T[:, 0:E // 2], rw2T[:, E // 2:],
                      fw1n[:, 0:FC // 2], fw1n[:, FC // 2:], fw2n[:, 0:1], fw2n[:, 1:2]]
            sp.wait_ge(w_split, 96)

            def load_piece(c):
                if c >= 2:
                    sp.wait_ge(mw_used, c - 1)
                sp.dma_start(stage[:, c % 2].rearrange("p (c n) -> p c n", c=pieces[c].shape[1]), pieces[c])\
                  .then_inc(mw_in[c % 2], 16)

            def bias(n, p):
                e = sp.value_load(expert_of[0:1, bass.ds(n, 1)], min_val=0, max_val=E - 1)
                sp.dma_start(b2_now[:, p], b2[bass.ds(e, 1)].broadcast_to([P, D])).then_inc(b2_in[p], 16)

            for c in range(2):
                load_piece(c)
            sp.wait_ge(route_done, 1)
            bias(0, 0)

            def tile(n, m, p):
                if not is_tile(n, SLOT_TILES - 1):
                    if not is_tile(n, 0):
                        sp.wait_ge(out_ready, n)
                    bias(n + 1, 1 - p)
                if isinstance(n, int) and n < JOBS:
                    for c in range(2 * n + 2, min(2 * n + 4, 8)) if n < 4 else range(n + 4, min(n + 5, len(pieces))):
                        load_piece(c)

            slot_tiles(sp, tile)

            pairs_in = pairs_d[0:PAIRS].rearrange("(k j p) d -> p k j d", k=2, p=P)
            sp.wait_ge(l2_psum, SLOT_TILES)
            sp.dma_start(x1[:, 0:GT], xn[:, 0:GT]).then_inc(x_in[0], 16)
            sp.wait_ge(pairs_out[0], 16 * (SLOT_TILES + 1))
            sp.wait_ge(pairs_out[1], 16 * (SLOT_TILES - 1))

            def results(g, p):
                for k in range(2):
                    sp.dma_start(o_in[:, p, k], pairs_in[:, k, bass.ds(GT * g, GT)]).then_inc(o_arrived[p], 16)

            results(0, 0)
            sp.dma_start(x1[:, GT:2 * GT], xn[:, GT:2 * GT]).then_inc(x_in[1], 16)
            results(1, 1)
            sp.dma_start(bq2, fb2.broadcast_to([P, D])).then_inc(bq2_in, 16)
            with sp.Fori(1, GROUPS // 2) as h:
                for p in range(2):
                    sp.wait_ge(x1_ready, 2 * h + p - 1)
                    sp.dma_start(x1[:, bass.ds(2 * GT * h + GT * p, GT)], xn[:, bass.ds(2 * GT * h + GT * p, GT)])\
                      .then_inc(x_in[p], 16)
                    results(2 * h + p, p)

            with sp.Fori(0, GROUPS) as g:
                sp.wait_ge(ob, 2 * g + 2)
                sp.dma_start(out[:, bass.ds(GT * g, GT)], x1[:, bass.ds(GT * g, GT)]).then_inc(out_done, 16)
            sp.wait_ge(out_done, 16 * GROUPS)

        @block.gpsimd
        def _(pool):
            pool.memset(b_mat, 0.0).then_inc(const0, 1)
            pool.memset(hring[:, 1], 0.0).then_inc(const0, 1)
            pool.memset(zs.rearrange("p h s c b v -> p (h s c b v)"), 0.0).then_inc(const0, 1)
            for h in range(2):
                pool.memset(hrow[:, h], 0.0).then_inc(row_out[h], 1)
            for e in range(E):
                pool.memset(prio[:, e:e + 1], float(E - e)).then_inc(idents, 1)
            pool.memset(ident[:], 0.0).then_inc(idents, 1)
            pool.wait_ge(idents, 9)
            pool.affine_select(out=ident[:], in_=ident[:], compare_op=ALU.not_equal, fill=1.0, base=0,
                               pattern=[[-1, P]], channel_multiplier=1).then_inc(idents, 1)
            pool.wait_ge(idents, 10)
            pool.tensor_copy(identh[:], ident[:]).then_inc(idents, 1)
            pool.tensor_copy(identb[:], ident[:]).then_inc(idents, 1)
            pool.memset(sums[:], 0.0).then_inc(idents, 1)
            pool.memset(w_scale[:], W_SCALE).then_inc(idents, 1)
            pool.memset(magic[:], MAGIC).then_inc(idents, 1)
            pool.memset(ones16, 1.0).then_inc(idents, 1)

            def load(e, c):
                src = (w1T, w2T)[c // 2][bass.ds(e, 1)].rearrange("a p n -> p (a n)")
                pool.dma_start(stage[:, c % 2], src[:, 1024 * (c % 2):1024 * (c % 2) + 1024]).then_inc(piece_in[c % 2], 16)

            def split(e, c):
                st, n = stage[:, c % 2], slice(1024 * (c % 2), 1024 * (c % 2) + 1024)
                hi, lo = (W[:, c // 2, bass.ds(e, 1), s, n].rearrange("p a n -> p (a n)") for s in range(2))
                done = 12 * e + 3 * c
                pool.wait_ge(piece_in[c % 2], 32 * e + 16 * (c // 2) + 16)
                pool.tensor_tensor(st, st, w_scale[:].broadcast_to([P, 1024]), ALU.mult).then_inc(w_split, 1)
                pool.wait_ge(w_split, done + 1)
                pool.tensor_copy(hi, st).then_inc(w_split, 1)
                pool.wait_ge(w_split, done + 2)
                pool.tensor_tensor(lo, st, hi, ALU.subtract).then_inc(w_split, 1)
                pool.wait_ge(w_split, done + 3)

            pool.wait_ge(idents, 16)
            load(0, 0)
            load(0, 1)
            with pool.Fori(0, E - 1) as e:
                for c in range(4):
                    split(e, c)
                    load(e + c // 2, (c + 2) % 4)
            for c in range(4):
                split(E - 1, c)
                if c < 2:
                    load(E - 1, c + 2)
            pool.wait_ge(small_in, 112)
            pool.tensor_copy(tri, cst[:, C_TRI:CONSTS]).then_inc(cst_ready, 1)
            pool.wait_ge(cst_ready, 1)
            pool.tensor_copy(cst16[:], cst[:, 0:C_TILE]).then_inc(cst_ready, 1)
            pool.wait_ge(cst_ready, 2)
            pool.tensor_scalar(b1s[:], b1s[:], A_SCALE, None, ALU.mult).then_inc(cst_ready, 1)
            pool.wait_ge(cst_ready, 3)
            experts_pool(pool)
            ffn_pool(pool)

        @block.scalar
        def _(act):
            def rows_copy(J2, j, s):
                if s == 0:
                    act.wait_ge(row_out[j % 2], 16 * J2 + 1)
                act.activation(hrow[:, j % 2, s * D:(s + 1) * D], psh(4)[:, s * D:(s + 1) * D], ACT.Copy)\
                   .then_inc(row_cp, 1)

            def step(i, s, last_tile=False):
                j, c = s // STEPS_PER_TILE, (s % STEPS_PER_TILE) * BATCH
                act.wait_ge(pre_ready, 32 * i + s + 1)
                act.activation(gate_rest[:, :, :, 0], ps[:, 2 * (j % 2):2 * (j % 2) + 2, c:c + BATCH], ACT.Tanh,
                               scale=0.5 / PRE_SCALE).then_inc(gate_ready, 1)
                act.wait_ge(u_ready, 32 * i + s + 1)
                act.activation(hring[:, j % 2, 0, :, c:c + BATCH], u[:, :, :, 1], ACT.Tanh, scale=0.5)\
                   .then_inc(hi_ready, 1)
                act.activation(h32[:], u[:, :, :, 1], ACT.Tanh, scale=0.5).then_inc(h32_ready, 1)
                part = s % STEPS_PER_TILE
                if part in (3, 4):
                    if part == 3:
                        act.wait_ge(row_ps, RING * i + j + 1)
                    rows_copy(2 * i + j // 2, j, part - 3)
                if part == 6 and not last_tile:
                    act.wait_ge(z_in[(j + 1) % RING], 16 * i + (32 if j == RING - 1 else 16))
                    spread(j + 1)

            def spread(j):
                act.activation(zs[:, j % 2].rearrange("p s c b v -> p c s b v")[:, :, :, :, 1],
                               z[:, j % RING].rearrange("p c (s b) -> p c s b", b=BATCH), ACT.Copy).then_inc(zs_ready, 1)

            act.wait_ge(const0, 3)
            act.wait_ge(z_in[0], 16)
            spread(0)
            steps = RING * STEPS_PER_TILE
            with act.Fori(0, TILES // RING - 1) as i:
                for s in range(steps):
                    step(i, s)
            for s in range(steps):
                step(TILES // RING - 1, s, last_tile=s >= steps - STEPS_PER_TILE)
            act.wait_ge(row_ps, TILES + 1)
            for s in range(2):
                rows_copy(TILES // 2, 0, s)
            experts_act(act)
            mixture_act(act)
            ffn_act(act)

        @block.vector
        def _(dve):
            dve.memset(ones[:], 1.0).then_inc(prep, 1)
            dve.wait_ge(w_in, 64)
            dve.wait_ge(prep, 1)
            dve.tensor_scalar(wh_hi, wst[:, 0:2], W_SCALE, None, ALU.mult).then_inc(prep, 1)
            dve.tensor_scalar(wz, wst[:, 2:4], PRE_SCALE, None, ALU.mult).then_inc(prep, 1)
            dve.tensor_scalar(b_mat, b_mat, PRE_SCALE, None, ALU.mult).then_inc(prep, 1)
            dve.tensor_scalar(alpha[:], alpha[:], -2.0, 2.0, ALU.mult, ALU.add).then_inc(prep, 1)
            dve.wait_ge(prep, 5)
            dve.scalar_tensor_tensor(wh_lo, wst[:, 0:2], W_SCALE, wh_hi, ALU.mult, ALU.subtract).then_inc(prep, 1)
            dve.wait_ge(gw_in, 16)
            dve.tensor_scalar(gw_s[:, 0], gw[:], W_SCALE, None, ALU.mult).then_inc(prep, 1)
            dve.wait_ge(prep, 7)
            dve.scalar_tensor_tensor(gw_s[:, 1], gw[:], W_SCALE, gw_s[:, 0], ALU.mult, ALU.subtract).then_inc(prep, 1)
            h_hi, h_lo = hring[:, 1, 0, :, P - BATCH:P], hring[:, 1, 1, :, P - BATCH:P]
            dve.wait_ge(const0, 2)
            dve.tensor_copy(h_hi, h0[:]).then_inc(hi_ready, 1)
            dve.wait_ge(hi_ready, 1)
            dve.tensor_tensor(h_lo, h0[:], h_hi, ALU.subtract).then_inc(lo_ready, 1)

            def rest(h, j, c):
                for k in range(DC):
                    dve.scalar_tensor_tensor(gate_rest[:, k, :, 1], h[:, k], alpha[:, k:k + 1], z[:, j, k, c:c + BATCH],
                                             ALU.mult, ALU.add).then_inc(rest_ready, 1)

            dve.wait_ge(z_in[0], 16)
            rest(h0, 0, 0)

            def step(i, s, last=False):
                j, c = s // STEPS_PER_TILE, (s % STEPS_PER_TILE) * BATCH
                if s % STEPS_PER_TILE == 0:
                    dve.wait_ge(zs_ready, RING * i + j + 1)
                if isinstance(i, int):
                    dve.wait_ge(gate_ready, 32 * i + s + 1)
                    dve.wait_ge(rest_ready, 64 * i + 2 * s + 2)
                else:
                    dve.wait_ge(rest_ready, 64 * i + 2 * s + 2)
                    dve.wait_ge(gate_ready, 32 * i + s + 1)
                dve.tensor_tensor_scan(u[:].rearrange("p c b v -> p (c b v)"),
                                       zs[:, j % 2, s % STEPS_PER_TILE].rearrange("p c b v -> p (c b v)"),
                                       gate_rest[:].rearrange("p c b v -> p (c b v)"), 0.0, ALU.mult, ALU.add)\
                   .then_inc(u_ready, 1)
                dve.wait_ge(h32_ready, 32 * i + s + 1)
                dve.tensor_tensor(hring[:, j % 2, 1, :, c:c + BATCH], h32[:], hring[:, j % 2, 0, :, c:c + BATCH],
                                  ALU.subtract).then_inc(lo_ready, 1)
                if not last:
                    n = (s + 1) % steps
                    if n % STEPS_PER_TILE == 0:
                        dve.wait_ge(z_in[n // STEPS_PER_TILE], 16 * i + (32 if n == 0 else 16))
                    rest(h32, n // STEPS_PER_TILE, n % STEPS_PER_TILE * BATCH)

            steps = RING * STEPS_PER_TILE
            with dve.Fori(0, TILES // RING - 1) as i:
                for s in range(steps):
                    step(i, s)
            for s in range(steps):
                step(TILES // RING - 1, s, last=s == steps - 1)
            dve.wait_ge(cst_ready, 3)
            route(dve)
            experts_dve(dve)
            mixture_dve(dve)
            ffn_dve(dve)

        @block.tensor
        def _(pe):
            def z_part(slot, part):
                m, k = part // 3, part % 3
                dst = ps[:, 2 * (slot % 2) + m, 0:P]
                cols = slice(m * P, (m + 1) * P)
                if k < 2:
                    pe.matmul(dst, wz[:, k, cols], z[:, slot, k, :], start=(k == 0), stop=False, skip_group_check=True)
                else:
                    pe.matmul(dst, b_mat[:, cols], ones[:], start=False, stop=False, skip_group_check=True)

            def rows(half):
                for s in range(2):
                    for k in range(DC):
                        last = pe.transpose(psh(4)[:, (s * DC + k) * P:(s * DC + k + 1) * P], hring[:, half, s, k],
                                            identh[:])
                last.then_inc(row_ps, 1)

            def logits(half, col):
                for n, (a, b) in enumerate(((0, 0), (0, 1), (1, 0))):
                    for k in range(DC):
                        last = pe.matmul(ps[:, 5, bass.ds(col, E)], hring[:, half, a, k], gw_s[:, b, k],
                                         start=(n == 0 and k == 0), stop=(n == 2 and k == DC - 1))
                return last

            def step(i, s, last_tile=False):
                j, c = s // STEPS_PER_TILE, (s % STEPS_PER_TILE) * BATCH
                half, b = j % 2, 2 * (j % 2)
                part = s % STEPS_PER_TILE
                prev, pc = (half, c - BATCH) if part else (1 - half, P - BATCH)
                pe.wait_ge(hi_ready, 32 * i + s + 1)
                for w in (wh_hi, wh_lo):
                    for m in range(DC):
                        for k in range(DC):
                            pe.matmul(ps[:, b + m, c:c + BATCH], w[:, k, m * P:(m + 1) * P],
                                      hring[:, prev, 0, k, pc:pc + BATCH], start=False, stop=False, skip_group_check=True)
                pe.wait_ge(lo_ready, 32 * i + s + 1)
                for m in range(DC):
                    for k in range(DC):
                        last = pe.matmul(ps[:, b + m, c:c + BATCH], wh_hi[:, k, m * P:(m + 1) * P],
                                         hring[:, prev, 1, k, pc:pc + BATCH], start=False, stop=(k == DC - 1),
                                         skip_group_check=True)
                last.then_inc(pre_ready, 1)
                if part < 3 * DC and not last_tile:
                    if part == 0:
                        pe.wait_ge(z_in[(j + 1) % RING], 16 * i + (32 if j == RING - 1 else 16))
                    z_part((j + 1) % RING, part)
                if part == 1:
                    rows(1 - half)
                if part == 6:
                    logits(1 - half, E * RING * i + E * j)

            pe.wait_ge(prep, 8)
            pe.wait_ge(z_in[0], 16)
            pe.wait_ge(idents, 11)
            for part in range(3 * DC):
                z_part(0, part)
            steps = RING * STEPS_PER_TILE
            with pe.Fori(0, TILES // RING - 1) as i:
                for s in range(steps):
                    step(i, s)
            for s in range(steps):
                step(TILES // RING - 1, s, last_tile=s >= steps - STEPS_PER_TILE)
            pe.wait_ge(lo_ready, STEPS + 1)
            logits(1, E * TILES).then_inc(logits_ready, 1)
            rows(1)

            pe.wait_ge(chosen_ready, 1)
            pe.wait_ge(cst_ready, 3)
            pe.wait_ge(row_cp, 2 * TILES + 2)
            flat = m16.rearrange("p j e -> p (j e)")
            pe.matmul(ps[:, 4, 0:(TILES + 1) * E], tri, flat, start=True, stop=False, skip_group_check=True)
            for j in range(TILES):
                last = pe.matmul(ps[:, 4, (j + 1) * E:(TILES + 1) * E], ones16,
                                 m16[:, j:j + 1].broadcast_to([P, TILES - j, E]), start=False, stop=(j == TILES - 1),
                                 skip_group_check=True)
            last.then_inc(pos_ready, 1)
            quarter = TILES // 2
            for t in range(2 * TILES):
                if t in POOL_PAIRS:
                    pe.wait_ge(pool_onehots, 2 * (t - POOL_PAIRS[0]) + 2)
                elif t in DVE_PAIRS:
                    pe.wait_ge(onehots, 2 * DVE_PAIRS.index(t) + 2)
                q = t // quarter
                last = pe.matmul(ps[:, 7, q * BLOCKS:(q + 1) * BLOCKS], lane1h[:, t], block1h[:, t],
                                 start=(t % quarter == 0), stop=(t % quarter == quarter - 1))
            last.then_inc(slots_ready, 1)
            experts_pe(pe)
            mixture_pe(pe)
            ffn_pe(pe)


_INS = ['zT', 'xn', 'h0T', 'WT', 'b_row', 'alphaT', 'gate_wT', 'gate_b', 'w1T', 'b1T', 'w2T', 'b2', 'rwT', 'rtwT', 'rbias',
        'sw1T', 'sw3T', 'sw2T', 'rw1T', 'rw2T', 'fw1n', 'fb1T', 'fw2n', 'fb2', 'const']


def kernel(x, cond_1024, L0_cond_W, L0_cond_b, L0_cond_alpha, L0_ffn_gate_w, L0_ffn_gate_b, L0_ffn_w1, L0_ffn_b1,
           L0_ffn_w2, L0_ffn_b2, L1_cond_router_w, L1_cond_router_t_w, L1_cond_router_bias, L1_cond_sw1, L1_cond_sw3,
           L1_cond_sw2, L1_cond_rw1, L1_cond_rw2, L1_ffn_w1, L1_ffn_b1, L1_ffn_w2, L1_ffn_b2):
    import numpy as np
    import concourse.bacc as bacc
    from concourse.bass_utils import run_bass_kernel_spmd as run

    def rows(a):
        return np.asarray(a).reshape(-1, P, a.shape[-1]).transpose(1, 0, 2)

    x = np.asarray(x)
    arrays = {
        "zT": x.transpose(2, 1, 0).reshape(DC, P, TILES, P).transpose(1, 2, 0, 3),
        "xn": x.transpose(1, 0, 2).reshape(TILES, P, D).transpose(1, 0, 2),
        "h0T": rows(np.asarray(cond_1024).T),
        "WT": rows(np.asarray(L0_cond_W).T),
        "b_row": np.asarray(L0_cond_b)[None],
        "alphaT": np.asarray(L0_cond_alpha).reshape(DC, P).T,
        "gate_wT": rows(L0_ffn_gate_w),
        "gate_b": np.asarray(L0_ffn_gate_b)[None],
        "w1T": np.asarray(L0_ffn_w1).reshape(E, DC, P, F).transpose(0, 2, 1, 3).reshape(E, P, DC * F),
        "b1T": np.asarray(L0_ffn_b1).reshape(E, FC, P).transpose(2, 0, 1),
        "w2T": np.asarray(L0_ffn_w2).reshape(E, FC, P, D).transpose(0, 2, 1, 3).reshape(E, P, FC * D),
        "b2": np.asarray(L0_ffn_b2),
        "rwT": rows(np.asarray(L1_cond_router_w).T),
        "rtwT": rows(np.asarray(L1_cond_router_t_w).T),
        "rbias": np.asarray(L1_cond_router_bias)[None],
        "sw1T": rows(np.asarray(L1_cond_sw1).T),
        "sw3T": rows(np.asarray(L1_cond_sw3).T),
        "sw2T": rows(np.asarray(L1_cond_sw2).T),
        "rw1T": rows(np.asarray(L1_cond_rw1).transpose(2, 0, 1).reshape(D, E * P)),
        "rw2T": np.asarray(L1_cond_rw2).transpose(2, 0, 1),
        "fw1n": rows(L1_ffn_w1),
        "fb1T": np.asarray(L1_ffn_b1).reshape(FC, P).T,
        "fw2n": rows(L1_ffn_w2),
        "fb2": np.asarray(L1_ffn_b2)[None],
    }
    p, b = np.arange(P), np.arange(BLOCKS)
    const = np.zeros((P, CONSTS), np.float32)
    const[:, C_LANE:C_LANE + P] = p
    const[:, C_BLOCK:C_BLOCK + BLOCKS] = b
    const[:, C_TILE:C_TILE + TILES // 2] = P * np.arange(TILES // 2)[None] + p[:, None] + 1
    const[:, C_PAD:C_PAD + BLOCKS] = 1 + PAIRS + P * b[None] + p[:, None]
    const[:, C_SLOT_TILE:C_SLOT_TILE + SLOT_TILES] = np.arange(SLOT_TILES)
    const[:, C_TRI:C_TRI + P] = p[:, None] < p[None]
    arrays["const"] = const
    arrays = {k: np.ascontiguousarray(v) for k, v in arrays.items()}
    nc = bacc.Bacc("TRN2", target_bir_lowering=False, num_devices=1)
    args = [nc.dram_tensor(f"in_{n}", arrays[n].shape, F32, kind="ExternalInput").ap() for n in _INS]
    args.append(nc.dram_tensor("rows", (N + P, 2 * D), F16).ap())
    args.append(nc.dram_tensor("pairs", (PAIRS + SLOT_TILES * ST, D), F32).ap())
    args.append(nc.dram_tensor("out", (P, TILES, D), F32, kind="ExternalOutput").ap())
    build_program(nc, *args)
    r = run(nc, [{f"in_{n}": arrays[n] for n in _INS}], core_ids=[0])
    got = r.results[0]["out"]
    return np.ascontiguousarray(got.transpose(1, 0, 2).reshape(STEPS, BATCH, D).transpose(1, 0, 2))
```
